# Optimizing a Trainium2 kernel written in Bass

```python
import numpy as np
import jax
import jax.numpy as jnp

def _softmax(x, axis=-1):
    return jax.nn.softmax(x, axis=axis)

def _gelu(x):
    return jax.nn.gelu(x, approximate=True)

def _silu(x):
    return jax.nn.silu(x)

def _sigmoid(x):
    return jax.nn.sigmoid(x)

def _layernorm(x, axis=-1, eps=1e-05):
    m = jnp.mean(x, axis=axis, keepdims=True)
    v = jnp.var(x, axis=axis, keepdims=True)
    return (x - m) / jnp.sqrt(v + eps)

def _scatter_add(tgt, idx, src, axis=0):
    return tgt.at[idx].add(src)

def _segment_sum(src, seg, n):
    return jax.ops.segment_sum(src, seg, n)
kernel_name = 'mk_macaron_d2_jaxref_r8_5d2359'

def setup_inputs(seed: int=0):
    np.random.seed(seed)
    _w = jnp.asarray

    def _L0_attn_setup():
        import jax, jax.numpy as jnp
        import numpy as np
        DT_RANK = 64
        D_STATE = 16

        def _dwconv_silu(x, w, b, dil):
            k = w.shape[-1]
            out = jax.lax.conv_general_dilated(x, w[:, None, :], window_strides=(1,), padding=[(dil * (k - 1), 0)], rhs_dilation=(dil,), dimension_numbers=('NCH', 'OIH', 'NCH'), feature_group_count=x.shape[1])
            return jax.nn.silu(out + b[None, :, None])
        key = jax.random.key(seed)
        ks = jax.random.split(key, 12)
        b, l, d_model, d_inner = (4, 256, 128, 256)
        s = lambda fan: 1.0 / np.sqrt(fan)
        inp = {'hidden_states': jax.random.normal(ks[0], (b, l, d_model), jnp.float32), 'W_in': jax.random.normal(ks[1], (2 * d_inner, d_model), jnp.float32) * s(d_model), 'conv_w1': jax.random.normal(ks[2], (d_inner, 4), jnp.float32) * 0.5, 'conv_b1': jax.random.normal(ks[3], (d_inner,), jnp.float32) * 0.1, 'conv_w2': jax.random.normal(ks[4], (d_inner, 4), jnp.float32) * 0.5, 'conv_b2': jax.random.normal(ks[5], (d_inner,), jnp.float32) * 0.1, 'conv_gates': jnp.ones((2,), jnp.float32), 'W_x': jax.random.normal(ks[6], (DT_RANK + 2 * D_STATE, d_inner), jnp.float32) * s(d_inner), 'W_dt': jax.random.normal(ks[7], (d_inner, DT_RANK), jnp.float32) * s(DT_RANK), 'b_dt': jax.random.normal(ks[8], (d_inner,), jnp.float32) - 4.0, 'A_log': jnp.log(1.0 + 15.0 * jax.random.uniform(ks[9], (d_inner, D_STATE), jnp.float32)), 'D_param': jnp.ones((d_inner,), jnp.float32), 'W_out': jax.random.normal(ks[10], (d_model, d_inner), jnp.float32) * s(d_inner)}
        return inp
    _L0_attn_in = _L0_attn_setup()

    def _L0_ffn_setup():
        import jax, jax.numpy as jnp
        import numpy as np
        DIM = 128

        def _reference_tuple_inner(x, W_r, W_k, W_v, mu_r, mu_k):
            B, T, C = x.shape
            x_prev = jnp.concatenate([jnp.zeros((B, 1, C), x.dtype), x[:, :-1, :]], axis=1)
            xr = mu_r * x + (1.0 - mu_r) * x_prev
            xk = mu_k * x + (1.0 - mu_k) * x_prev
            r = jax.nn.sigmoid(jnp.einsum('btc,dc->btd', xr, W_r))
            k = jnp.einsum('btc,dc->btd', xk, W_k)
            k_act = jnp.square(jax.nn.relu(k))
            out = r * jnp.einsum('btc,dc->btd', k_act, W_v)
            new_state = x[:, -1, :]
            return (out, new_state)
        key = jax.random.key(seed)
        ks = jax.random.split(key, 6)
        B, T, C = (8, 256, DIM)
        x = jax.random.normal(ks[0], (B, T, C), dtype=jnp.float32)
        s = 1.0 / np.sqrt(C)
        W_r = jax.random.uniform(ks[1], (C, C), jnp.float32, -s, s)
        W_k = jax.random.uniform(ks[2], (C, C), jnp.float32, -s, s)
        W_v = jax.random.uniform(ks[3], (C, C), jnp.float32, -s, s)
        mu_r = jax.random.uniform(ks[4], (C,), jnp.float32)
        mu_k = jax.random.uniform(ks[5], (C,), jnp.float32)
        return {'x': x, 'W_r': W_r, 'W_k': W_k, 'W_v': W_v, 'mu_r': mu_r, 'mu_k': mu_k}
    _L0_ffn_in = _L0_ffn_setup()

    def _L1_attn_setup():
        import jax, jax.numpy as jnp
        import numpy as np
        DIM = 128
        DIM_HEAD = 128
        HEADS = 8
        DIM_INNER = DIM_HEAD * HEADS
        key = jax.random.key(seed)
        k_x, k_qkv, k_out = jax.random.split(key, 3)
        x = jax.random.normal(k_x, (2, 256, DIM), dtype=jnp.float32)
        gamma = jnp.ones((DIM,), dtype=jnp.float32)
        w_qkv = jax.random.uniform(k_qkv, (DIM_INNER * 3, DIM), dtype=jnp.float32, minval=-1.0, maxval=1.0) / np.sqrt(DIM)
        w_out = jax.random.uniform(k_out, (DIM, DIM_INNER), dtype=jnp.float32, minval=-1.0, maxval=1.0) / np.sqrt(DIM_INNER)
        return {'x': x, 'gamma': gamma, 'w_qkv': w_qkv, 'w_out': w_out}
    _L1_attn_in = _L1_attn_setup()

    def _L1_ffn_setup():
        import jax, jax.numpy as jnp
        import numpy as np
        B, N, C, F, E, K = (2, 256, 128, 512, 8, 2)
        key = jax.random.key(seed)
        k = jax.random.split(key, 6)
        xavier1 = float(np.sqrt(6.0 / (C + F)))
        xavier2 = float(np.sqrt(6.0 / (F + C)))
        return {'x': jax.random.normal(k[0], (B, N, C), dtype=jnp.float32), 'router_w': jax.random.normal(k[1], (E, C), dtype=jnp.float32) * 0.01, 'w1': jax.random.uniform(k[2], (E, F, C), dtype=jnp.float32, minval=-xavier1, maxval=xavier1), 'b1': jnp.zeros((E, F), dtype=jnp.float32), 'w2': jax.random.uniform(k[3], (E, C, F), dtype=jnp.float32, minval=-xavier2, maxval=xavier2), 'b2': jnp.zeros((E, C), dtype=jnp.float32)}
    _L1_ffn_in = _L1_ffn_setup()
    _d = {'L0_attn_hidden_states': _L0_attn_in['hidden_states'], 'L0_attn_W_in': _L0_attn_in['W_in'], 'L0_attn_conv_w1': _L0_attn_in['conv_w1'], 'L0_attn_conv_b1': _L0_attn_in['conv_b1'], 'L0_attn_conv_w2': _L0_attn_in['conv_w2'], 'L0_attn_conv_b2': _L0_attn_in['conv_b2'], 'L0_attn_conv_gates': _L0_attn_in['conv_gates'], 'L0_attn_W_x': _L0_attn_in['W_x'], 'L0_attn_W_dt': _L0_attn_in['W_dt'], 'L0_attn_b_dt': _L0_attn_in['b_dt'], 'L0_attn_A_log': _L0_attn_in['A_log'], 'L0_attn_D_param': _L0_attn_in['D_param'], 'L0_attn_W_out': _L0_attn_in['W_out'], 'L0_ffn_W_r': _L0_ffn_in['W_r'], 'L0_ffn_W_k': _L0_ffn_in['W_k'], 'L0_ffn_W_v': _L0_ffn_in['W_v'], 'L0_ffn_mu_r': _L0_ffn_in['mu_r'], 'L0_ffn_mu_k': _L0_ffn_in['mu_k'], 'L1_attn_gamma': _L1_attn_in['gamma'], 'L1_attn_w_qkv': _L1_attn_in['w_qkv'], 'L1_attn_w_out': _L1_attn_in['w_out'], 'L1_ffn_router_w': _L1_ffn_in['router_w'], 'L1_ffn_w1': _L1_ffn_in['w1'], 'L1_ffn_b1': _L1_ffn_in['b1'], 'L1_ffn_w2': _L1_ffn_in['w2'], 'L1_ffn_b2': _L1_ffn_in['b2']}
    _x0 = _d['L0_attn_hidden_states']
    _d['L0_attn_hidden_states'] = jax.random.normal(jax.random.fold_in(jax.random.key(seed), 1), (4, 1024, 128), dtype=_x0.dtype)
    del _x0
    return _d

def reference(L0_attn_hidden_states, L0_attn_W_in, L0_attn_conv_w1, L0_attn_conv_b1, L0_attn_conv_w2, L0_attn_conv_b2, L0_attn_conv_gates, L0_attn_W_x, L0_attn_W_dt, L0_attn_b_dt, L0_attn_A_log, L0_attn_D_param, L0_attn_W_out, L0_ffn_W_r, L0_ffn_W_k, L0_ffn_W_v, L0_ffn_mu_r, L0_ffn_mu_k, L1_attn_gamma, L1_attn_w_qkv, L1_attn_w_out, L1_ffn_router_w, L1_ffn_w1, L1_ffn_b1, L1_ffn_w2, L1_ffn_b2):

    def _L0_attn_ref(hidden_states, W_in, conv_w1, conv_b1, conv_w2, conv_b2, conv_gates, W_x, W_dt, b_dt, A_log, D_param, W_out):
        import jax, jax.numpy as jnp
        import numpy as np
        DT_RANK = 64
        D_STATE = 16

        def _dwconv_silu(x, w, b, dil):
            k = w.shape[-1]
            out = jax.lax.conv_general_dilated(x, w[:, None, :], window_strides=(1,), padding=[(dil * (k - 1), 0)], rhs_dilation=(dil,), dimension_numbers=('NCH', 'OIH', 'NCH'), feature_group_count=x.shape[1])
            return jax.nn.silu(out + b[None, :, None])
        b, l, d_model = hidden_states.shape
        d_inner = W_in.shape[0] // 2
        xz = jnp.einsum('bld,ed->bel', hidden_states, W_in)
        x, z = (xz[:, :d_inner], xz[:, d_inner:])
        x1 = _dwconv_silu(x, conv_w1, conv_b1, 1)
        x2 = _dwconv_silu(x, conv_w2, conv_b2, 2)
        gate = jax.nn.softmax(conv_gates)
        xc = gate[0] * x1 + gate[1] * x2
        xT = jnp.swapaxes(xc, 1, 2)
        x_dbl = jnp.einsum('bld,ed->ble', xT, W_x)
        dt_low = x_dbl[..., :DT_RANK]
        B = x_dbl[..., DT_RANK:DT_RANK + D_STATE]
        C = x_dbl[..., DT_RANK + D_STATE:]
        dt = jnp.einsum('blr,dr->bld', dt_low, W_dt)
        delta = jax.nn.softplus(dt + b_dt)
        A = -jnp.exp(A_log)

        def step(h, inp):
            dlt_t, B_t, C_t, x_t = inp
            dA = jnp.exp(dlt_t[:, :, None] * A)
            h = h * dA + dlt_t[:, :, None] * B_t[:, None, :] * x_t[:, :, None]
            y_t = jnp.einsum('bdn,bn->bd', h, C_t)
            return (h, y_t)
        h0 = jnp.zeros((b, d_inner, D_STATE), xT.dtype)
        seq = (jnp.swapaxes(delta, 0, 1), jnp.swapaxes(B, 0, 1), jnp.swapaxes(C, 0, 1), jnp.swapaxes(xT, 0, 1))
        _, ys = jax.lax.scan(step, h0, seq)
        y = jnp.swapaxes(ys, 0, 1)
        y = y + D_param * xT
        y = y * jax.nn.silu(jnp.swapaxes(z, 1, 2))
        return jnp.einsum('bld,od->blo', y, W_out)

    def _L0_ffn_ref(x, W_r, W_k, W_v, mu_r, mu_k):
        import jax, jax.numpy as jnp
        import numpy as np
        DIM = 128

        def _reference_tuple_inner(x, W_r, W_k, W_v, mu_r, mu_k):
            B, T, C = x.shape
            x_prev = jnp.concatenate([jnp.zeros((B, 1, C), x.dtype), x[:, :-1, :]], axis=1)
            xr = mu_r * x + (1.0 - mu_r) * x_prev
            xk = mu_k * x + (1.0 - mu_k) * x_prev
            r = jax.nn.sigmoid(jnp.einsum('btc,dc->btd', xr, W_r))
            k = jnp.einsum('btc,dc->btd', xk, W_k)
            k_act = jnp.square(jax.nn.relu(k))
            out = r * jnp.einsum('btc,dc->btd', k_act, W_v)
            new_state = x[:, -1, :]
            return (out, new_state)
        return _reference_tuple_inner(x, W_r, W_k, W_v, mu_r, mu_k)[0]

    def _L1_attn_ref(x, gamma, w_qkv, w_out):
        import jax, jax.numpy as jnp
        import numpy as np
        DIM = 128
        DIM_HEAD = 128
        HEADS = 8
        DIM_INNER = DIM_HEAD * HEADS
        scale_norm = DIM ** 0.5
        scale_attn = DIM_HEAD ** (-0.5)
        l2 = jnp.sqrt(jnp.sum(x * x, axis=-1, keepdims=True))
        xn = x / jnp.maximum(l2, 1e-12) * scale_norm * gamma
        qkv = jnp.einsum('bnc,fc->bnf', xn, w_qkv)
        b, n, _ = qkv.shape
        qkv = qkv.reshape(b, n, 3, HEADS, DIM_HEAD)
        q, k, v = (qkv[:, :, 0], qkv[:, :, 1], qkv[:, :, 2])
        q = q * scale_attn
        sim = jnp.einsum('bihd,bjhd->bhij', q, k)
        causal_mask = jnp.triu(jnp.ones((n, n), dtype=bool), k=1)
        neg = -jnp.finfo(sim.dtype).max
        sim = jnp.where(causal_mask, neg, sim)
        attn = jax.nn.softmax(sim, axis=-1)
        out = jnp.einsum('bhij,bjhd->bihd', attn, v)
        out = out.reshape(b, n, DIM_INNER)
        return jnp.einsum('bnf,cf->bnc', out, w_out)

    def _L1_ffn_ref(x, router_w, w1, b1, w2, b2):
        import jax, jax.numpy as jnp
        import numpy as np
        B, N, C, F, E, K = (2, 256, 128, 512, 8, 2)
        Bb, Nn, Cc = x.shape
        x_flat = x.reshape(-1, Cc)
        logits = jnp.einsum('tc,ec->te', x_flat, router_w)
        probs = jax.nn.softmax(logits, axis=-1)
        top_w, top_idx = jax.lax.top_k(probs, K)
        top_w = top_w / (jnp.sum(top_w, axis=-1, keepdims=True) + 1e-09)
        h = jnp.einsum('tc,efc->tef', x_flat, w1) + b1[None]
        h = jax.nn.relu(h)
        y = jnp.einsum('tef,ecf->tec', h, w2) + b2[None]
        sel = jnp.take_along_axis(y, top_idx[:, :, None], axis=1)
        out = jnp.einsum('tkc,tk->tc', sel, top_w)
        return out.reshape(Bb, Nn, Cc)
    x = L0_attn_hidden_states
    x = x + 0.5 * _L0_ffn_ref(_layernorm(x, axis=-1), L0_ffn_W_r, L0_ffn_W_k, L0_ffn_W_v, L0_ffn_mu_r, L0_ffn_mu_k)
    x = x + _L0_attn_ref(_layernorm(x, axis=-1), L0_attn_W_in, L0_attn_conv_w1, L0_attn_conv_b1, L0_attn_conv_w2, L0_attn_conv_b2, L0_attn_conv_gates, L0_attn_W_x, L0_attn_W_dt, L0_attn_b_dt, L0_attn_A_log, L0_attn_D_param, L0_attn_W_out)
    x = x + 0.5 * _L0_ffn_ref(_layernorm(x, axis=-1), L0_ffn_W_r, L0_ffn_W_k, L0_ffn_W_v, L0_ffn_mu_r, L0_ffn_mu_k)
    x = x + 0.5 * _L1_ffn_ref(_layernorm(x, axis=-1), L1_ffn_router_w, L1_ffn_w1, L1_ffn_b1, L1_ffn_w2, L1_ffn_b2)
    x = x + _L1_attn_ref(_layernorm(x, axis=-1), L1_attn_gamma, L1_attn_w_qkv, L1_attn_w_out)
    x = x + 0.5 * _L1_ffn_ref(_layernorm(x, axis=-1), L1_ffn_router_w, L1_ffn_w1, L1_ffn_b1, L1_ffn_w2, L1_ffn_b2)
    return x

_drawn_inputs = setup_inputs


def setup_inputs(seed=0):
    import zlib

    import numpy as np

    out = dict(_drawn_inputs(seed))
    spreads = {'L0_attn_conv_gates': (1.0, 0.6),
     'L0_attn_D_param': (1.0, 0.2),
     'L1_attn_gamma': (1.0, 0.6),
     'L1_ffn_b1': (0.0, 0.1),
     'L1_ffn_b2': (0.0, 0.1)}
    factors = {}
    for name, (base, spread) in spreads.items():
        noise = np.random.default_rng([zlib.crc32(name.encode()), seed]).standard_normal(out[name].shape)
        drawn = base * np.exp(spread * noise) if base else spread * noise
        out[name] = jnp.asarray(drawn.astype(out[name].dtype))
    for name, factor in factors.items():
        out[name] = (out[name] * factor).astype(out[name].dtype)
    return out
```

```python
from contextlib import ExitStack

import numpy as np

import concourse.bass as bass
from concourse import mybir

F32 = mybir.dt.float32
BF16 = mybir.dt.bfloat16
I32 = mybir.dt.int32
U32 = mybir.dt.uint32
ALU = mybir.AluOpType
ACT = mybir.ActivationFunctionType
AX = mybir.AxisListType

P = 128
B, L, D = 4, 1024, 128
NT = B * L // P
TB = L // P
CH = 512
HALVES = L // CH
HALO = 6
LN_EPS = 1e-5

NB = 2
NS = 16
R = 64
BC = 2 * NS
KW = 4

H, DH = 8, 128

E, F = 8, 512
FC = F // P
MT = 72
XSLOTS = 8
YSLOTS = 4
assert MT % XSLOTS == 0 and MT >= 2 * NT + E - 1


class Scope:

    def __init__(self, nc, tag):
        self.nc, self.tag, self.stack, self.sems = nc, tag, ExitStack(), []

    def __enter__(self):
        return self

    def __exit__(self, *e):
        self.stack.__exit__(*e)
        if e[0] is None and self.sems:
            self.nc.clear_and_free_semaphores(self.sems)
            self.nc.all_engine_barrier()

    def sb(self, name, shape, dt=F32):
        return self.stack.enter_context(self.nc.sbuf_tensor(f"{self.tag}_{name}", shape, dt))

    def ps(self, name, shape, dt=F32):
        return self.stack.enter_context(self.nc.psum_tensor(f"{self.tag}_{name}", shape, dt))

    def sem(self, name):
        handle = self.nc.alloc_semaphore(f"{self.tag}_{name}")
        self.sems.append(handle)
        return handle

    def block(self):
        return self.stack.enter_context(self.nc.Block())


def load_phase(nc, g, A):
    with Scope(nc, "load") as s:
        dma_in = s.sem("dma_in")
        halo_zero = s.sem("halo_zero")
        ident_zero = s.sem("ident_zero")
        ident_done = s.sem("ident_done")
        block = s.block()

        @block.sync
        def _(sp):
            hid = A["hidden"].rearrange("(n p) c -> p n c", p=P)
            for q in range(4):
                n = NT // 4
                sp.dma_start(g.x[:, q * n:(q + 1) * n, :], hid[:, q * n:(q + 1) * n, :]).then_inc(dma_in, 16)
            sp.wait_ge(dma_in, 64)

        @block.scalar
        def _(act):
            for dst, name in g.weights:
                act.dma_start(dst, A[name]).then_inc(g.loaded, 16)

        @block.gpsimd
        def _(pool):
            pool.memset(g.ident[:, :], 0.0).then_inc(ident_zero, 1)
            pool.wait_ge(ident_zero, 1)
            pool.affine_select(out=g.ident[:, :], in_=g.ident[:, :], compare_op=ALU.not_equal, fill=1.0,
                               base=0, pattern=[[-1, P]], channel_multiplier=1).then_inc(ident_done, 1)

        @block.vector
        def _(dve):
            dve.memset(g.xnT[:, :, 0:HALO], 0.0).then_inc(halo_zero, 1)


def layernorm_phase(nc, g, tag, keep_tokens=False, rms_gamma=None):
    with Scope(nc, tag) as s:
        stats = s.sb("stats", [P, NT, 6])
        work = s.sb("work", [P, 9, NT])
        stage = s.sb("stage", [P, HALVES, 4, P])
        psT = s.ps("psT", [P, HALVES, CH])
        stats_done = s.sem("stats_done")
        chain = s.sem("chain")
        var_ready = s.sem("var_ready")
        std_ready = s.sem("std_ready")
        staged = s.sem("staged")
        rows_kept = [s.sem(f"rows_kept{h}") for h in range(HALVES)]
        transposed = s.sem("transposed")
        waited = s.sem("waited")
        psT_free = s.sem("psT_free")
        diff, total, m2, var, std, rstd, mean, shift, lengths = (work[:, k, :] for k in range(9))
        if rms_gamma is not None:
            square = s.sb("square", [P, TB, D])
            shift_ready = s.sem("shift_ready")
            lengths_ready = s.sem("lengths_ready")
            roots_ready = s.sem("roots_ready")
        block = s.block()

        @block.vector
        def _(dve):
            with dve.Fori(0, B) as b:
                for t in range(TB):
                    last = dve.bn_stats(out=stats[:, b * TB + t, :], in_=g.x[:, b * TB + t, :])
                last.then_inc(stats_done, 1)
            dve.wait_ge(stats_done, B)
            dve.tensor_tensor(diff, stats[:, :, 1], stats[:, :, 4], ALU.subtract).then_inc(chain, 1)
            dve.tensor_tensor(total, stats[:, :, 1], stats[:, :, 4], ALU.add).then_inc(chain, 1)
            dve.tensor_tensor(m2, stats[:, :, 2], stats[:, :, 5], ALU.add).then_inc(chain, 1)
            dve.wait_ge(chain, 3)
            dve.tensor_tensor(diff, diff, diff, ALU.mult).then_inc(chain, 1)
            dve.tensor_scalar(mean, total, 0.5, None, ALU.mult).then_inc(chain, 1)
            dve.tensor_scalar(m2, m2, 1.0 / D, LN_EPS, ALU.mult, ALU.add).then_inc(chain, 1)
            dve.wait_ge(chain, 6)
            dve.scalar_tensor_tensor(out=var, in0=diff, scalar=0.25, in1=m2, op0=ALU.mult, op1=ALU.add)\
               .then_inc(var_ready, 1)
            dve.wait_ge(std_ready, 1)
            dve.reciprocal(rstd, std).then_inc(chain, 1)
            dve.wait_ge(chain, 7)
            if rms_gamma is not None:
                dve.scalar_tensor_tensor(out=shift, in0=mean, scalar=-1.0, in1=rstd, op0=ALU.mult, op1=ALU.mult)\
                   .then_inc(shift_ready, 1)
                dve.wait_ge(roots_ready, 1)
                dve.tensor_scalar(lengths, lengths, 1e-12, float(D) ** -0.5, ALU.max, ALU.mult).then_inc(chain, 1)
                dve.wait_ge(chain, 8)
                dve.reciprocal(total, lengths).then_inc(chain, 1)
                dve.wait_ge(chain, 9)
                dve.tensor_tensor(rstd, rstd, total, ALU.mult).then_inc(chain, 1)
                dve.wait_ge(chain, 10)
            with dve.Fori(0, B) as b:
                for h in range(HALVES):
                    dve.wait_ge(psT_free, HALVES * b + h + 1)
                    if keep_tokens:
                        dve.wait_ge(rows_kept[h], 16 * b + 16)
                    for j in range(4):
                        t = b * TB + (h * 4 + j)
                        last = dve.tensor_scalar(stage[:, h, j, :], g.x[:, t, :], mean[:, bass.ds(t, 1)],
                                                 rstd[:, bass.ds(t, 1)], ALU.subtract, ALU.mult)
                    last.then_inc(staged, 1)

        @block.tensor
        def _(pe):
            with pe.Fori(0, B) as b:
                for h in range(HALVES):
                    pe.wait_ge(staged, HALVES * b + h + 1)
                    for j in range(4):
                        last = pe.transpose(psT[:, h, j * P:(j + 1) * P], stage[:, h, j, :], g.ident[:, :])
                    last.then_inc(transposed, 1)

        @block.scalar
        def _(act):
            act.sem_inc(psT_free, HALVES)
            act.wait_ge(var_ready, 1)
            act.activation(std, var, ACT.Sqrt).then_inc(std_ready, 1)
            if rms_gamma is not None:
                act.wait_ge(shift_ready, 1)
                with act.Fori(0, B) as b:
                    act.wait_ge(lengths_ready, b)
                    act.sem_inc(waited, 1)
                    for j in range(TB):
                        t = bass.ds(b * TB + j, 1)
                        last = act.activation(square[:, j, :], g.x[:, b * TB + j, :], ACT.Square,
                                              bias=shift[:, t], scale=rstd[:, t], accum_out=lengths[:, t])
                    last.then_inc(lengths_ready, 1)
                act.wait_ge(lengths_ready, B)
                act.activation(lengths, lengths, ACT.Sqrt).then_inc(roots_ready, 1)
            with act.Fori(0, B) as b:
                for h in range(HALVES):
                    act.wait_ge(transposed, HALVES * b + h + 1)
                    act.sem_inc(waited, 1)
                    out = g.xnT[:, b, HALO + h * CH:HALO + (h + 1) * CH]
                    if rms_gamma is None:
                        act.activation(out, psT[:, h, :], ACT.Copy).then_inc(psT_free, 1)
                    else:
                        act.activation(out, psT[:, h, :], ACT.Identity, scale=rms_gamma).then_inc(psT_free, 1)

        if keep_tokens:
            @block.sync
            def _(sp):
                for h in range(HALVES):
                    sp.sem_inc(rows_kept[h], 16)
                with sp.Fori(0, B) as b:
                    for h in range(HALVES):
                        sp.wait_ge(staged, HALVES * b + h + 1)
                        sp.dma_start(g.token_rows[bass.ds(b * L + h * CH, CH), :].rearrange("(j p) c -> p j c", p=P),
                                     stage[:, h, :, :]).then_inc(rows_kept[h], 16)
                for h in range(HALVES):
                    sp.wait_ge(rows_kept[h], 16 * (B + 1))


def ffn_phase(nc, g, tag):
    with Scope(nc, tag) as s:
        w, mu = g.w_ffn, g.mu
        one_minus = s.sb("one_minus", [P, 2])
        part = s.sb("part", [P, 2, CH])
        mixed = s.sb("mixed", [P, HALVES, 2, CH])
        relu = s.sb("relu", [P, HALVES, CH])
        gate = s.sb("gate", [P, HALVES, CH])
        prod = s.sb("prod", [P, HALVES, CH])
        ps_r = s.ps("ps_r", [P, HALVES, CH])
        ps_k = s.ps("ps_k", [P, HALVES, CH])
        ps_v = s.ps("ps_v", [P, HALVES, CH])
        ps_t = s.ps("ps_t", [P, HALVES, CH])
        consts = s.sem("consts")
        waited = s.sem("waited")
        part_ready = s.sem("part_ready")
        mix_ready = s.sem("mix_ready")
        r_ready = s.sem("r_ready")
        k_ready = s.sem("k_ready")
        gate_ready = s.sem("gate_ready")
        relu_ready = s.sem("relu_ready")
        square_ready = s.sem("square_ready")
        v_ready = s.sem("v_ready")
        prod_ready = s.sem("prod_ready")
        back = s.sem("back")
        added = s.sem("added")
        block = s.block()

        @block.scalar
        def _(act):
            act.wait_ge(g.loaded, g.LOADED)
            with act.Fori(0, B) as b:
                for h in range(HALVES):
                    for k in range(2):
                        act.wait_ge(mix_ready, 4 * b + 2 * h + k + 1)
                        act.sem_inc(waited, 1)
                        act.activation(part[:, k, :], g.xnT[:, b, HALO + h * CH:HALO + (h + 1) * CH], ACT.Identity,
                                       scale=mu[:, k:k + 1]).then_inc(part_ready, 1)
                for h in range(HALVES):
                    act.wait_ge(r_ready, HALVES * b + h + 1)
                    act.activation(gate[:, h, :], ps_r[:, h, :], ACT.Sigmoid).then_inc(gate_ready, 1)
                    act.wait_ge(k_ready, HALVES * b + h + 1)
                    act.activation(relu[:, h, :], ps_k[:, h, :], ACT.Relu).then_inc(relu_ready, 1)
                    act.wait_ge(relu_ready, HALVES * b + h + 1)
                    act.activation(relu[:, h, :], relu[:, h, :], ACT.Square).then_inc(square_ready, 1)

        @block.tensor
        def _(pe):
            pe.wait_ge(g.loaded, g.LOADED)
            with pe.Fori(0, B) as b:
                for h in range(HALVES):
                    pe.wait_ge(added, HALVES * b)
                    pe.wait_ge(mix_ready, 4 * b + 2 * h + 1 + 2)
                    pe.matmul(ps_r[:, h, :], w[:, 0, :], mixed[:, h, 0, :], start=True, stop=True).then_inc(r_ready, 1)
                    pe.wait_ge(mix_ready, 4 * b + 2 * h + 2 + 2)
                    pe.matmul(ps_k[:, h, :], w[:, 1, :], mixed[:, h, 1, :], start=True, stop=True).then_inc(k_ready, 1)
                for h in range(HALVES):
                    pe.wait_ge(square_ready, HALVES * b + h + 1)
                    pe.matmul(ps_v[:, h, :], w[:, 2, :], relu[:, h, :], start=True, stop=True).then_inc(v_ready, 1)
                for h in range(HALVES):
                    pe.wait_ge(prod_ready, HALVES * b + h + 1)
                    for j in range(4):
                        last = pe.transpose(ps_t[:, h, j * P:(j + 1) * P], prod[:, h, j * P:(j + 1) * P], g.ident[:, :])
                    last.then_inc(back, 1)

        @block.vector
        def _(dve):
            dve.wait_ge(g.loaded, g.LOADED)
            dve.tensor_scalar(one_minus[:, :], mu[:, :], -1.0, 1.0, ALU.mult, ALU.add).then_inc(consts, 1)
            dve.wait_ge(consts, 1)
            dve.sem_inc(mix_ready, 2)
            with dve.Fori(0, B) as b:
                for h in range(HALVES):
                    for k in range(2):
                        dve.wait_ge(part_ready, 4 * b + 2 * h + k + 1)
                        lo = HALO - 1 + h * CH
                        dve.scalar_tensor_tensor(out=mixed[:, h, k, :], in0=g.xnT[:, b, lo:lo + CH],
                                                 scalar=one_minus[:, k:k + 1], in1=part[:, k, :],
                                                 op0=ALU.mult, op1=ALU.add).then_inc(mix_ready, 1)
                for h in range(HALVES):
                    dve.wait_ge(gate_ready, HALVES * b + h + 1)
                    dve.wait_ge(v_ready, HALVES * b + h + 1)
                    dve.tensor_tensor(prod[:, h, :], gate[:, h, :], ps_v[:, h, :], ALU.mult).then_inc(prod_ready, 1)
                for h in range(HALVES):
                    dve.wait_ge(back, HALVES * b + h + 1)
                    x = g.x[:, bass.ds(b * TB + h * 4, 4), :]
                    dve.scalar_tensor_tensor(out=x, in0=ps_t[:, h, :].rearrange("p (j c) -> p j c", j=4), scalar=0.5,
                                             in1=x, op0=ALU.mult, op1=ALU.add).then_inc(added, 1)


def mamba_phase(nc, g, A):
    with Scope(nc, "mamba") as s:
        xin = s.sb("xin", [P, NB, HALO + L])
        silu1 = s.sb("silu1", [P, NB, CH])
        silu2 = s.sb("silu2", [P, NB, CH])
        xc = s.sb("xc", [P, NB, L])
        zs = s.sb("zs", [P, NB, L])
        low = s.sb("low", [R, CH])
        bc_hi = s.sb("bc_hi", [3 * BC, CH], BF16)
        bc_rest = s.sb("bc_rest", [3 * BC, CH])
        bc_mid = s.sb("bc_mid", [3 * BC, CH], BF16)
        bc = s.sb("bc", [3 * BC, L], BF16)
        v = s.sb("v", [P, NB, CH])
        mag = s.sb("mag", [P, NB, CH])
        pos = s.sb("pos", [P, NB, CH])
        ex = s.sb("ex", [P, NB, CH])
        ln = s.sb("ln", [P, NB, CH])
        low_bits = s.sb("low_bits", [P, NB, CH])
        delta = s.sb("delta", [P, NB, L])
        u = s.sb("u", [P, NB, L])
        decay = s.sb("decay", [P, NB, L])
        drive = s.sb("drive", [P, NB, L])
        state = s.sb("state", [P, NB, L])
        c_all = s.sb("c_all", [P, 2, L])
        read = s.sb("read", [P, NB, L])
        y = s.sb("y", [P, NB, L])
        taps = s.sb("taps", [P, NB, 2 * KW, P])
        pick = s.sb("pick", [3 * BC, BC, P], BF16)
        gates = s.sb("gates", [P, 2])
        gsum = s.sb("gsum", [P, 1])
        neg_a = s.sb("neg_a", [P, NB, NS])
        bank = s.ps("bank", [P, 8, CH])

        gate_exp = s.sem("gate_exp")
        consts = s.sem("consts")
        consts_done = s.sem("consts_done")
        pick_steps = s.sem("pick_steps")
        x_ready = s.sem("x_ready")
        x_copied = s.sem("x_copied")
        conv_ready = s.sem("conv_ready")
        silu_ready = s.sem("silu_ready")
        z_ready = s.sem("z_ready")
        zs_ready = s.sem("zs_ready")
        xc_part = s.sem("xc_part")
        xc_ready = s.sem("xc_ready")
        low_ready = s.sem("low_ready")
        low_copied = s.sem("low_copied")
        bc_split = s.sem("bc_split")
        bc_rest_ready = s.sem("bc_rest_ready")
        bc_ready = s.sem("bc_ready")
        dt_ready = s.sem("dt_ready")
        v_ready = s.sem("v_ready")
        mag_ready = s.sem("mag_ready")
        pos_ready = s.sem("pos_ready")
        ex_ready = s.sem("ex_ready")
        ln_ready = s.sem("ln_ready")
        delta_steps = s.sem("delta_steps")
        delta_ready = s.sem("delta_ready")
        u_ready = s.sem("u_ready")
        b_spread = s.sem("b_spread")
        c_spread = s.sem("c_spread")
        c_copied = s.sem("c_copied")
        decay_ready = s.sem("decay_ready")
        driven = s.sem("driven")
        scanned = s.sem("scanned")
        read_ready = s.sem("read_ready")
        summed = s.sem("summed")
        y_part = s.sem("y_part")
        y_ready = s.sem("y_ready")
        projected = s.sem("projected")
        added = s.sem("added")
        block = s.block()

        def xn(b, h):
            return g.xnT[:, b, HALO + h * CH:HALO + (h + 1) * CH]

        def cols(h):
            return slice(h * CH, (h + 1) * CH)

        @block.gpsimd
        def _(pool):
            pool.memset(xin[:, :, 0:HALO], 0.0).then_inc(pick_steps, 1)
            pool.memset(pick[:, :, :], 0.0).then_inc(pick_steps, 1)
            for part in range(3):
                pool.wait_ge(pick_steps, 2 + part)
                pool.affine_select(out=pick[:, :, :], in_=pick[:, :, :], compare_op=ALU.not_equal, fill=1.0,
                                   base=-BC * part, pattern=[[-1, BC], [0, P]], channel_multiplier=1)\
                    .then_inc(pick_steps, 1)
            pool.sem_inc(read_ready, 4)
            with pool.Fori(0, B) as b:
                for h in range(HALVES):
                    pool.wait_ge(xc_ready, HALVES * b + h + 1)
                    pool.wait_ge(delta_ready, HALVES * b + h + 1)
                    pool.tensor_tensor(u[:, :, cols(h)], delta[:, :, cols(h)], xc[:, :, cols(h)], ALU.mult)\
                        .then_inc(u_ready, 1)
                for n in range(NS):
                    for blk in range(NB):
                        j = NB * n + blk
                        pool.wait_ge(c_copied, NS * b + n + 1)
                        pool.wait_ge(scanned, NB * NS * b + j + 1 + NB)
                        pool.wait_ge(summed, NB * NS * b + j + 1)
                        pool.tensor_tensor(read[:, blk, :], state[:, blk, :], c_all[:, n % 2, :], ALU.mult)\
                            .then_inc(read_ready, 1)

        @block.scalar
        def _(act):
            act.wait_ge(g.loaded, g.LOADED)
            act.activation(gates[:, :], g.gates[:, :], ACT.Exp, accum_out=gsum[:, :]).then_inc(gate_exp, 1)
            act.activation(neg_a[:, :, :], g.a_log[:, :, :], ACT.Exp).then_inc(gate_exp, 1)
            with act.Fori(0, B) as b:
                for h in range(HALVES):
                    for blk in range(NB):
                        act.wait_ge(x_ready, 2 * NB * b + NB * h + blk + 1)
                        act.activation(xin[:, blk, HALO + h * CH:HALO + (h + 1) * CH], bank[:, blk, :], ACT.Copy)\
                            .then_inc(x_copied, 1)
                    for blk in range(NB):
                        for k in range(2):
                            act.wait_ge(conv_ready, 8 * b + 4 * h + 2 * blk + k + 1)
                            act.wait_ge(xc_ready, HALVES * b + h)
                            act.activation((silu1, silu2)[k][:, blk, :], bank[:, 2 + 2 * blk + k, :], ACT.Silu,
                                           bias=g.conv_b[:, blk, k:k + 1]).then_inc(silu_ready, 1)
                    for blk in range(NB):
                        act.wait_ge(z_ready, 4 * b + NB * h + blk + 1)
                        act.wait_ge(y_ready, NB * b)
                        act.activation(zs[:, blk, cols(h)], bank[:, 6 + blk, :], ACT.Silu).then_inc(zs_ready, 1)
                    act.wait_ge(low_ready, HALVES * b + h + 1)
                    act.activation(low[:, :], bank[0:R, 0, :], ACT.Copy).then_inc(low_copied, 1)
                    act.activation(bc_hi[:, :], bank[0:3 * BC, 1, :], ACT.Copy).then_inc(bc_split, 1)
                    act.activation(bc[0:BC, cols(h)], bank[0:BC, 1, :], ACT.Copy).then_inc(bc_split, 1)
                    act.wait_ge(bc_rest_ready, HALVES * b + h + 1)
                    act.activation(bc_mid[2 * BC:3 * BC, :], bc_rest[2 * BC:3 * BC, :], ACT.Copy).then_inc(bc_split, 1)
                    act.activation(bc[BC:2 * BC, cols(h)], bc_rest[BC:2 * BC, :], ACT.Copy).then_inc(bc_split, 1)
                    for blk in range(NB):
                        act.wait_ge(dt_ready, 4 * b + NB * h + blk + 1)
                        act.activation(v[:, blk, :], bank[:, 2 + blk, :], ACT.Identity, bias=g.b_dt[:, blk:blk + 1])\
                            .then_inc(v_ready, 1)
                    act.wait_ge(v_ready, 4 * b + NB * h + NB)
                    act.activation(mag[:, :, :], v[:, :, :], ACT.Abs).then_inc(mag_ready, 1)
                    act.wait_ge(mag_ready, HALVES * b + h + 1)
                    act.wait_ge(delta_ready, HALVES * b + h)
                    act.activation(ex[:, :, :], mag[:, :, :], ACT.Exp, scale=-1.0).then_inc(ex_ready, 1)
                    act.wait_ge(ex_ready, HALVES * b + h + 1)
                    act.activation(ln[:, :, :], ex[:, :, :], ACT.Ln, bias=1.0).then_inc(ln_ready, 1)
                act.wait_ge(delta_ready, HALVES * b + HALVES)
                for n in range(NS):
                    for blk in range(NB):
                        j = NB * n + blk
                        act.wait_ge(scanned, NB * NS * b + j + 1)
                        act.activation(decay[:, blk, :], delta[:, blk, :], ACT.Exp, scale=g.neg_a[:, blk, n:n + 1])\
                            .then_inc(decay_ready, 1)
                    act.wait_ge(c_spread, NS * b + n + 1)
                    act.wait_ge(read_ready, NB * NS * b + NB * n + 2)
                    act.activation(c_all[:, n % 2, :], bank[:, 2:4, :].rearrange("p k t -> p (k t)"), ACT.Copy)\
                        .then_inc(c_copied, 1)

        @block.vector
        def _(dve):
            dve.wait_ge(gate_exp, 2)
            dve.reciprocal(gsum[:, :], gsum[:, :]).then_inc(consts, 1)
            dve.tensor_scalar(g.neg_a[:, :, :], neg_a[:, :, :], -1.0, None, ALU.mult).then_inc(consts_done, 1)
            for blk in range(NB):
                for k in range(2 * KW):
                    dve.tensor_scalar(taps[:, blk, k, :], g.ident[:, :], g.conv_w[:, blk, k:k + 1], None, ALU.mult)\
                        .then_inc(consts_done, 1)
            dve.wait_ge(consts, 1)
            dve.tensor_scalar(gates[:, :], gates[:, :], gsum[:, :], None, ALU.mult).then_inc(consts, 1)
            dve.wait_ge(consts, 2)
            dve.sem_inc(scanned, NB)
            with dve.Fori(0, B) as b:
                for h in range(HALVES):
                    dve.wait_ge(silu_ready, 8 * b + 4 * h + 4)
                    dve.wait_ge(u_ready, HALVES * b)
                    dve.tensor_scalar(xc[:, :, cols(h)], silu1[:, :, :], gates[:, 0:1], None, ALU.mult)\
                        .then_inc(xc_part, 1)
                    dve.wait_ge(xc_part, HALVES * b + h + 1)
                    dve.scalar_tensor_tensor(out=xc[:, :, cols(h)], in0=silu2[:, :, :], scalar=gates[:, 1:2],
                                             in1=xc[:, :, cols(h)], op0=ALU.mult, op1=ALU.add).then_inc(xc_ready, 1)
                    dve.wait_ge(bc_split, 8 * b + 4 * h + 1)
                    dve.tensor_tensor(bc_rest[BC:2 * BC, :], bank[BC:2 * BC, 1, :], bc_hi[BC:2 * BC, :], ALU.subtract)
                    dve.tensor_tensor(bc_rest[2 * BC:3 * BC, :], bank[2 * BC:3 * BC, 1, :], bc_hi[2 * BC:3 * BC, :],
                                      ALU.subtract).then_inc(bc_rest_ready, 1)
                    dve.wait_ge(bc_split, 8 * b + 4 * h + 4)
                    dve.tensor_tensor(bc[2 * BC:3 * BC, cols(h)], bc_rest[2 * BC:3 * BC, :], bc_mid[2 * BC:3 * BC, :],
                                      ALU.subtract).then_inc(bc_ready, 1)
                    dve.wait_ge(v_ready, 4 * b + NB * h + NB)
                    dve.tensor_scalar(pos[:, :, :], v[:, :, :], 0.0, None, ALU.max).then_inc(pos_ready, 1)
                    c = 3 * (HALVES * b + h)
                    dve.wait_ge(ex_ready, HALVES * b + h + 1)
                    dve.tensor_scalar(low_bits[:, :, :], ex[:, :, :], 1.0, -1.0, ALU.add, ALU.add).then_inc(delta_steps, 1)
                    dve.wait_ge(delta_steps, c + 1)
                    dve.tensor_tensor(low_bits[:, :, :], ex[:, :, :], low_bits[:, :, :], ALU.subtract)\
                        .then_inc(delta_steps, 1)
                    dve.wait_ge(ln_ready, HALVES * b + h + 1)
                    dve.wait_ge(delta_steps, c + 2)
                    dve.tensor_tensor(low_bits[:, :, :], ln[:, :, :], low_bits[:, :, :], ALU.add).then_inc(delta_steps, 1)
                    dve.wait_ge(delta_steps, c + 3)
                    dve.wait_ge(pos_ready, HALVES * b + h + 1)
                    dve.tensor_tensor(delta[:, :, cols(h)], pos[:, :, :], low_bits[:, :, :], ALU.add)\
                        .then_inc(delta_ready, 1)
                dve.wait_ge(u_ready, HALVES * b + HALVES)
                for n in range(NS):
                    for blk in range(NB):
                        dve.wait_ge(b_spread, NS * b + n + 1)
                        dve.wait_ge(scanned, NB * NS * b + NB * n + blk + 1)
                        dve.tensor_tensor(drive[:, blk, :], u[:, blk, :],
                                          bank[:, 0:2, :].rearrange("p k t -> p (k t)"), ALU.mult).then_inc(driven, 1)
                    for blk in range(NB):
                        j = NB * n + blk
                        dve.wait_ge(decay_ready, NB * NS * b + j + 1)
                        dve.wait_ge(driven, NB * NS * b + j + 1)
                        dve.wait_ge(read_ready, NB * NS * b + j + 3)
                        dve.tensor_tensor_scan(state[:, blk, :], decay[:, blk, :], drive[:, blk, :], 0.0,
                                               ALU.mult, ALU.add).then_inc(scanned, 1)
                for blk in range(NB):
                    dve.wait_ge(summed, NB * NS * b + NB * NS + NB)
                    dve.wait_ge(projected, b)
                    dve.scalar_tensor_tensor(out=y[:, blk, :], in0=xc[:, blk, :], scalar=g.d_param[:, blk:blk + 1],
                                             in1=bank[:, 4 + 2 * blk:6 + 2 * blk, :].rearrange("p k t -> p (k t)"),
                                             op0=ALU.mult, op1=ALU.add).then_inc(y_part, 1)
                for blk in range(NB):
                    dve.wait_ge(y_part, NB * b + blk + 1)
                    dve.wait_ge(zs_ready, 4 * b + 4)
                    dve.tensor_tensor(y[:, blk, :], y[:, blk, :], zs[:, blk, :], ALU.mult).then_inc(y_ready, 1)
                dve.wait_ge(projected, b + 1)
                xb = g.x[:, bass.ds(b * TB, TB), :]
                dve.tensor_tensor(xb, xb, bank[:, 0:2, :].rearrange("p k (j c) -> p (k j) c", c=D), ALU.add)\
                    .then_inc(added, 1)

        @block.tensor
        def _(pe):
            pe.wait_ge(consts_done, 1 + NB * 2 * KW)
            pe.wait_ge(pick_steps, 5)
            pe.sem_inc(summed, NB)
            with pe.Fori(0, B) as b:
                for h in range(HALVES):
                    pe.wait_ge(added, b)
                    pe.wait_ge(bc_rest_ready, HALVES * b + h)
                    pe.wait_ge(bc_split, 8 * b + 4 * h)
                    for blk in range(NB):
                        pe.matmul(bank[:, blk, :], g.w_in[:, blk * P:(blk + 1) * P], xn(b, h), start=True, stop=True)\
                            .then_inc(x_ready, 1)
                    pe.wait_ge(zs_ready, 4 * b + NB * h)
                    for blk in range(NB):
                        pe.matmul(bank[:, 6 + blk, :], g.w_in[:, (NB + blk) * P:(NB + blk + 1) * P], xn(b, h),
                                  start=True, stop=True).then_inc(z_ready, 1)
                    pe.wait_ge(v_ready, 4 * b + NB * h)
                    pe.wait_ge(silu_ready, 8 * b + 4 * h)
                    pe.wait_ge(c_copied, NS * b)
                    for blk in range(NB):
                        pe.wait_ge(x_copied, 2 * NB * b + NB * h + blk + 1)
                        for k in range(2):
                            for tap in range(KW):
                                at = HALO + h * CH - (k + 1) * (KW - 1 - tap)
                                last = pe.matmul(bank[:, 2 + 2 * blk + k, :], taps[:, blk, k * KW + tap, :],
                                                 xin[:, blk, at:at + CH], start=(tap == 0), stop=(tap == KW - 1))
                            last.then_inc(conv_ready, 1)
                    pe.wait_ge(xc_ready, HALVES * b + h + 1)
                    for blk in range(NB):
                        pe.matmul(bank[0:R, 0, :], g.w_x[:, blk, 0:R], xc[:, blk, cols(h)],
                                  start=(blk == 0), stop=(blk == NB - 1))
                    for blk in range(NB):
                        last = pe.matmul(bank[0:3 * BC, 1, :], g.w_x[:, blk, R:R + 3 * BC], xc[:, blk, cols(h)],
                                         start=(blk == 0), stop=(blk == NB - 1))
                    last.then_inc(low_ready, 1)
                    pe.wait_ge(low_copied, HALVES * b + h + 1)
                    pe.wait_ge(silu_ready, 8 * b + 4 * h + 4)
                    for blk in range(NB):
                        pe.matmul(bank[:, 2 + blk, :], g.w_dt[:, blk * P:(blk + 1) * P], low[:, :],
                                  start=True, stop=True).then_inc(dt_ready, 1)
                pe.wait_ge(bc_ready, HALVES * b + HALVES)
                pe.wait_ge(zs_ready, 4 * b + 4)
                pe.wait_ge(v_ready, 4 * b + 4)

                def spread(n):
                    pe.wait_ge(driven, NB * NS * b + NB * n)
                    for h in range(HALVES):
                        last = pe.matmul(bank[:, h, :], pick[:, n, :], bc[:, cols(h)], start=True, stop=True)
                    last.then_inc(b_spread, 1)
                    pe.wait_ge(c_copied, NS * b + n)
                    for h in range(HALVES):
                        last = pe.matmul(bank[:, 2 + h, :], pick[:, NS + n, :], bc[:, cols(h)], start=True, stop=True)
                    last.then_inc(c_spread, 1)

                spread(0)
                for n in range(NS):
                    if n + 1 < NS:
                        spread(n + 1)
                    for blk in range(NB):
                        j = NB * n + blk
                        pe.wait_ge(read_ready, NB * NS * b + j + 5)
                        for h in range(HALVES):
                            last = pe.matmul(bank[:, 4 + 2 * blk + h, :], g.ident[:, :], read[:, blk, cols(h)],
                                             start=(n == 0), stop=(n == NS - 1))
                        last.then_inc(summed, 1)
                pe.wait_ge(y_ready, NB * b + NB)
                for t in range(TB):
                    for blk in range(NB):
                        last = pe.matmul(bank[:, t // 4, (t % 4) * P:(t % 4 + 1) * P], y[:, blk, t * P:(t + 1) * P],
                                         g.w_out[:, blk, :], start=(blk == 0), stop=(blk == NB - 1))
                last.then_inc(projected, 1)

        @block.sync
        def _(sp):
            sp.wait_ge(added, B)


def load_experts_phase(nc, g, A):
    with Scope(nc, "fetch") as s:
        block = s.block()

        @block.sync
        def _(sp):
            for dst, name in g.late_weights:
                sp.dma_start(dst, A[name]).then_inc(g.late_loaded, 16)


def moe_route_phase(nc, g, tag):
    with Scope(nc, tag) as s:
        def field(name):
            return s.sb(name, [P, NT, E])

        def column(name):
            return s.sb(name, [P, NT])

        prob, score, equal = field("prob"), field("score"), field("equal")
        first, second, both = field("first"), field("second"), field("both")
        total, until, place = field("total"), field("until"), field("place")
        top, denom, best, p1, p2 = (column(x) for x in ("top", "denom", "best", "p1", "p2"))
        both16 = s.sb("both16", [P, NT * E], BF16)
        rev = s.sb("rev", [P, E])
        ones_col = s.sb("ones_col", [P, NT])
        before = s.sb("before", [P, P], BF16)
        everyone = s.sb("everyone", [P, P], BF16)
        count_i = s.sb("count_i", [P, E], I32)
        tiles = s.sb("tiles", [P, E])
        tiles_until = s.sb("tiles_until", [P, E])
        base = s.sb("base", [P, E])
        row_f = s.sb("row_f", [P, 2, NT])
        row_i = s.sb("row_i", [P, 2 * NT], I32)
        part_i = s.sb("part_i", [P, 2, 2 * NT], I32)
        row_lo = s.sb("row_lo", [P, 2 * NT])
        row_hi = s.sb("row_hi", [P, 2 * NT])
        lane = s.sb("lane", [P, P])
        tile_of = s.sb("tile_of", [P, MT])
        choice = s.sb("choice", [P, 2 * NT])
        in_lane = s.sb("in_lane", [P, 2 * NT, P])
        in_tile = s.sb("in_tile", [P, 2 * NT, MT])
        found = s.sb("found", [P, MT])
        none = s.sb("none", [P, MT])
        source_f = s.sb("source_f", [P, MT])
        source_i = s.sb("source_i", [P, MT], I32)
        ps_list = s.ps("ps_list", [P, CH])
        lists_ready = s.sem("lists_ready")
        list_found = s.sem("list_found")
        tile_no = s.sb("tile_no", [1, MT, E])
        owner = s.sb("owner", [1, MT])
        ps_logit = s.ps("ps_logit", [P, CH])
        ps_before = s.ps("ps_before", [P, CH])
        ps_total = s.ps("ps_total", [P, CH])
        made = s.sem("made")
        before_zero = s.sem("before_zero")
        logits_ready = s.sem("logits_ready")
        shifted = s.sem("shifted")
        exp_ready = s.sem("exp_ready")
        chain = s.sem("chain")
        choice_ready = s.sem("choice_ready")
        ranks_ready = s.sem("ranks_ready")
        rows_ready = s.sem("rows_ready")
        block = s.block()
        logits = ps_logit[:, 0:NT * E].rearrange("p (t e) -> p t e", e=E)

        GROUP = 16

        def spread(col):
            return col[:, :, None].to_broadcast([P, NT, E])

        @block.gpsimd
        def _(pool):
            pool.iota(rev[:, :], [[-1, E]], base=E, channel_multiplier=0,
                      allow_small_or_imprecise_dtypes=True).then_inc(made, 1)
            pool.iota(tile_no[:, :, :], [[1, MT], [0, E]], base=0, channel_multiplier=0,
                      allow_small_or_imprecise_dtypes=True).then_inc(made, 1)
            pool.iota(lane[:, :], [[1, P]], base=0, channel_multiplier=0,
                      allow_small_or_imprecise_dtypes=True).then_inc(made, 1)
            pool.iota(tile_of[:, :], [[1, MT]], base=0, channel_multiplier=0,
                      allow_small_or_imprecise_dtypes=True).then_inc(made, 1)
            pool.iota(choice[:, :], [[P, 2 * NT]], base=1, channel_multiplier=1,
                      allow_small_or_imprecise_dtypes=True).then_inc(made, 1)
            pool.memset(ones_col[:, :], 1.0).then_inc(made, 1)
            pool.memset(everyone[:, :], 1.0).then_inc(made, 1)
            pool.memset(before[:, :], 1.0).then_inc(before_zero, 1)
            pool.wait_ge(before_zero, 1)
            pool.affine_select(out=before[:, :], in_=before[:, :], compare_op=ALU.is_gt, fill=0.0,
                               base=0, pattern=[[1, P]], channel_multiplier=-1).then_inc(made, 1)

        @block.tensor
        def _(pe):
            pe.wait_ge(g.late_loaded, g.LATE_LOADED)
            for t in range(NT):
                lo = HALO + (t % TB) * P
                last = pe.matmul(ps_logit[:, t * E:(t + 1) * E], g.xnT[:, t // TB, lo:lo + P], g.router[:, :],
                                 start=True, stop=True)
            last.then_inc(logits_ready, 1)
            pe.wait_ge(choice_ready, 1)
            pe.wait_ge(made, 8)
            pe.matmul(ps_before[:, 0:NT * E], before[:, :], both16[:, :], start=True, stop=True)
            pe.matmul(ps_total[:, 0:NT * E], everyone[:, :], both16[:, :], start=True, stop=True)\
                .then_inc(ranks_ready, 1)
            for T in range(2 * NT):
                if T % GROUP == 0:
                    pe.wait_ge(lists_ready, T // GROUP + 1)
                last = pe.matmul(ps_list[:, 0:MT], in_lane[:, T, :], in_tile[:, T, :], start=(T == 0),
                                 stop=(T == 2 * NT - 1))
            last.then_inc(list_found, 1)

        @block.scalar
        def _(act):
            act.wait_ge(shifted, 1)
            act.activation(score[:, :, :], prob[:, :, :], ACT.Exp).then_inc(exp_ready, 1)

        @block.vector
        def _(dve):
            done = [0]

            def then(instruction):
                done[0] += 1
                instruction.then_inc(chain, 1)
                dve.wait_ge(chain, done[0])

            dve.wait_ge(made, 8)
            dve.wait_ge(logits_ready, 1)
            then(dve.tensor_reduce(top[:, :], logits, AX.X, ALU.max))
            dve.tensor_tensor(prob[:, :, :], logits, spread(top), ALU.subtract).then_inc(shifted, 1)
            dve.wait_ge(exp_ready, 1)
            then(dve.tensor_reduce(denom[:, :], score[:, :, :], AX.X, ALU.add))
            then(dve.reciprocal(denom[:, :], denom[:, :]))
            then(dve.tensor_tensor(prob[:, :, :], score[:, :, :], spread(denom), ALU.mult))
            for chosen, p in ((first, p1), (second, p2)):
                then(dve.tensor_reduce(p[:, :], prob[:, :, :], AX.X, ALU.max))
                then(dve.tensor_tensor(equal[:, :, :], prob[:, :, :], spread(p), ALU.is_equal))
                then(dve.tensor_tensor(score[:, :, :], equal[:, :, :], rev[:, None, :].to_broadcast([P, NT, E]),
                                       ALU.mult))
                then(dve.tensor_reduce(best[:, :], score[:, :, :], AX.X, ALU.max))
                then(dve.tensor_tensor(chosen[:, :, :], score[:, :, :], spread(best), ALU.is_equal))
                if chosen is first:
                    then(dve.scalar_tensor_tensor(out=prob[:, :, :], in0=chosen[:, :, :], scalar=-2.0,
                                                  in1=prob[:, :, :], op0=ALU.mult, op1=ALU.add))
            then(dve.tensor_tensor(both[:, :, :], first[:, :, :], second[:, :, :], ALU.add))
            dve.tensor_copy(both16[:, :], both[:, :, :].rearrange("p t e -> p (t e)")).then_inc(choice_ready, 1)
            then(dve.tensor_tensor(denom[:, :], p1[:, :], p2[:, :], ALU.add))
            then(dve.tensor_scalar(denom[:, :], denom[:, :], 1e-9, None, ALU.add))
            then(dve.reciprocal(denom[:, :], denom[:, :]))
            then(dve.tensor_scalar(denom[:, :], denom[:, :], 0.5, None, ALU.mult))
            dve.tensor_tensor(g.weight[:, 0, :], p1[:, :], denom[:, :], ALU.mult).then_inc(rows_ready, 1)
            dve.tensor_tensor(g.weight[:, 1, :], p2[:, :], denom[:, :], ALU.mult).then_inc(rows_ready, 1)
            dve.wait_ge(ranks_ready, 1)
            then(dve.tensor_copy(total[:, :, :], ps_total[:, 0:NT * E].rearrange("p (t e) -> p t e", e=E)))
            for e in range(E):
                dve.tensor_tensor_scan(until[:, :, e], ones_col[:, :], total[:, :, e], 0.0, ALU.mult, ALU.add)\
                    .then_inc(chain, 1)
            done[0] += E
            dve.wait_ge(chain, done[0])
            then(dve.tensor_scalar(tiles[:, :], until[:, NT - 1, :], float(P - 1), None, ALU.add))
            then(dve.tensor_copy(count_i[:, :], tiles[:, :]))
            then(dve.tensor_scalar(count_i[:, :], count_i[:, :], 7, None, ALU.arith_shift_right))
            then(dve.tensor_copy(tiles[:, :], count_i[:, :]))
            then(dve.tensor_tensor_scan(tiles_until[:, :], ones_col[:, 0:E], tiles[:, :], 0.0, ALU.mult, ALU.add))
            then(dve.tensor_tensor(base[:, :], tiles_until[:, :], tiles[:, :], ALU.subtract))
            then(dve.tensor_tensor(until[:, :, :], until[:, :, :], total[:, :, :], ALU.subtract))
            then(dve.tensor_tensor(until[:, :, :], until[:, :, :],
                                   ps_before[:, 0:NT * E].rearrange("p (t e) -> p t e", e=E), ALU.add))
            then(dve.scalar_tensor_tensor(out=place[:, :, :], in0=base[:, None, :].to_broadcast([P, NT, E]),
                                          scalar=float(P), in1=until[:, :, :], op0=ALU.mult, op1=ALU.add))
            for k, chosen in enumerate((first, second)):
                then(dve.tensor_tensor(total[:, :, :], chosen[:, :, :], place[:, :, :], ALU.mult))
                then(dve.tensor_reduce(row_f[:, k, :], total[:, :, :], AX.X, ALU.add))
            then(dve.tensor_copy(row_i[:, :], row_f[:, :, :].rearrange("p k t -> p (k t)")))
            dve.tensor_scalar(part_i[:, 0, :], row_i[:, :], P - 1, None, ALU.bitwise_and).then_inc(chain, 1)
            dve.tensor_scalar(part_i[:, 1, :], row_i[:, :], 7, None, ALU.arith_shift_right).then_inc(chain, 1)
            done[0] += 2
            dve.wait_ge(chain, done[0])
            dve.tensor_copy(row_lo[:, :], part_i[:, 0, :]).then_inc(chain, 1)
            dve.tensor_copy(row_hi[:, :], part_i[:, 1, :]).then_inc(chain, 1)
            done[0] += 2
            dve.wait_ge(chain, done[0])
            for T in range(0, 2 * NT, GROUP):
                some = slice(T, T + GROUP)
                dve.tensor_tensor(in_lane[:, some, :], lane[:, None, :].to_broadcast([P, GROUP, P]),
                                  row_lo[:, some, None].to_broadcast([P, GROUP, P]), ALU.is_equal)
                then(dve.tensor_tensor(in_tile[:, some, :], tile_of[:, None, :].to_broadcast([P, GROUP, MT]),
                                       row_hi[:, some, None].to_broadcast([P, GROUP, MT]), ALU.is_equal))
                dve.tensor_tensor(in_tile[:, some, :], in_tile[:, some, :],
                                  choice[:, some, None].to_broadcast([P, GROUP, MT]), ALU.mult)\
                   .then_inc(lists_ready, 1)
            then(dve.tensor_tensor(tile_no[:, :, :], tile_no[:, :, :], base[0:1, None, :].to_broadcast([1, MT, E]),
                                   ALU.is_ge))
            then(dve.tensor_reduce(owner[:, :], tile_no[:, :, :], AX.X, ALU.add))
            then(dve.tensor_scalar(owner[:, :], owner[:, :], -1.0, None, ALU.add))
            then(dve.tensor_copy(g.owner[:, :], owner[:, :]))
            dve.wait_ge(list_found, 1)
            then(dve.tensor_scalar(found[:, :], ps_list[:, 0:MT], -1.0, None, ALU.add))
            dve.tensor_scalar(none[:, :], found[:, :], 0.0, float(4 * B * L), ALU.is_lt, ALU.mult).then_inc(chain, 1)
            dve.tensor_scalar(source_f[:, :], found[:, :], 0.0, None, ALU.max).then_inc(chain, 1)
            done[0] += 2
            dve.wait_ge(chain, done[0])
            dve.tensor_tensor(found[:, :], found[:, :], none[:, :], ALU.add).then_inc(chain, 1)
            dve.tensor_copy(source_i[:, :], source_f[:, :]).then_inc(chain, 1)
            done[0] += 2
            dve.wait_ge(chain, done[0])
            then(dve.tensor_copy(g.target[:, :], found[:, :]))
            then(dve.tensor_scalar(g.source[:, :], source_i[:, :].bitcast(U32), B * L - 1, None, ALU.bitwise_and))


def moe_expert_phase(nc, g, tag):
    with Scope(nc, tag) as s:
        xs = s.sb("xs", [P, XSLOTS, D])
        xT = s.sb("xT", [P, 2, P])
        pre = s.sb("pre", [P, 2, F])
        hT = s.sb("hT", [P, 2, FC, P])
        ys = s.sb("ys", [P, YSLOTS, D])
        ps_x = s.ps("ps_x", [P, 2, CH])
        ps_h = s.ps("ps_h", [P, 2, CH])
        ps_t = s.ps("ps_t", [P, 2, CH])
        ps_y = s.ps("ps_y", [P, 2, CH])
        x_in = [s.sem(f"x_in{k}") for k in range(XSLOTS)]
        x_turned = s.sem("x_turned")
        xT_ready = s.sem("xT_ready")
        up_ready = s.sem("up_ready")
        pre_ready = s.sem("pre_ready")
        h_turned = s.sem("h_turned")
        hT_ready = s.sem("hT_ready")
        down_ready = s.sem("down_ready")
        y_ready = s.sem("y_ready")
        y_out = [s.sem(f"y_out{k}") for k in range(YSLOTS)]
        block = s.block()

        def steps(eng, step):
            for n in range(XSLOTS):
                step(n, n, n)
            with eng.Fori(1, MT // XSLOTS) as q:
                for r in range(XSLOTS):
                    step(q * XSLOTS + r, r, None)
            for n in range(MT, MT + 3):
                step(n, n % XSLOTS, n)

        def on(n, lag):
            return n is None or 0 <= n - lag < MT

        @block.gpsimd
        def _(pool):
            def gather(n):
                if n >= XSLOTS:
                    pool.wait_ge(x_turned, n - XSLOTS + 1)
                pool.indirect_dma_start(
                    out=xs[:, n % XSLOTS, :], out_offset=None, in_=g.token_rows[:, :],
                    in_offset=bass.IndirectOffsetOnAxis(ap=g.source[:, n:n + 1], axis=0))\
                    .then_inc(x_in[n % XSLOTS], 16)

            for n in range(XSLOTS - 2):
                gather(n)
            for n in range(MT):
                if n + XSLOTS - 2 < MT:
                    gather(n + XSLOTS - 2)
                pool.wait_ge(y_ready, n + 1)
                pool.indirect_dma_start(
                    out=g.expert_rows[:, :], out_offset=bass.IndirectOffsetOnAxis(ap=g.target[:, n:n + 1], axis=0),
                    in_=ys[:, n % YSLOTS, :], in_offset=None, bounds_check=2 * B * L - 1, oob_is_err=False)\
                    .then_inc(y_out[n % YSLOTS], 16)
            for k in range(YSLOTS):
                pool.wait_ge(y_out[k], 16 * (MT // YSLOTS))

        @block.tensor
        def _(pe):
            def step(n, r, known):
                if on(known, 0):
                    k = r % XSLOTS
                    pe.wait_ge(x_in[k], (n - r) * (16 // XSLOTS) + 16 if known is None
                               else 16 * (known // XSLOTS + 1))
                    pe.wait_ge(xT_ready, n + 1)
                    pe.transpose(ps_x[:, r % 2, 0:P], xs[:, k, :], g.ident[:, :]).then_inc(x_turned, 1)
                if on(known, 1):
                    m = (r + 1) % 2
                    e = pe.value_load(g.owner[0:1, bass.ds(n - 1, 1)], min_val=0, max_val=E - 1)
                    pe.wait_ge(xT_ready, n - 1 + 3)
                    pe.wait_ge(pre_ready, n - 1 + 1)
                    pe.matmul(ps_h[:, m, :], xT[:, m, :], g.w1[:, bass.ds(e * F, F)], start=True, stop=True)\
                        .then_inc(up_ready, 1)
                if on(known, 2):
                    m = r % 2
                    pe.wait_ge(pre_ready, n - 2 + 3)
                    pe.wait_ge(hT_ready, n - 2 + 1)
                    for c in range(FC):
                        last = pe.transpose(ps_t[:, m, c * P:(c + 1) * P], pre[:, m, c * P:(c + 1) * P], g.ident[:, :])
                    last.then_inc(h_turned, 1)
                if on(known, 3):
                    m = (r + 1) % 2
                    e = pe.value_load(g.owner[0:1, bass.ds(n - 3, 1)], min_val=0, max_val=E - 1)
                    pe.wait_ge(hT_ready, n - 3 + 3)
                    pe.wait_ge(y_ready, n - 3 + 1 - 2 if known is None else max(known - 4, 0))
                    for c in range(FC):
                        last = pe.matmul(ps_y[:, m, 0:D], hT[:, m, c, :], g.w2[:, bass.ds(e * F + c * D, D)],
                                         start=(c == 0), stop=(c == FC - 1))
                    last.then_inc(down_ready, 1)

            steps(pe, step)

        @block.scalar
        def _(act):
            act.sem_inc(xT_ready, 2)
            act.sem_inc(hT_ready, 2)

            def step(n, r, known):
                if on(known, 0):
                    act.wait_ge(x_turned, n + 1)
                    if known is None or known >= 2:
                        act.wait_ge(up_ready, n - 1)
                    act.activation(xT[:, r % 2, :], ps_x[:, r % 2, 0:P], ACT.Copy).then_inc(xT_ready, 1)
                if on(known, 2):
                    act.wait_ge(h_turned, n - 2 + 1)
                    if known is None or known >= 4:
                        act.wait_ge(down_ready, n - 3)
                    act.activation(hT[:, r % 2, :, :].rearrange("p c t -> p (c t)"), ps_t[:, r % 2, :], ACT.Relu)\
                        .then_inc(hT_ready, 1)

            steps(act, step)

        @block.vector
        def _(dve):
            dve.sem_inc(pre_ready, 2)

            def step(n, r, known):
                if on(known, 1):
                    m = (r + 1) % 2
                    e = dve.value_load(g.owner[0:1, bass.ds(n - 1, 1)], min_val=0, max_val=E - 1)
                    dve.wait_ge(up_ready, n - 1 + 1)
                    if known is None or known >= 3:
                        dve.wait_ge(h_turned, n - 2)
                    dve.tensor_tensor(pre[:, m, :], ps_h[:, m, :], g.b1[:, bass.ds(e * F, F)], ALU.add)\
                        .then_inc(pre_ready, 1)
                if on(known, 3):
                    k = (r + 1) % YSLOTS
                    e = dve.value_load(g.owner[0:1, bass.ds(n - 3, 1)], min_val=0, max_val=E - 1)
                    dve.wait_ge(down_ready, n - 3 + 1)
                    if known is None:
                        first = (r - 3) % YSLOTS
                        dve.wait_ge(y_out[k], (n - 3 - first) * (16 // YSLOTS))
                    elif known - 3 >= YSLOTS:
                        dve.wait_ge(y_out[k], 16 * ((known - 3) // YSLOTS))
                    dve.tensor_tensor(ys[:, k, :], ps_y[:, m_of(r), 0:D], g.b2[:, bass.ds(e * D, D)], ALU.add)\
                        .then_inc(y_ready, 1)

            def m_of(r):
                return (r + 1) % 2

            steps(dve, step)


def moe_combine_phase(nc, g, tag):
    with Scope(nc, tag) as s:
        GROUP = 4
        rows = s.sb("rows", [P, 2, NT, D])
        fetched = [s.sem(f"fetched{q}") for q in range(NT // GROUP)]
        half_added = s.sem("half_added")
        block = s.block()

        @block.sync
        def _(sp):
            src = g.expert_rows.rearrange("(k t p) c -> p k t c", p=P, t=NT)
            for q in range(NT // GROUP):
                some = slice(q * GROUP, (q + 1) * GROUP)
                for k in range(2):
                    sp.dma_start(rows[:, k, some, :], src[:, k, some, :]).then_inc(fetched[q], 16)

        @block.vector
        def _(dve):
            for q in range(NT // GROUP):
                dve.wait_ge(fetched[q], 16 * 2)
                for k in range(2):
                    for t in range(q * GROUP, (q + 1) * GROUP):
                        if k == 1:
                            dve.wait_ge(half_added, t + 1)
                        last = dve.scalar_tensor_tensor(out=g.x[:, t, :], in0=rows[:, k, t, :],
                                                        scalar=g.weight[:, k, t:t + 1], in1=g.x[:, t, :],
                                                        op0=ALU.mult, op1=ALU.add)
                        if k == 0:
                            last.then_inc(half_added, 1)


def attention_phase(nc, g, A):
    order = [("Q", 0), ("T", 0), ("S", 2), ("Q", 1), ("T", 1), ("S", 3), ("Q", 2), ("T", 2), ("S", 4), ("Q", 3),
             ("T", 3), ("S", 5), ("PV", 0), ("T", 4), ("S", 6), ("PR", 0), ("T", 5), ("S", 7), ("Q", 4), ("T", 6),
             ("Q", 5), ("T", 7), ("S", TB), ("PV", 1), ("S", TB + 1), ("PR", 1)]
    parts = [[(lo, min(lo + 4, i + 1)) for lo in range(0, i + 1, 4)] for i in range(TB)]
    upto = [sum(len(p) for p in parts[:i + 1]) for i in range(TB)]
    NQ, NG = 6, TB // 4
    with Scope(nc, "attn") as s:
        xs = s.sb("xs", [P, L])
        w = s.sb("w", [P, 2, 3 * DH])
        q = s.sb("q", [P, 2, L])
        k = s.sb("k", [P, 2, L])
        v = s.sb("v", [P, 2, TB * DH])
        probs = s.sb("probs", [P, 2, L])
        pT = [s.sb(f"pT{G}", [P, 4 * (G + 1), CH]) for G in range(NG)]
        oT = s.sb("oT", [P, NG, CH])
        neg_max = s.sb("neg_max", [P, 2])
        row_sum = s.sb("row_sum", [P, 2, TB])
        inv_sum = s.sb("inv_sum", [P, NG, 4])
        ident16 = s.sb("ident16", [P, P], BF16)
        causal = s.sb("causal", [P, P], BF16)
        ps_s = s.ps("ps_s", [P, 2, L])
        ps_t = s.ps("ps_t", [P, 2, CH])
        ps_q = s.ps("ps_q", [P, CH])
        ps_o = s.ps("ps_o", [P, CH])
        mask_steps = s.sem("mask_steps")
        x_staged = s.sem("x_staged")
        w_staged = s.sem("w_staged")
        waited = s.sem("waited")
        proj_ready = s.sem("proj_ready")
        proj_copied = s.sem("proj_copied")
        scores_ready = s.sem("scores_ready")
        max_ready = s.sem("max_ready")
        probs_ready = s.sem("probs_ready")
        turned = s.sem("turned")
        pT_copied = s.sem("pT_copied")
        pv_ready = s.sem("pv_ready")
        oT_copied = s.sem("oT_copied")
        out_ready = s.sem("out_ready")
        inv_ready = s.sem("inv_ready")
        added = s.sem("added")
        block = s.block()

        def heads(eng, run):
            with eng.Fori(0, B) as b:
                with eng.Fori(0, H // 2) as pair:
                    for slot in range(2):
                        run(b * H + pair * 2 + slot, b, pair * 2 + slot, slot)

        @block.gpsimd
        def _(pool):
            pool.memset(ident16[:, :], 0.0).then_inc(mask_steps, 1)
            pool.memset(causal[:, :], 0.0).then_inc(mask_steps, 1)
            pool.wait_ge(mask_steps, 2)
            pool.affine_select(out=ident16[:, :], in_=ident16[:, :], compare_op=ALU.not_equal, fill=1.0,
                               base=0, pattern=[[-1, P]], channel_multiplier=1).then_inc(mask_steps, 1)
            pool.affine_select(out=causal[:, :], in_=causal[:, :], compare_op=ALU.is_ge, fill=-1e30,
                               base=0, pattern=[[-1, P]], channel_multiplier=1).then_inc(mask_steps, 1)

            def stage_w(it, h, slot):
                pool.wait_ge(proj_ready, NQ * it)
                pool.sem_inc(waited, 1)
                pool.tensor_copy(w[:, slot, :], g.w_qkv[:, bass.ds(h * 3 * DH, 3 * DH)]).then_inc(w_staged, 1)

            with pool.Fori(0, B) as b:
                pool.wait_ge(proj_ready, NQ * H * b + NQ)
                pool.sem_inc(waited, 1)
                pool.tensor_copy(xs[:, :], g.xnT[:, b, HALO:HALO + L]).then_inc(x_staged, 1)
                with pool.Fori(0, H // 2) as pair:
                    for slot in range(2):
                        stage_w(b * H + pair * 2 + slot, pair * 2 + slot, slot)
            stage_w(B * H, 0, 0)

        def project(eng, it, c, slot):
            eng.wait_ge(proj_copied, NQ * it + c)
            if c == 0:
                eng.wait_ge(w_staged, it + 1)
            if c < 4:
                last = eng.matmul(ps_q[:, :], w[:, slot, (c // 2) * DH:(c // 2 + 1) * DH],
                                  xs[:, (c % 2) * CH:(c % 2 + 1) * CH], start=True, stop=True)
            else:
                for j in range(4):
                    t = (c - 4) * 4 + j
                    last = eng.matmul(ps_q[:, j * DH:(j + 1) * DH], xs[:, t * P:(t + 1) * P],
                                      w[:, slot, 2 * DH:3 * DH], start=True, stop=True)
            last.then_inc(proj_ready, 1)

        def scores(eng, it, i, slot):
            eng.wait_ge(proj_copied, NQ * it + 4)
            eng.wait_ge(probs_ready, TB * it + i + 1)
            n = (i + 1) * P
            for lo in range(0, n, CH):
                hi = min(lo + CH, n)
                last = eng.matmul(ps_s[:, i % 2, lo:hi], q[:, slot, i * P:(i + 1) * P], k[:, slot, lo:hi],
                                  start=True, stop=(hi < n))
            last = eng.matmul(ps_s[:, i % 2, i * P:n], ident16[:, :], causal[:, :], start=False, stop=True)
            last.then_inc(scores_ready, 1)

        @block.tensor
        def _(pe):
            pe.sem_inc(proj_ready, NQ)
            pe.wait_ge(x_staged, 1)
            pe.wait_ge(mask_steps, 4)
            for c in range(NQ):
                project(pe, 0, c, 0)
            scores(pe, 0, 0, 0)
            scores(pe, 0, 1, 0)

            def head(it, b, h, slot):
                for what, i in order:
                    if what == "Q":
                        project(pe, it + 1, i, 1 - slot)
                    elif what == "S":
                        scores(pe, it + i // TB, i % TB, slot if i < TB else 1 - slot)
                    elif what == "T":
                        pe.wait_ge(probs_ready, TB * it + i + 3)
                        for n, (lo, hi) in enumerate(parts[i]):
                            u = upto[i] - len(parts[i]) + n
                            pe.wait_ge(pT_copied, upto[-1] * it + u + 1)
                            for j in range(lo, hi):
                                last = pe.transpose(ps_t[:, u % 2, (j - lo) * P:(j - lo + 1) * P],
                                                    probs[:, i % 2, j * P:(j + 1) * P], g.ident[:, :])
                            last.then_inc(turned, 1)
                    elif what == "PV":
                        pe.wait_ge(pT_copied, upto[-1] * it + upto[4 * i + 3] + 2)
                        pe.wait_ge(proj_copied, NQ * it + NQ)
                        pe.wait_ge(added, NG * it + i)
                        for j in range(4 * i + 4):
                            lo = max(0, j - 4 * i) * P
                            last = pe.matmul(ps_o[:, lo:CH], v[:, slot, j * DH:(j + 1) * DH], pT[i][:, j, lo:CH],
                                             start=(j == 0), stop=(j == 4 * i + 3))
                        last.then_inc(pv_ready, 1)
                    else:
                        pe.wait_ge(oT_copied, NG * it + i + 1)
                        for j in range(4):
                            last = pe.matmul(ps_o[:, j * D:(j + 1) * D], oT[:, i, j * P:(j + 1) * P],
                                             g.w_o[:, bass.ds(h * D, D)], start=True, stop=True)
                        last.then_inc(out_ready, 1)

            heads(pe, head)

        def take_projection(act, it, c, slot):
            act.wait_ge(proj_ready, NQ * it + c + 1 + NQ)
            if c < 4:
                dst = (q, k)[c // 2][:, slot, (c % 2) * CH:(c % 2 + 1) * CH]
            else:
                dst = v[:, slot, (c - 4) * CH:(c - 3) * CH]
            act.activation(dst, ps_q[:, :], ACT.Copy, scale=DH ** -0.5 if c < 2 else 1.0).then_inc(proj_copied, 1)

        def exponentials(act, it, i, slot):
            act.wait_ge(max_ready, TB * it + i + 1)
            n = (i + 1) * P
            act.activation(probs[:, i % 2, 0:n], ps_s[:, i % 2, 0:n], ACT.Exp, bias=neg_max[:, i % 2:i % 2 + 1],
                           accum_out=row_sum[:, slot, i:i + 1]).then_inc(probs_ready, 1)

        @block.scalar
        def _(act):
            act.sem_inc(probs_ready, 2)
            for c in range(NQ):
                take_projection(act, 0, c, 0)
            exponentials(act, 0, 0, 0)
            exponentials(act, 0, 1, 0)

            def head(it, b, h, slot):
                for what, i in order:
                    if what == "Q":
                        take_projection(act, it + 1, i, 1 - slot)
                    elif what == "S":
                        act.wait_ge(pT_copied, upto[-1] * it + upto[i - 2] + 2)
                        exponentials(act, it + i // TB, i % TB, slot if i < TB else 1 - slot)
                    elif what == "PV":
                        act.wait_ge(pv_ready, NG * it + i + 1)
                        act.activation(oT[:, i, :], ps_o[:, :], ACT.Copy).then_inc(oT_copied, 1)

            heads(act, head)

        def maxima(dve, it, i):
            dve.wait_ge(scores_ready, TB * it + i + 1)
            dve.tensor_reduce(neg_max[:, i % 2:i % 2 + 1], ps_s[:, i % 2, 0:(i + 1) * P], AX.X, ALU.max, negate=True)\
               .then_inc(max_ready, 1)

        @block.vector
        def _(dve):
            dve.sem_inc(pT_copied, 2)
            maxima(dve, 0, 0)
            maxima(dve, 0, 1)

            def head(it, b, h, slot):
                for what, i in order:
                    if what == "S":
                        maxima(dve, it + i // TB, i % TB)
                    elif what == "T":
                        G = i // 4
                        for n, (lo, hi) in enumerate(parts[i]):
                            u = upto[i] - len(parts[i]) + n
                            dve.wait_ge(turned, upto[-1] * it + u + 1)
                            dve.wait_ge(pv_ready, NG * it)
                            dve.tensor_copy(pT[G][:, lo:hi, (i % 4) * P:(i % 4 + 1) * P],
                                            ps_t[:, u % 2, 0:(hi - lo) * P].rearrange("p (j c) -> p j c", c=P))\
                               .then_inc(pT_copied, 1)
                    elif what == "PR":
                        dve.wait_ge(probs_ready, TB * it + 4 * i + 4 + 2)
                        dve.reciprocal(inv_sum[:, i, :], row_sum[:, slot, 4 * i:4 * i + 4]).then_inc(inv_ready, 1)
                        dve.wait_ge(inv_ready, NG * it + i + 1)
                        dve.wait_ge(out_ready, NG * it + i + 1)
                        for j in range(4):
                            x = g.x[:, b * TB + (4 * i + j), :]
                            last = dve.scalar_tensor_tensor(out=x, in0=ps_o[:, j * D:(j + 1) * D],
                                                            scalar=inv_sum[:, i, j:j + 1], in1=x,
                                                            op0=ALU.mult, op1=ALU.add)
                        last.then_inc(added, 1)

            heads(dve, head)


def store_phase(nc, g, out):
    with Scope(nc, "store") as s:
        stored = s.sem("stored")
        block = s.block()

        @block.sync
        def _(sp):
            view = out.rearrange("b (n p) c -> p (b n) c", p=P)
            for q in range(4):
                n = NT // 4
                sp.dma_start(view[:, q * n:(q + 1) * n, :], g.x[:, q * n:(q + 1) * n, :]).then_inc(stored, 16)
            sp.wait_ge(stored, 64)


class Shared:
    pass


STAGES = 6
SKIP = 0


def program(nc, A, out):
    _ = 0
    with ExitStack() as stack:
        g = Shared()
        g.x = stack.enter_context(nc.sbuf_tensor("x", [P, NT, D], F32))
        g.xnT = stack.enter_context(nc.sbuf_tensor("xnT", [P, B, HALO + L], F32))
        g.ident = stack.enter_context(nc.sbuf_tensor("ident", [P, P], F32))
        g.w_ffn = stack.enter_context(nc.sbuf_tensor("w_ffn", [P, 3, D], F32))
        g.mu = stack.enter_context(nc.sbuf_tensor("mu", [P, 2], F32))
        g.w_in = stack.enter_context(nc.sbuf_tensor("w_in", [P, 2 * NB * P], F32))
        g.w_x = stack.enter_context(nc.sbuf_tensor("w_x", [P, NB, R + 3 * BC], F32))
        g.w_dt = stack.enter_context(nc.sbuf_tensor("w_dt", [R, NB * P], F32))
        g.w_out = stack.enter_context(nc.sbuf_tensor("w_out", [P, NB, D], F32))
        g.conv_w = stack.enter_context(nc.sbuf_tensor("conv_w", [P, NB, 2 * KW], F32))
        g.conv_b = stack.enter_context(nc.sbuf_tensor("conv_b", [P, NB, 2], F32))
        g.b_dt = stack.enter_context(nc.sbuf_tensor("b_dt", [P, NB], F32))
        g.d_param = stack.enter_context(nc.sbuf_tensor("d_param", [P, NB], F32))
        g.a_log = stack.enter_context(nc.sbuf_tensor("a_log", [P, NB, NS], F32))
        g.neg_a = stack.enter_context(nc.sbuf_tensor("neg_a", [P, NB, NS], F32))
        g.gates = stack.enter_context(nc.sbuf_tensor("gates", [P, 2], F32))
        g.weights = [(g.w_ffn[:, :, :], "w_ffn"), (g.mu[:, :], "mu"), (g.w_in[:, :], "w_in"), (g.w_x[:, :, :], "w_x"),
                     (g.w_dt[:, :], "w_dt"), (g.w_out[:, :, :], "w_out"), (g.conv_w[:, :, :], "conv_w"),
                     (g.conv_b[:, :, :], "conv_b"), (g.b_dt[:, :], "b_dt"), (g.d_param[:, :], "d_param"),
                     (g.a_log[:, :, :], "a_log"), (g.gates[:, :], "gates")]
        g.loaded = stack.enter_context(nc.semaphore("loaded"))
        g.LOADED = 16 * len(g.weights)
        g.token_rows = nc.dram_tensor("token_rows", (B * L, D), F32, kind="Internal").ap()
        g.expert_rows = nc.dram_tensor("expert_rows", (2 * B * L, D), F32, kind="Internal").ap()
        load_phase(nc, g, A)
        if STAGES >= 1:
            layernorm_phase(nc, g, "ln0")
            ffn_phase(nc, g, "ffn0")
        if STAGES >= 2 and not SKIP:
            layernorm_phase(nc, g, "ln1")
            mamba_phase(nc, g, A)
        if STAGES >= 3:
            layernorm_phase(nc, g, "ln2")
            g.w1 = stack.enter_context(nc.sbuf_tensor("w1", [P, E * F], F32))
            g.w2 = stack.enter_context(nc.sbuf_tensor("w2", [P, E * F], F32))
            g.b1 = stack.enter_context(nc.sbuf_tensor("b1", [P, E * F], F32))
            g.b2 = stack.enter_context(nc.sbuf_tensor("b2", [P, E * D], F32))
            g.router = stack.enter_context(nc.sbuf_tensor("router", [P, E], F32))
            g.source = stack.enter_context(nc.sbuf_tensor("source", [P, MT], U32))
            g.target = stack.enter_context(nc.sbuf_tensor("target", [P, MT], U32))
            g.weight = stack.enter_context(nc.sbuf_tensor("weight", [P, 2, NT], F32))
            g.owner = stack.enter_context(nc.sbuf_tensor("owner", [1, MT], I32))
            g.w_qkv = stack.enter_context(nc.sbuf_tensor("w_qkv", [P, H * 3 * DH], F32))
            g.w_o = stack.enter_context(nc.sbuf_tensor("w_o", [P, H * D], F32))
            g.gamma = stack.enter_context(nc.sbuf_tensor("gamma", [P, 1], F32))
            g.late_loaded = stack.enter_context(nc.semaphore("late_loaded"))
            g.late_weights = [(g.w1[:, :], "w1"), (g.w2[:, :], "w2"), (g.b1[:, :], "b1"), (g.b2[:, :], "b2"),
                              (g.router[:, :], "router"), (g.w_qkv[:, :], "w_qkv"), (g.w_o[:, :], "w_o"),
                              (g.gamma[:, :], "gamma")]
            g.LATE_LOADED = 16 * len(g.late_weights)
            load_experts_phase(nc, g, A)
            ffn_phase(nc, g, "ffn1")
        if STAGES >= 4:
            layernorm_phase(nc, g, "ln3", keep_tokens=True)
            moe_route_phase(nc, g, "route0")
            moe_expert_phase(nc, g, "experts0")
            moe_combine_phase(nc, g, "combine0")
        if STAGES >= 5:
            layernorm_phase(nc, g, "ln4", rms_gamma=g.gamma[:, 0:1])
            attention_phase(nc, g, A)
        if STAGES >= 6:
            layernorm_phase(nc, g, "ln5", keep_tokens=True)
            moe_route_phase(nc, g, "route1")
            moe_expert_phase(nc, g, "experts1")
            moe_combine_phase(nc, g, "combine1")
        store_phase(nc, g, out)




def laid_out(i):
    def t(a):
        return np.ascontiguousarray(np.asarray(a).T)
    def blocks(a):
        a = np.asarray(a)
        return np.ascontiguousarray(a.reshape(NB, P, -1).transpose(1, 0, 2))

    w_x = np.asarray(i["L0_attn_W_x"]).T
    return {
        "hidden": np.ascontiguousarray(np.asarray(i["L0_attn_hidden_states"]).reshape(B * L, D)),
        "w_ffn": np.stack([t(i["L0_ffn_W_r"]), t(i["L0_ffn_W_k"]), t(i["L0_ffn_W_v"])], axis=1),
        "mu": np.stack([np.asarray(i["L0_ffn_mu_r"]), np.asarray(i["L0_ffn_mu_k"])], axis=1),
        "w_in": t(i["L0_attn_W_in"]),
        "w_x": blocks(np.concatenate([w_x[:, :R]] + 3 * [w_x[:, R:]], axis=1)),
        "w_dt": t(i["L0_attn_W_dt"]),
        "w_out": blocks(t(i["L0_attn_W_out"])),
        "conv_w": blocks(np.concatenate([i["L0_attn_conv_w1"], i["L0_attn_conv_w2"]], axis=1)),
        "conv_b": blocks(np.stack([i["L0_attn_conv_b1"], i["L0_attn_conv_b2"]], axis=1)),
        "b_dt": blocks(i["L0_attn_b_dt"])[:, :, 0],
        "d_param": blocks(i["L0_attn_D_param"])[:, :, 0],
        "a_log": blocks(i["L0_attn_A_log"]),
        "w1": np.asarray(i["L1_ffn_w1"]).transpose(2, 0, 1).reshape(P, E * F),
        "w2": np.asarray(i["L1_ffn_w2"]).reshape(E, D, FC, P).transpose(3, 0, 2, 1).reshape(P, E * F),
        "b1": np.broadcast_to(np.asarray(i["L1_ffn_b1"]).reshape(1, E * F), (P, E * F)),
        "b2": np.broadcast_to(np.asarray(i["L1_ffn_b2"]).reshape(1, E * D), (P, E * D)),
        "w_qkv": np.asarray(i["L1_attn_w_qkv"]).reshape(3, H, DH, D).transpose(3, 1, 0, 2).reshape(D, 3 * H * DH),
        "w_o": np.asarray(i["L1_attn_w_out"]).reshape(D, H, DH).transpose(2, 1, 0).reshape(DH, H * D),
        "gamma": np.asarray(i["L1_attn_gamma"])[:, None],
        "router": t(i["L1_ffn_router_w"]),
        "gates": np.broadcast_to(np.asarray(i["L0_attn_conv_gates"])[None], (P, 2)),
    }


def kernel(**inputs):
    import concourse.bacc as bacc
    from concourse.bass_utils import run_bass_kernel_spmd

    nc = bacc.Bacc("TRN2", target_bir_lowering=False, num_devices=1)
    arrays, aps = {}, {}
    for name, a in laid_out(inputs).items():
        a = np.ascontiguousarray(a)
        arrays[f"in_{name}"] = a
        aps[name] = nc.dram_tensor(f"in_{name}", a.shape, mybir.dt.from_np(a.dtype), kind="ExternalInput").ap()
    out = nc.dram_tensor("out_x", (B, L, D), F32, kind="ExternalOutput").ap()
    program(nc, aps, out)
    r = run_bass_kernel_spmd(nc, [arrays], core_ids=[0])
    return r.results[0]["out_x"]
```

```python
from contextlib import ExitStack

import numpy as np

import concourse.bass as bass
from concourse import mybir

F32 = mybir.dt.float32
F32R = mybir.dt.float32r
BF16 = mybir.dt.bfloat16
I32 = mybir.dt.int32
U32 = mybir.dt.uint32
ALU = mybir.AluOpType
ACT = mybir.ActivationFunctionType
AX = mybir.AxisListType

P = 128
B, L, D = 4, 1024, 128
NT = B * L // P
TB = L // P
CH = 512
HALVES = L // CH
HALO = 6
LN_EPS = 1e-5

NB = 2
NS = 16
R = 64
BC = 2 * NS
KW = 4

H, DH = 8, 128

E, F = 8, 512
FC = F // P
MT = 72
XSLOTS = 8
YSLOTS = 4
assert MT % XSLOTS == 0 and MT >= 2 * NT + E - 1


class Scope:

    def __init__(self, nc, tag):
        self.nc, self.tag, self.stack, self.sems = nc, tag, ExitStack(), []

    def __enter__(self):
        return self

    def __exit__(self, *e):
        self.stack.__exit__(*e)
        if e[0] is None and self.sems:
            self.nc.clear_and_free_semaphores(self.sems)
            self.nc.all_engine_barrier()

    def sb(self, name, shape, dt=F32):
        return self.stack.enter_context(self.nc.sbuf_tensor(f"{self.tag}_{name}", shape, dt))

    def ps(self, name, shape, dt=F32):
        return self.stack.enter_context(self.nc.psum_tensor(f"{self.tag}_{name}", shape, dt))

    def sem(self, name):
        handle = self.nc.alloc_semaphore(f"{self.tag}_{name}")
        self.sems.append(handle)
        return handle

    def block(self):
        return self.stack.enter_context(self.nc.Block())


def load_phase(nc, g, A):
    with Scope(nc, "load") as s:
        dma_in = s.sem("dma_in")
        halo_zero = s.sem("halo_zero")
        ident_zero = s.sem("ident_zero")
        ident_done = s.sem("ident_done")
        block = s.block()

        @block.sync
        def _(sp):
            hid = A["hidden"].rearrange("(n p) c -> p n c", p=P)
            for q in range(4):
                n = NT // 4
                sp.dma_start(g.x[:, q * n:(q + 1) * n, :], hid[:, q * n:(q + 1) * n, :]).then_inc(dma_in, 16)
            sp.wait_ge(dma_in, 64)

        @block.scalar
        def _(act):
            for dst, name in g.weights:
                act.dma_start(dst, A[name]).then_inc(g.loaded, 16)

        @block.gpsimd
        def _(pool):
            pool.memset(g.ident[:, :], 0.0).then_inc(ident_zero, 1)
            pool.wait_ge(ident_zero, 1)
            pool.affine_select(out=g.ident[:, :], in_=g.ident[:, :], compare_op=ALU.not_equal, fill=1.0,
                               base=0, pattern=[[-1, P]], channel_multiplier=1).then_inc(ident_done, 1)

        @block.vector
        def _(dve):
            dve.memset(g.xnT[:, :, 0:HALO], 0.0).then_inc(halo_zero, 1)


def layernorm_phase(nc, g, tag, keep_tokens=False, rms_gamma=None):
    with Scope(nc, tag) as s:
        stats = s.sb("stats", [P, NT, 6])
        work = s.sb("work", [P, 9, NT])
        stage = s.sb("stage", [P, HALVES, 4, P])
        psT = s.ps("psT", [P, HALVES, CH])
        stats_done = s.sem("stats_done")
        chain = s.sem("chain")
        var_ready = s.sem("var_ready")
        std_ready = s.sem("std_ready")
        staged = s.sem("staged")
        rows_kept = [s.sem(f"rows_kept{h}") for h in range(HALVES)]
        transposed = s.sem("transposed")
        waited = s.sem("waited")
        psT_free = s.sem("psT_free")
        diff, total, m2, var, std, rstd, mean, shift, lengths = (work[:, k, :] for k in range(9))
        if rms_gamma is not None:
            square = s.sb("square", [P, TB, D])
            shift_ready = s.sem("shift_ready")
            lengths_ready = s.sem("lengths_ready")
            roots_ready = s.sem("roots_ready")
        block = s.block()

        @block.vector
        def _(dve):
            with dve.Fori(0, B) as b:
                for t in range(TB):
                    last = dve.bn_stats(out=stats[:, b * TB + t, :], in_=g.x[:, b * TB + t, :])
                last.then_inc(stats_done, 1)
            dve.wait_ge(stats_done, B)
            dve.tensor_tensor(diff, stats[:, :, 1], stats[:, :, 4], ALU.subtract).then_inc(chain, 1)
            dve.tensor_tensor(total, stats[:, :, 1], stats[:, :, 4], ALU.add).then_inc(chain, 1)
            dve.tensor_tensor(m2, stats[:, :, 2], stats[:, :, 5], ALU.add).then_inc(chain, 1)
            dve.wait_ge(chain, 3)
            dve.tensor_tensor(diff, diff, diff, ALU.mult).then_inc(chain, 1)
            dve.tensor_scalar(mean, total, 0.5, None, ALU.mult).then_inc(chain, 1)
            dve.tensor_scalar(m2, m2, 1.0 / D, LN_EPS, ALU.mult, ALU.add).then_inc(chain, 1)
            dve.wait_ge(chain, 6)
            dve.scalar_tensor_tensor(out=var, in0=diff, scalar=0.25, in1=m2, op0=ALU.mult, op1=ALU.add)\
               .then_inc(var_ready, 1)
            dve.wait_ge(std_ready, 1)
            dve.reciprocal(rstd, std).then_inc(chain, 1)
            dve.wait_ge(chain, 7)
            if rms_gamma is not None:
                dve.scalar_tensor_tensor(out=shift, in0=mean, scalar=-1.0, in1=rstd, op0=ALU.mult, op1=ALU.mult)\
                   .then_inc(shift_ready, 1)
                dve.wait_ge(roots_ready, 1)
                dve.tensor_scalar(lengths, lengths, 1e-12, float(D) ** -0.5, ALU.max, ALU.mult).then_inc(chain, 1)
                dve.wait_ge(chain, 8)
                dve.reciprocal(total, lengths).then_inc(chain, 1)
                dve.wait_ge(chain, 9)
                dve.tensor_tensor(rstd, rstd, total, ALU.mult).then_inc(chain, 1)
                dve.wait_ge(chain, 10)
            with dve.Fori(0, B) as b:
                for h in range(HALVES):
                    dve.wait_ge(psT_free, HALVES * b + h + 1)
                    if keep_tokens:
                        dve.wait_ge(rows_kept[h], 16 * b + 16)
                    for j in range(4):
                        t = b * TB + (h * 4 + j)
                        last = dve.tensor_scalar(stage[:, h, j, :], g.x[:, t, :], mean[:, bass.ds(t, 1)],
                                                 rstd[:, bass.ds(t, 1)], ALU.subtract, ALU.mult)
                    last.then_inc(staged, 1)

        @block.tensor
        def _(pe):
            with pe.Fori(0, B) as b:
                for h in range(HALVES):
                    pe.wait_ge(staged, HALVES * b + h + 1)
                    for j in range(4):
                        last = pe.transpose(psT[:, h, j * P:(j + 1) * P], stage[:, h, j, :], g.ident[:, :])
                    last.then_inc(transposed, 1)

        @block.scalar
        def _(act):
            act.sem_inc(psT_free, HALVES)
            act.wait_ge(var_ready, 1)
            act.activation(std, var, ACT.Sqrt).then_inc(std_ready, 1)
            if rms_gamma is not None:
                act.wait_ge(shift_ready, 1)
                with act.Fori(0, B) as b:
                    act.wait_ge(lengths_ready, b)
                    act.sem_inc(waited, 1)
                    for j in range(TB):
                        t = bass.ds(b * TB + j, 1)
                        last = act.activation(square[:, j, :], g.x[:, b * TB + j, :], ACT.Square,
                                              bias=shift[:, t], scale=rstd[:, t], accum_out=lengths[:, t])
                    last.then_inc(lengths_ready, 1)
                act.wait_ge(lengths_ready, B)
                act.activation(lengths, lengths, ACT.Sqrt).then_inc(roots_ready, 1)
            with act.Fori(0, B) as b:
                for h in range(HALVES):
                    act.wait_ge(transposed, HALVES * b + h + 1)
                    act.sem_inc(waited, 1)
                    out = g.xnT[:, b, HALO + h * CH:HALO + (h + 1) * CH]
                    if rms_gamma is None:
                        act.activation(out, psT[:, h, :], ACT.Copy).then_inc(psT_free, 1)
                    else:
                        act.activation(out, psT[:, h, :], ACT.Identity, scale=rms_gamma).then_inc(psT_free, 1)

        if keep_tokens:
            @block.sync
            def _(sp):
                for h in range(HALVES):
                    sp.sem_inc(rows_kept[h], 16)
                with sp.Fori(0, B) as b:
                    for h in range(HALVES):
                        sp.wait_ge(staged, HALVES * b + h + 1)
                        sp.dma_start(g.token_rows[bass.ds(b * L + h * CH, CH), :].rearrange("(j p) c -> p j c", p=P),
                                     stage[:, h, :, :]).then_inc(rows_kept[h], 16)
                for h in range(HALVES):
                    sp.wait_ge(rows_kept[h], 16 * (B + 1))


def ffn_phase(nc, g, tag):
    with Scope(nc, tag) as s:
        w, mu = g.w_ffn, g.mu
        one_minus = s.sb("one_minus", [P, 2])
        part = s.sb("part", [P, 2, CH])
        mixed = s.sb("mixed", [P, HALVES, 2, CH])
        relu = s.sb("relu", [P, HALVES, CH])
        gate = s.sb("gate", [P, HALVES, CH])
        prod = s.sb("prod", [P, HALVES, CH])
        ps_r = s.ps("ps_r", [P, HALVES, CH])
        ps_k = s.ps("ps_k", [P, HALVES, CH])
        ps_v = s.ps("ps_v", [P, HALVES, CH])
        ps_t = s.ps("ps_t", [P, HALVES, CH])
        consts = s.sem("consts")
        waited = s.sem("waited")
        part_ready = s.sem("part_ready")
        mix_ready = s.sem("mix_ready")
        r_ready = s.sem("r_ready")
        k_ready = s.sem("k_ready")
        gate_ready = s.sem("gate_ready")
        relu_ready = s.sem("relu_ready")
        square_ready = s.sem("square_ready")
        v_ready = s.sem("v_ready")
        prod_ready = s.sem("prod_ready")
        back = s.sem("back")
        added = s.sem("added")
        block = s.block()

        @block.scalar
        def _(act):
            act.wait_ge(g.loaded, g.LOADED)
            with act.Fori(0, B) as b:
                for h in range(HALVES):
                    for k in range(2):
                        act.wait_ge(mix_ready, 4 * b + 2 * h + k + 1)
                        act.sem_inc(waited, 1)
                        act.activation(part[:, k, :], g.xnT[:, b, HALO + h * CH:HALO + (h + 1) * CH], ACT.Identity,
                                       scale=mu[:, k:k + 1]).then_inc(part_ready, 1)
                for h in range(HALVES):
                    act.wait_ge(r_ready, HALVES * b + h + 1)
                    act.activation(gate[:, h, :], ps_r[:, h, :], ACT.Sigmoid).then_inc(gate_ready, 1)
                    act.wait_ge(k_ready, HALVES * b + h + 1)
                    act.activation(relu[:, h, :], ps_k[:, h, :], ACT.Relu).then_inc(relu_ready, 1)
                    act.wait_ge(relu_ready, HALVES * b + h + 1)
                    act.activation(relu[:, h, :], relu[:, h, :], ACT.Square).then_inc(square_ready, 1)

        @block.tensor
        def _(pe):
            pe.wait_ge(g.loaded, g.LOADED)
            with pe.Fori(0, B) as b:
                for h in range(HALVES):
                    pe.wait_ge(added, HALVES * b)
                    pe.wait_ge(mix_ready, 4 * b + 2 * h + 1 + 2)
                    pe.matmul(ps_r[:, h, :], w[:, 0, :], mixed[:, h, 0, :], start=True, stop=True).then_inc(r_ready, 1)
                    pe.wait_ge(mix_ready, 4 * b + 2 * h + 2 + 2)
                    pe.matmul(ps_k[:, h, :], w[:, 1, :], mixed[:, h, 1, :], start=True, stop=True).then_inc(k_ready, 1)
                for h in range(HALVES):
                    pe.wait_ge(square_ready, HALVES * b + h + 1)
                    pe.matmul(ps_v[:, h, :], w[:, 2, :], relu[:, h, :], start=True, stop=True).then_inc(v_ready, 1)
                for h in range(HALVES):
                    pe.wait_ge(prod_ready, HALVES * b + h + 1)
                    for j in range(4):
                        last = pe.transpose(ps_t[:, h, j * P:(j + 1) * P], prod[:, h, j * P:(j + 1) * P], g.ident[:, :])
                    last.then_inc(back, 1)

        @block.vector
        def _(dve):
            dve.wait_ge(g.loaded, g.LOADED)
            dve.tensor_scalar(one_minus[:, :], mu[:, :], -1.0, 1.0, ALU.mult, ALU.add).then_inc(consts, 1)
            dve.wait_ge(consts, 1)
            dve.sem_inc(mix_ready, 2)
            with dve.Fori(0, B) as b:
                for h in range(HALVES):
                    for k in range(2):
                        dve.wait_ge(part_ready, 4 * b + 2 * h + k + 1)
                        lo = HALO - 1 + h * CH
                        dve.scalar_tensor_tensor(out=mixed[:, h, k, :], in0=g.xnT[:, b, lo:lo + CH],
                                                 scalar=one_minus[:, k:k + 1], in1=part[:, k, :],
                                                 op0=ALU.mult, op1=ALU.add).then_inc(mix_ready, 1)
                for h in range(HALVES):
                    dve.wait_ge(gate_ready, HALVES * b + h + 1)
                    dve.wait_ge(v_ready, HALVES * b + h + 1)
                    dve.tensor_tensor(prod[:, h, :], gate[:, h, :], ps_v[:, h, :], ALU.mult).then_inc(prod_ready, 1)
                for h in range(HALVES):
                    dve.wait_ge(back, HALVES * b + h + 1)
                    x = g.x[:, bass.ds(b * TB + h * 4, 4), :]
                    dve.scalar_tensor_tensor(out=x, in0=ps_t[:, h, :].rearrange("p (j c) -> p j c", j=4), scalar=0.5,
                                             in1=x, op0=ALU.mult, op1=ALU.add).then_inc(added, 1)


def mamba_phase(nc, g, A):
    with Scope(nc, "mamba") as s:
        xin = s.sb("xin", [P, NB, HALO + L])
        silu1 = s.sb("silu1", [P, NB, CH])
        silu2 = s.sb("silu2", [P, NB, CH])
        xc = s.sb("xc", [P, NB, L])
        zs = s.sb("zs", [P, NB, L])
        low = s.sb("low", [R, CH])
        bc_hi = s.sb("bc_hi", [3 * BC, CH], BF16)
        bc_rest = s.sb("bc_rest", [3 * BC, CH])
        bc_mid = s.sb("bc_mid", [3 * BC, CH], BF16)
        bc = s.sb("bc", [3 * BC, L], BF16)
        v = s.sb("v", [P, NB, CH])
        mag = s.sb("mag", [P, NB, CH])
        pos = s.sb("pos", [P, NB, CH])
        ex = s.sb("ex", [P, NB, CH])
        ln = s.sb("ln", [P, NB, CH])
        low_bits = s.sb("low_bits", [P, NB, CH])
        delta = s.sb("delta", [P, NB, L])
        u = s.sb("u", [P, NB, L])
        decay = s.sb("decay", [P, NB, L])
        drive = s.sb("drive", [P, NB, L])
        state = s.sb("state", [P, NB, L])
        c_all = s.sb("c_all", [P, 2, L])
        read = s.sb("read", [P, NB, L])
        y = s.sb("y", [P, NB, L])
        taps = s.sb("taps", [P, NB, 2 * KW, P])
        pick = s.sb("pick", [3 * BC, BC, P], BF16)
        gates = s.sb("gates", [P, 2])
        gsum = s.sb("gsum", [P, 1])
        neg_a = s.sb("neg_a", [P, NB, NS])
        bank = s.ps("bank", [P, 8, CH])

        gate_exp = s.sem("gate_exp")
        consts = s.sem("consts")
        consts_done = s.sem("consts_done")
        pick_steps = s.sem("pick_steps")
        x_ready = s.sem("x_ready")
        x_copied = s.sem("x_copied")
        conv_ready = s.sem("conv_ready")
        silu_ready = s.sem("silu_ready")
        z_ready = s.sem("z_ready")
        zs_ready = s.sem("zs_ready")
        xc_part = s.sem("xc_part")
        xc_ready = s.sem("xc_ready")
        low_ready = s.sem("low_ready")
        low_copied = s.sem("low_copied")
        bc_split = s.sem("bc_split")
        bc_rest_ready = s.sem("bc_rest_ready")
        bc_ready = s.sem("bc_ready")
        dt_ready = s.sem("dt_ready")
        v_ready = s.sem("v_ready")
        mag_ready = s.sem("mag_ready")
        pos_ready = s.sem("pos_ready")
        ex_ready = s.sem("ex_ready")
        ln_ready = s.sem("ln_ready")
        delta_steps = s.sem("delta_steps")
        delta_ready = s.sem("delta_ready")
        u_ready = s.sem("u_ready")
        b_spread = s.sem("b_spread")
        c_spread = s.sem("c_spread")
        c_copied = s.sem("c_copied")
        decay_ready = s.sem("decay_ready")
        driven = s.sem("driven")
        scanned = s.sem("scanned")
        read_ready = s.sem("read_ready")
        summed = s.sem("summed")
        y_part = s.sem("y_part")
        y_ready = s.sem("y_ready")
        projected = s.sem("projected")
        added = s.sem("added")
        block = s.block()

        def xn(b, h):
            return g.xnT[:, b, HALO + h * CH:HALO + (h + 1) * CH]

        def cols(h):
            return slice(h * CH, (h + 1) * CH)

        @block.gpsimd
        def _(pool):
            pool.memset(xin[:, :, 0:HALO], 0.0).then_inc(pick_steps, 1)
            pool.memset(pick[:, :, :], 0.0).then_inc(pick_steps, 1)
            for part in range(3):
                pool.wait_ge(pick_steps, 2 + part)
                pool.affine_select(out=pick[:, :, :], in_=pick[:, :, :], compare_op=ALU.not_equal, fill=1.0,
                                   base=-BC * part, pattern=[[-1, BC], [0, P]], channel_multiplier=1)\
                    .then_inc(pick_steps, 1)
            pool.sem_inc(read_ready, 4)
            with pool.Fori(0, B) as b:
                for h in range(HALVES):
                    pool.wait_ge(xc_ready, HALVES * b + h + 1)
                    pool.wait_ge(delta_ready, HALVES * b + h + 1)
                    pool.tensor_tensor(u[:, :, cols(h)], delta[:, :, cols(h)], xc[:, :, cols(h)], ALU.mult)\
                        .then_inc(u_ready, 1)
                for n in range(NS):
                    for blk in range(NB):
                        j = NB * n + blk
                        pool.wait_ge(c_copied, NS * b + n + 1)
                        pool.wait_ge(scanned, NB * NS * b + j + 1 + NB)
                        pool.wait_ge(summed, NB * NS * b + j + 1)
                        pool.tensor_tensor(read[:, blk, :], state[:, blk, :], c_all[:, n % 2, :], ALU.mult)\
                            .then_inc(read_ready, 1)

        @block.scalar
        def _(act):
            act.wait_ge(g.loaded, g.LOADED)
            act.activation(gates[:, :], g.gates[:, :], ACT.Exp, accum_out=gsum[:, :]).then_inc(gate_exp, 1)
            act.activation(neg_a[:, :, :], g.a_log[:, :, :], ACT.Exp).then_inc(gate_exp, 1)
            with act.Fori(0, B) as b:
                for h in range(HALVES):
                    for blk in range(NB):
                        act.wait_ge(x_ready, 2 * NB * b + NB * h + blk + 1)
                        act.activation(xin[:, blk, HALO + h * CH:HALO + (h + 1) * CH], bank[:, blk, :], ACT.Copy)\
                            .then_inc(x_copied, 1)
                    for blk in range(NB):
                        for k in range(2):
                            act.wait_ge(conv_ready, 8 * b + 4 * h + 2 * blk + k + 1)
                            act.wait_ge(xc_ready, HALVES * b + h)
                            act.activation((silu1, silu2)[k][:, blk, :], bank[:, 2 + 2 * blk + k, :], ACT.Silu,
                                           bias=g.conv_b[:, blk, k:k + 1]).then_inc(silu_ready, 1)
                    for blk in range(NB):
                        act.wait_ge(z_ready, 4 * b + NB * h + blk + 1)
                        act.wait_ge(y_ready, NB * b)
                        act.activation(zs[:, blk, cols(h)], bank[:, 6 + blk, :], ACT.Silu).then_inc(zs_ready, 1)
                    act.wait_ge(low_ready, HALVES * b + h + 1)
                    act.activation(low[:, :], bank[0:R, 0, :], ACT.Copy).then_inc(low_copied, 1)
                    act.activation(bc_hi[:, :], bank[0:3 * BC, 1, :], ACT.Copy).then_inc(bc_split, 1)
                    act.activation(bc[0:BC, cols(h)], bank[0:BC, 1, :], ACT.Copy).then_inc(bc_split, 1)
                    act.wait_ge(bc_rest_ready, HALVES * b + h + 1)
                    act.activation(bc_mid[2 * BC:3 * BC, :], bc_rest[2 * BC:3 * BC, :], ACT.Copy).then_inc(bc_split, 1)
                    act.activation(bc[BC:2 * BC, cols(h)], bc_rest[BC:2 * BC, :], ACT.Copy).then_inc(bc_split, 1)
                    for blk in range(NB):
                        act.wait_ge(dt_ready, 4 * b + NB * h + blk + 1)
                        act.activation(v[:, blk, :], bank[:, 2 + blk, :], ACT.Identity, bias=g.b_dt[:, blk:blk + 1])\
                            .then_inc(v_ready, 1)
                    act.wait_ge(v_ready, 4 * b + NB * h + NB)
                    act.activation(mag[:, :, :], v[:, :, :], ACT.Abs).then_inc(mag_ready, 1)
                    act.wait_ge(mag_ready, HALVES * b + h + 1)
                    act.wait_ge(delta_ready, HALVES * b + h)
                    act.activation(ex[:, :, :], mag[:, :, :], ACT.Exp, scale=-1.0).then_inc(ex_ready, 1)
                    act.wait_ge(ex_ready, HALVES * b + h + 1)
                    act.activation(ln[:, :, :], ex[:, :, :], ACT.Ln, bias=1.0).then_inc(ln_ready, 1)
                act.wait_ge(delta_ready, HALVES * b + HALVES)
                for n in range(NS):
                    for blk in range(NB):
                        j = NB * n + blk
                        act.wait_ge(scanned, NB * NS * b + j + 1)
                        act.activation(decay[:, blk, :], delta[:, blk, :], ACT.Exp, scale=g.neg_a[:, blk, n:n + 1])\
                            .then_inc(decay_ready, 1)
                    act.wait_ge(c_spread, NS * b + n + 1)
                    act.wait_ge(read_ready, NB * NS * b + NB * n + 2)
                    act.activation(c_all[:, n % 2, :], bank[:, 2:4, :].rearrange("p k t -> p (k t)"), ACT.Copy)\
                        .then_inc(c_copied, 1)

        @block.vector
        def _(dve):
            dve.wait_ge(gate_exp, 2)
            dve.reciprocal(gsum[:, :], gsum[:, :]).then_inc(consts, 1)
            dve.tensor_scalar(g.neg_a[:, :, :], neg_a[:, :, :], -1.0, None, ALU.mult).then_inc(consts_done, 1)
            for blk in range(NB):
                for k in range(2 * KW):
                    dve.tensor_scalar(taps[:, blk, k, :], g.ident[:, :], g.conv_w[:, blk, k:k + 1], None, ALU.mult)\
                        .then_inc(consts_done, 1)
            dve.wait_ge(consts, 1)
            dve.tensor_scalar(gates[:, :], gates[:, :], gsum[:, :], None, ALU.mult).then_inc(consts, 1)
            dve.wait_ge(consts, 2)
            dve.sem_inc(scanned, NB)
            with dve.Fori(0, B) as b:
                for h in range(HALVES):
                    dve.wait_ge(silu_ready, 8 * b + 4 * h + 4)
                    dve.wait_ge(u_ready, HALVES * b)
                    dve.tensor_scalar(xc[:, :, cols(h)], silu1[:, :, :], gates[:, 0:1], None, ALU.mult)\
                        .then_inc(xc_part, 1)
                    dve.wait_ge(xc_part, HALVES * b + h + 1)
                    dve.scalar_tensor_tensor(out=xc[:, :, cols(h)], in0=silu2[:, :, :], scalar=gates[:, 1:2],
                                             in1=xc[:, :, cols(h)], op0=ALU.mult, op1=ALU.add).then_inc(xc_ready, 1)
                    dve.wait_ge(bc_split, 8 * b + 4 * h + 1)
                    dve.tensor_tensor(bc_rest[BC:2 * BC, :], bank[BC:2 * BC, 1, :], bc_hi[BC:2 * BC, :], ALU.subtract)
                    dve.tensor_tensor(bc_rest[2 * BC:3 * BC, :], bank[2 * BC:3 * BC, 1, :], bc_hi[2 * BC:3 * BC, :],
                                      ALU.subtract).then_inc(bc_rest_ready, 1)
                    dve.wait_ge(bc_split, 8 * b + 4 * h + 4)
                    dve.tensor_tensor(bc[2 * BC:3 * BC, cols(h)], bc_rest[2 * BC:3 * BC, :], bc_mid[2 * BC:3 * BC, :],
                                      ALU.subtract).then_inc(bc_ready, 1)
                    dve.wait_ge(v_ready, 4 * b + NB * h + NB)
                    dve.tensor_scalar(pos[:, :, :], v[:, :, :], 0.0, None, ALU.max).then_inc(pos_ready, 1)
                    c = 3 * (HALVES * b + h)
                    dve.wait_ge(ex_ready, HALVES * b + h + 1)
                    dve.tensor_scalar(low_bits[:, :, :], ex[:, :, :], 1.0, -1.0, ALU.add, ALU.add).then_inc(delta_steps, 1)
                    dve.wait_ge(delta_steps, c + 1)
                    dve.tensor_tensor(low_bits[:, :, :], ex[:, :, :], low_bits[:, :, :], ALU.subtract)\
                        .then_inc(delta_steps, 1)
                    dve.wait_ge(ln_ready, HALVES * b + h + 1)
                    dve.wait_ge(delta_steps, c + 2)
                    dve.tensor_tensor(low_bits[:, :, :], ln[:, :, :], low_bits[:, :, :], ALU.add).then_inc(delta_steps, 1)
                    dve.wait_ge(delta_steps, c + 3)
                    dve.wait_ge(pos_ready, HALVES * b + h + 1)
                    dve.tensor_tensor(delta[:, :, cols(h)], pos[:, :, :], low_bits[:, :, :], ALU.add)\
                        .then_inc(delta_ready, 1)
                dve.wait_ge(u_ready, HALVES * b + HALVES)
                for n in range(NS):
                    for blk in range(NB):
                        dve.wait_ge(b_spread, NS * b + n + 1)
                        dve.wait_ge(scanned, NB * NS * b + NB * n + blk + 1)
                        dve.tensor_tensor(drive[:, blk, :], u[:, blk, :],
                                          bank[:, 0:2, :].rearrange("p k t -> p (k t)"), ALU.mult).then_inc(driven, 1)
                    for blk in range(NB):
                        j = NB * n + blk
                        dve.wait_ge(decay_ready, NB * NS * b + j + 1)
                        dve.wait_ge(driven, NB * NS * b + j + 1)
                        dve.wait_ge(read_ready, NB * NS * b + j + 3)
                        dve.tensor_tensor_scan(state[:, blk, :], decay[:, blk, :], drive[:, blk, :], 0.0,
                                               ALU.mult, ALU.add).then_inc(scanned, 1)
                for blk in range(NB):
                    dve.wait_ge(summed, NB * NS * b + NB * NS + NB)
                    dve.wait_ge(projected, b)
                    dve.scalar_tensor_tensor(out=y[:, blk, :], in0=xc[:, blk, :], scalar=g.d_param[:, blk:blk + 1],
                                             in1=bank[:, 4 + 2 * blk:6 + 2 * blk, :].rearrange("p k t -> p (k t)"),
                                             op0=ALU.mult, op1=ALU.add).then_inc(y_part, 1)
                for blk in range(NB):
                    dve.wait_ge(y_part, NB * b + blk + 1)
                    dve.wait_ge(zs_ready, 4 * b + 4)
                    dve.tensor_tensor(y[:, blk, :], y[:, blk, :], zs[:, blk, :], ALU.mult).then_inc(y_ready, 1)
                dve.wait_ge(projected, b + 1)
                xb = g.x[:, bass.ds(b * TB, TB), :]
                dve.tensor_tensor(xb, xb, bank[:, 0:2, :].rearrange("p k (j c) -> p (k j) c", c=D), ALU.add)\
                    .then_inc(added, 1)

        @block.tensor
        def _(pe):
            pe.wait_ge(consts_done, 1 + NB * 2 * KW)
            pe.wait_ge(pick_steps, 5)
            pe.sem_inc(summed, NB)
            with pe.Fori(0, B) as b:
                for h in range(HALVES):
                    pe.wait_ge(added, b)
                    pe.wait_ge(bc_rest_ready, HALVES * b + h)
                    pe.wait_ge(bc_split, 8 * b + 4 * h)
                    for blk in range(NB):
                        pe.matmul(bank[:, blk, :], g.w_in[:, blk * P:(blk + 1) * P], xn(b, h), start=True, stop=True)\
                            .then_inc(x_ready, 1)
                    pe.wait_ge(zs_ready, 4 * b + NB * h)
                    for blk in range(NB):
                        pe.matmul(bank[:, 6 + blk, :], g.w_in[:, (NB + blk) * P:(NB + blk + 1) * P], xn(b, h),
                                  start=True, stop=True).then_inc(z_ready, 1)
                    pe.wait_ge(v_ready, 4 * b + NB * h)
                    pe.wait_ge(silu_ready, 8 * b + 4 * h)
                    pe.wait_ge(c_copied, NS * b)
                    for blk in range(NB):
                        pe.wait_ge(x_copied, 2 * NB * b + NB * h + blk + 1)
                        for k in range(2):
                            for tap in range(KW):
                                at = HALO + h * CH - (k + 1) * (KW - 1 - tap)
                                last = pe.matmul(bank[:, 2 + 2 * blk + k, :], taps[:, blk, k * KW + tap, :],
                                                 xin[:, blk, at:at + CH], start=(tap == 0), stop=(tap == KW - 1))
                            last.then_inc(conv_ready, 1)
                    pe.wait_ge(xc_ready, HALVES * b + h + 1)
                    for blk in range(NB):
                        pe.matmul(bank[0:R, 0, :], g.w_x[:, blk, 0:R], xc[:, blk, cols(h)],
                                  start=(blk == 0), stop=(blk == NB - 1))
                    for blk in range(NB):
                        last = pe.matmul(bank[0:3 * BC, 1, :], g.w_x[:, blk, R:R + 3 * BC], xc[:, blk, cols(h)],
                                         start=(blk == 0), stop=(blk == NB - 1))
                    last.then_inc(low_ready, 1)
                    pe.wait_ge(low_copied, HALVES * b + h + 1)
                    pe.wait_ge(silu_ready, 8 * b + 4 * h + 4)
                    for blk in range(NB):
                        pe.matmul(bank[:, 2 + blk, :], g.w_dt[:, blk * P:(blk + 1) * P], low[:, :],
                                  start=True, stop=True).then_inc(dt_ready, 1)
                pe.wait_ge(bc_ready, HALVES * b + HALVES)
                pe.wait_ge(zs_ready, 4 * b + 4)
                pe.wait_ge(v_ready, 4 * b + 4)

                def spread(n):
                    pe.wait_ge(driven, NB * NS * b + NB * n)
                    for h in range(HALVES):
                        last = pe.matmul(bank[:, h, :], pick[:, n, :], bc[:, cols(h)], start=True, stop=True)
                    last.then_inc(b_spread, 1)
                    pe.wait_ge(c_copied, NS * b + n)
                    for h in range(HALVES):
                        last = pe.matmul(bank[:, 2 + h, :], pick[:, NS + n, :], bc[:, cols(h)], start=True, stop=True)
                    last.then_inc(c_spread, 1)

                spread(0)
                for n in range(NS):
                    if n + 1 < NS:
                        spread(n + 1)
                    for blk in range(NB):
                        j = NB * n + blk
                        pe.wait_ge(read_ready, NB * NS * b + j + 5)
                        for h in range(HALVES):
                            last = pe.matmul(bank[:, 4 + 2 * blk + h, :], g.ident[:, :], read[:, blk, cols(h)],
                                             start=(n == 0), stop=(n == NS - 1))
                        last.then_inc(summed, 1)
                pe.wait_ge(y_ready, NB * b + NB)
                for t in range(TB):
                    for blk in range(NB):
                        last = pe.matmul(bank[:, t // 4, (t % 4) * P:(t % 4 + 1) * P], y[:, blk, t * P:(t + 1) * P],
                                         g.w_out[:, blk, :], start=(blk == 0), stop=(blk == NB - 1))
                last.then_inc(projected, 1)

        @block.sync
        def _(sp):
            sp.wait_ge(added, B)


def load_experts_phase(nc, g, A):
    with Scope(nc, "fetch") as s:
        block = s.block()

        @block.sync
        def _(sp):
            for dst, name in g.late_weights:
                sp.dma_start(dst, A[name]).then_inc(g.late_loaded, 16)


def moe_route_phase(nc, g, tag):
    with Scope(nc, tag) as s:
        def field(name):
            return s.sb(name, [P, NT, E])

        def column(name):
            return s.sb(name, [P, NT])

        prob, score, equal = field("prob"), field("score"), field("equal")
        first, second, both = field("first"), field("second"), field("both")
        total, until, place = field("total"), field("until"), field("place")
        top, denom, best, p1, p2 = (column(x) for x in ("top", "denom", "best", "p1", "p2"))
        both16 = s.sb("both16", [P, NT * E], BF16)
        rev = s.sb("rev", [P, E])
        ones_col = s.sb("ones_col", [P, NT])
        before = s.sb("before", [P, P], BF16)
        everyone = s.sb("everyone", [P, P], BF16)
        count_i = s.sb("count_i", [P, E], I32)
        tiles = s.sb("tiles", [P, E])
        tiles_until = s.sb("tiles_until", [P, E])
        base = s.sb("base", [P, E])
        row_f = s.sb("row_f", [P, 2, NT])
        row_i = s.sb("row_i", [P, 2 * NT], I32)
        part_i = s.sb("part_i", [P, 2, 2 * NT], I32)
        row_lo = s.sb("row_lo", [P, 2 * NT])
        row_hi = s.sb("row_hi", [P, 2 * NT])
        lane = s.sb("lane", [P, P])
        tile_of = s.sb("tile_of", [P, MT])
        choice = s.sb("choice", [P, 2 * NT])
        in_lane = s.sb("in_lane", [P, 2 * NT, P])
        in_tile = s.sb("in_tile", [P, 2 * NT, MT])
        found = s.sb("found", [P, MT])
        none = s.sb("none", [P, MT])
        source_f = s.sb("source_f", [P, MT])
        source_i = s.sb("source_i", [P, MT], I32)
        ps_list = s.ps("ps_list", [P, CH])
        lists_ready = s.sem("lists_ready")
        list_found = s.sem("list_found")
        tile_no = s.sb("tile_no", [1, MT, E])
        owner = s.sb("owner", [1, MT])
        ps_logit = s.ps("ps_logit", [P, CH])
        ps_before = s.ps("ps_before", [P, CH])
        ps_total = s.ps("ps_total", [P, CH])
        made = s.sem("made")
        before_zero = s.sem("before_zero")
        logits_ready = s.sem("logits_ready")
        shifted = s.sem("shifted")
        exp_ready = s.sem("exp_ready")
        chain = s.sem("chain")
        choice_ready = s.sem("choice_ready")
        ranks_ready = s.sem("ranks_ready")
        rows_ready = s.sem("rows_ready")
        block = s.block()
        logits = ps_logit[:, 0:NT * E].rearrange("p (t e) -> p t e", e=E)

        GROUP = 16

        def spread(col):
            return col[:, :, None].to_broadcast([P, NT, E])

        @block.gpsimd
        def _(pool):
            pool.iota(rev[:, :], [[-1, E]], base=E, channel_multiplier=0,
                      allow_small_or_imprecise_dtypes=True).then_inc(made, 1)
            pool.iota(tile_no[:, :, :], [[1, MT], [0, E]], base=0, channel_multiplier=0,
                      allow_small_or_imprecise_dtypes=True).then_inc(made, 1)
            pool.iota(lane[:, :], [[1, P]], base=0, channel_multiplier=0,
                      allow_small_or_imprecise_dtypes=True).then_inc(made, 1)
            pool.iota(tile_of[:, :], [[1, MT]], base=0, channel_multiplier=0,
                      allow_small_or_imprecise_dtypes=True).then_inc(made, 1)
            pool.iota(choice[:, :], [[P, 2 * NT]], base=1, channel_multiplier=1,
                      allow_small_or_imprecise_dtypes=True).then_inc(made, 1)
            pool.memset(ones_col[:, :], 1.0).then_inc(made, 1)
            pool.memset(everyone[:, :], 1.0).then_inc(made, 1)
            pool.memset(before[:, :], 1.0).then_inc(before_zero, 1)
            pool.wait_ge(before_zero, 1)
            pool.affine_select(out=before[:, :], in_=before[:, :], compare_op=ALU.is_gt, fill=0.0,
                               base=0, pattern=[[1, P]], channel_multiplier=-1).then_inc(made, 1)

        @block.tensor
        def _(pe):
            pe.wait_ge(g.late_loaded, g.LATE_LOADED)
            for t in range(NT):
                lo = HALO + (t % TB) * P
                last = pe.matmul(ps_logit[:, t * E:(t + 1) * E], g.xnT[:, t // TB, lo:lo + P], g.router[:, :],
                                 start=True, stop=True)
            last.then_inc(logits_ready, 1)
            pe.wait_ge(choice_ready, 1)
            pe.wait_ge(made, 8)
            pe.matmul(ps_before[:, 0:NT * E], before[:, :], both16[:, :], start=True, stop=True)
            pe.matmul(ps_total[:, 0:NT * E], everyone[:, :], both16[:, :], start=True, stop=True)\
                .then_inc(ranks_ready, 1)
            for T in range(2 * NT):
                if T % GROUP == 0:
                    pe.wait_ge(lists_ready, T // GROUP + 1)
                last = pe.matmul(ps_list[:, 0:MT], in_lane[:, T, :], in_tile[:, T, :], start=(T == 0),
                                 stop=(T == 2 * NT - 1))
            last.then_inc(list_found, 1)

        @block.scalar
        def _(act):
            act.wait_ge(shifted, 1)
            act.activation(score[:, :, :], prob[:, :, :], ACT.Exp).then_inc(exp_ready, 1)

        @block.vector
        def _(dve):
            done = [0]

            def then(instruction):
                done[0] += 1
                instruction.then_inc(chain, 1)
                dve.wait_ge(chain, done[0])

            dve.wait_ge(made, 8)
            dve.wait_ge(logits_ready, 1)
            then(dve.tensor_reduce(top[:, :], logits, AX.X, ALU.max))
            dve.tensor_tensor(prob[:, :, :], logits, spread(top), ALU.subtract).then_inc(shifted, 1)
            dve.wait_ge(exp_ready, 1)
            then(dve.tensor_reduce(denom[:, :], score[:, :, :], AX.X, ALU.add))
            then(dve.reciprocal(denom[:, :], denom[:, :]))
            then(dve.tensor_tensor(prob[:, :, :], score[:, :, :], spread(denom), ALU.mult))
            for chosen, p in ((first, p1), (second, p2)):
                then(dve.tensor_reduce(p[:, :], prob[:, :, :], AX.X, ALU.max))
                then(dve.tensor_tensor(equal[:, :, :], prob[:, :, :], spread(p), ALU.is_equal))
                then(dve.tensor_tensor(score[:, :, :], equal[:, :, :], rev[:, None, :].to_broadcast([P, NT, E]),
                                       ALU.mult))
                then(dve.tensor_reduce(best[:, :], score[:, :, :], AX.X, ALU.max))
                then(dve.tensor_tensor(chosen[:, :, :], score[:, :, :], spread(best), ALU.is_equal))
                if chosen is first:
                    then(dve.scalar_tensor_tensor(out=prob[:, :, :], in0=chosen[:, :, :], scalar=-2.0,
                                                  in1=prob[:, :, :], op0=ALU.mult, op1=ALU.add))
            then(dve.tensor_tensor(both[:, :, :], first[:, :, :], second[:, :, :], ALU.add))
            dve.tensor_copy(both16[:, :], both[:, :, :].rearrange("p t e -> p (t e)")).then_inc(choice_ready, 1)
            then(dve.tensor_tensor(denom[:, :], p1[:, :], p2[:, :], ALU.add))
            then(dve.tensor_scalar(denom[:, :], denom[:, :], 1e-9, None, ALU.add))
            then(dve.reciprocal(denom[:, :], denom[:, :]))
            then(dve.tensor_scalar(denom[:, :], denom[:, :], 0.5, None, ALU.mult))
            dve.tensor_tensor(g.weight[:, 0, :], p1[:, :], denom[:, :], ALU.mult).then_inc(rows_ready, 1)
            dve.tensor_tensor(g.weight[:, 1, :], p2[:, :], denom[:, :], ALU.mult).then_inc(rows_ready, 1)
            dve.wait_ge(ranks_ready, 1)
            then(dve.tensor_copy(total[:, :, :], ps_total[:, 0:NT * E].rearrange("p (t e) -> p t e", e=E)))
            for e in range(E):
                dve.tensor_tensor_scan(until[:, :, e], ones_col[:, :], total[:, :, e], 0.0, ALU.mult, ALU.add)\
                    .then_inc(chain, 1)
            done[0] += E
            dve.wait_ge(chain, done[0])
            then(dve.tensor_scalar(tiles[:, :], until[:, NT - 1, :], float(P - 1), None, ALU.add))
            then(dve.tensor_copy(count_i[:, :], tiles[:, :]))
            then(dve.tensor_scalar(count_i[:, :], count_i[:, :], 7, None, ALU.arith_shift_right))
            then(dve.tensor_copy(tiles[:, :], count_i[:, :]))
            then(dve.tensor_tensor_scan(tiles_until[:, :], ones_col[:, 0:E], tiles[:, :], 0.0, ALU.mult, ALU.add))
            then(dve.tensor_tensor(base[:, :], tiles_until[:, :], tiles[:, :], ALU.subtract))
            then(dve.tensor_tensor(until[:, :, :], until[:, :, :], total[:, :, :], ALU.subtract))
            then(dve.tensor_tensor(until[:, :, :], until[:, :, :],
                                   ps_before[:, 0:NT * E].rearrange("p (t e) -> p t e", e=E), ALU.add))
            then(dve.scalar_tensor_tensor(out=place[:, :, :], in0=base[:, None, :].to_broadcast([P, NT, E]),
                                          scalar=float(P), in1=until[:, :, :], op0=ALU.mult, op1=ALU.add))
            for k, chosen in enumerate((first, second)):
                then(dve.tensor_tensor(total[:, :, :], chosen[:, :, :], place[:, :, :], ALU.mult))
                then(dve.tensor_reduce(row_f[:, k, :], total[:, :, :], AX.X, ALU.add))
            then(dve.tensor_copy(row_i[:, :], row_f[:, :, :].rearrange("p k t -> p (k t)")))
            dve.tensor_scalar(part_i[:, 0, :], row_i[:, :], P - 1, None, ALU.bitwise_and).then_inc(chain, 1)
            dve.tensor_scalar(part_i[:, 1, :], row_i[:, :], 7, None, ALU.arith_shift_right).then_inc(chain, 1)
            done[0] += 2
            dve.wait_ge(chain, done[0])
            dve.tensor_copy(row_lo[:, :], part_i[:, 0, :]).then_inc(chain, 1)
            dve.tensor_copy(row_hi[:, :], part_i[:, 1, :]).then_inc(chain, 1)
            done[0] += 2
            dve.wait_ge(chain, done[0])
            for T in range(0, 2 * NT, GROUP):
                some = slice(T, T + GROUP)
                dve.tensor_tensor(in_lane[:, some, :], lane[:, None, :].to_broadcast([P, GROUP, P]),
                                  row_lo[:, some, None].to_broadcast([P, GROUP, P]), ALU.is_equal)
                then(dve.tensor_tensor(in_tile[:, some, :], tile_of[:, None, :].to_broadcast([P, GROUP, MT]),
                                       row_hi[:, some, None].to_broadcast([P, GROUP, MT]), ALU.is_equal))
                dve.tensor_tensor(in_tile[:, some, :], in_tile[:, some, :],
                                  choice[:, some, None].to_broadcast([P, GROUP, MT]), ALU.mult)\
                   .then_inc(lists_ready, 1)
            then(dve.tensor_tensor(tile_no[:, :, :], tile_no[:, :, :], base[0:1, None, :].to_broadcast([1, MT, E]),
                                   ALU.is_ge))
            then(dve.tensor_reduce(owner[:, :], tile_no[:, :, :], AX.X, ALU.add))
            then(dve.tensor_scalar(owner[:, :], owner[:, :], -1.0, None, ALU.add))
            then(dve.tensor_copy(g.owner[:, :], owner[:, :]))
            dve.wait_ge(list_found, 1)
            then(dve.tensor_scalar(found[:, :], ps_list[:, 0:MT], -1.0, None, ALU.add))
            dve.tensor_scalar(none[:, :], found[:, :], 0.0, float(4 * B * L), ALU.is_lt, ALU.mult).then_inc(chain, 1)
            dve.tensor_scalar(source_f[:, :], found[:, :], 0.0, None, ALU.max).then_inc(chain, 1)
            done[0] += 2
            dve.wait_ge(chain, done[0])
            dve.tensor_tensor(found[:, :], found[:, :], none[:, :], ALU.add).then_inc(chain, 1)
            dve.tensor_copy(source_i[:, :], source_f[:, :]).then_inc(chain, 1)
            done[0] += 2
            dve.wait_ge(chain, done[0])
            then(dve.tensor_copy(g.target[:, :], found[:, :]))
            then(dve.tensor_scalar(g.source[:, :], source_i[:, :].bitcast(U32), B * L - 1, None, ALU.bitwise_and))


def moe_expert_phase(nc, g, tag):
    with Scope(nc, tag) as s:
        xs = s.sb("xs", [P, XSLOTS, D])
        xT = s.sb("xT", [P, 2, P])
        pre = s.sb("pre", [P, 2, F])
        hT = s.sb("hT", [P, 2, FC, P])
        ys = s.sb("ys", [P, YSLOTS, D])
        ps_x = s.ps("ps_x", [P, 2, CH])
        ps_h = s.ps("ps_h", [P, 2, CH])
        ps_t = s.ps("ps_t", [P, 2, CH])
        ps_y = s.ps("ps_y", [P, 2, CH])
        x_in = [s.sem(f"x_in{k}") for k in range(XSLOTS)]
        x_turned = s.sem("x_turned")
        xT_ready = s.sem("xT_ready")
        up_ready = s.sem("up_ready")
        pre_ready = s.sem("pre_ready")
        h_turned = s.sem("h_turned")
        hT_ready = s.sem("hT_ready")
        down_ready = s.sem("down_ready")
        y_ready = s.sem("y_ready")
        y_out = [s.sem(f"y_out{k}") for k in range(YSLOTS)]
        block = s.block()

        def steps(eng, step):
            for n in range(XSLOTS):
                step(n, n, n)
            with eng.Fori(1, MT // XSLOTS) as q:
                for r in range(XSLOTS):
                    step(q * XSLOTS + r, r, None)
            for n in range(MT, MT + 3):
                step(n, n % XSLOTS, n)

        def on(n, lag):
            return n is None or 0 <= n - lag < MT

        @block.gpsimd
        def _(pool):
            def gather(n):
                if n >= XSLOTS:
                    pool.wait_ge(x_turned, n - XSLOTS + 1)
                pool.indirect_dma_start(
                    out=xs[:, n % XSLOTS, :], out_offset=None, in_=g.token_rows[:, :],
                    in_offset=bass.IndirectOffsetOnAxis(ap=g.source[:, n:n + 1], axis=0))\
                    .then_inc(x_in[n % XSLOTS], 16)

            for n in range(XSLOTS - 2):
                gather(n)
            for n in range(MT):
                if n + XSLOTS - 2 < MT:
                    gather(n + XSLOTS - 2)
                pool.wait_ge(y_ready, n + 1)
                pool.indirect_dma_start(
                    out=g.expert_rows[:, :], out_offset=bass.IndirectOffsetOnAxis(ap=g.target[:, n:n + 1], axis=0),
                    in_=ys[:, n % YSLOTS, :], in_offset=None, bounds_check=2 * B * L - 1, oob_is_err=False)\
                    .then_inc(y_out[n % YSLOTS], 16)
            for k in range(YSLOTS):
                pool.wait_ge(y_out[k], 16 * (MT // YSLOTS))

        @block.tensor
        def _(pe):
            def step(n, r, known):
                if on(known, 0):
                    k = r % XSLOTS
                    pe.wait_ge(x_in[k], (n - r) * (16 // XSLOTS) + 16 if known is None
                               else 16 * (known // XSLOTS + 1))
                    pe.wait_ge(xT_ready, n + 1)
                    pe.transpose(ps_x[:, r % 2, 0:P], xs[:, k, :], g.ident[:, :]).then_inc(x_turned, 1)
                if on(known, 1):
                    m = (r + 1) % 2
                    e = pe.value_load(g.owner[0:1, bass.ds(n - 1, 1)], min_val=0, max_val=E - 1)
                    pe.wait_ge(xT_ready, n - 1 + 3)
                    pe.wait_ge(pre_ready, n - 1 + 1)
                    pe.matmul(ps_h[:, m, :], xT[:, m, :], g.w1[:, bass.ds(e * F, F)], start=True, stop=True)\
                        .then_inc(up_ready, 1)
                if on(known, 2):
                    m = r % 2
                    pe.wait_ge(pre_ready, n - 2 + 3)
                    pe.wait_ge(hT_ready, n - 2 + 1)
                    for c in range(FC):
                        last = pe.transpose(ps_t[:, m, c * P:(c + 1) * P], pre[:, m, c * P:(c + 1) * P], g.ident[:, :])
                    last.then_inc(h_turned, 1)
                if on(known, 3):
                    m = (r + 1) % 2
                    e = pe.value_load(g.owner[0:1, bass.ds(n - 3, 1)], min_val=0, max_val=E - 1)
                    pe.wait_ge(hT_ready, n - 3 + 3)
                    pe.wait_ge(y_ready, n - 3 + 1 - 2 if known is None else max(known - 4, 0))
                    for c in range(FC):
                        last = pe.matmul(ps_y[:, m, 0:D], hT[:, m, c, :], g.w2[:, bass.ds(e * F + c * D, D)],
                                         start=(c == 0), stop=(c == FC - 1))
                    last.then_inc(down_ready, 1)

            steps(pe, step)

        @block.scalar
        def _(act):
            act.sem_inc(xT_ready, 2)
            act.sem_inc(hT_ready, 2)

            def step(n, r, known):
                if on(known, 0):
                    act.wait_ge(x_turned, n + 1)
                    if known is None or known >= 2:
                        act.wait_ge(up_ready, n - 1)
                    act.activation(xT[:, r % 2, :], ps_x[:, r % 2, 0:P], ACT.Copy).then_inc(xT_ready, 1)
                if on(known, 2):
                    act.wait_ge(h_turned, n - 2 + 1)
                    if known is None or known >= 4:
                        act.wait_ge(down_ready, n - 3)
                    act.activation(hT[:, r % 2, :, :].rearrange("p c t -> p (c t)"), ps_t[:, r % 2, :], ACT.Relu)\
                        .then_inc(hT_ready, 1)

            steps(act, step)

        @block.vector
        def _(dve):
            dve.sem_inc(pre_ready, 2)

            def step(n, r, known):
                if on(known, 1):
                    m = (r + 1) % 2
                    e = dve.value_load(g.owner[0:1, bass.ds(n - 1, 1)], min_val=0, max_val=E - 1)
                    dve.wait_ge(up_ready, n - 1 + 1)
                    if known is None or known >= 3:
                        dve.wait_ge(h_turned, n - 2)
                    dve.tensor_tensor(pre[:, m, :], ps_h[:, m, :], g.b1[:, bass.ds(e * F, F)], ALU.add)\
                        .then_inc(pre_ready, 1)
                if on(known, 3):
                    k = (r + 1) % YSLOTS
                    e = dve.value_load(g.owner[0:1, bass.ds(n - 3, 1)], min_val=0, max_val=E - 1)
                    dve.wait_ge(down_ready, n - 3 + 1)
                    if known is None:
                        first = (r - 3) % YSLOTS
                        dve.wait_ge(y_out[k], (n - 3 - first) * (16 // YSLOTS))
                    elif known - 3 >= YSLOTS:
                        dve.wait_ge(y_out[k], 16 * ((known - 3) // YSLOTS))
                    dve.tensor_tensor(ys[:, k, :], ps_y[:, m_of(r), 0:D], g.b2[:, bass.ds(e * D, D)], ALU.add)\
                        .then_inc(y_ready, 1)

            def m_of(r):
                return (r + 1) % 2

            steps(dve, step)


def moe_combine_phase(nc, g, tag):
    with Scope(nc, tag) as s:
        GROUP = 4
        rows = s.sb("rows", [P, 2, NT, D])
        fetched = [s.sem(f"fetched{q}") for q in range(NT // GROUP)]
        half_added = s.sem("half_added")
        block = s.block()

        @block.sync
        def _(sp):
            src = g.expert_rows.rearrange("(k t p) c -> p k t c", p=P, t=NT)
            for q in range(NT // GROUP):
                some = slice(q * GROUP, (q + 1) * GROUP)
                for k in range(2):
                    sp.dma_start(rows[:, k, some, :], src[:, k, some, :]).then_inc(fetched[q], 16)

        @block.vector
        def _(dve):
            for q in range(NT // GROUP):
                dve.wait_ge(fetched[q], 16 * 2)
                for k in range(2):
                    for t in range(q * GROUP, (q + 1) * GROUP):
                        if k == 1:
                            dve.wait_ge(half_added, t + 1)
                        last = dve.scalar_tensor_tensor(out=g.x[:, t, :], in0=rows[:, k, t, :],
                                                        scalar=g.weight[:, k, t:t + 1], in1=g.x[:, t, :],
                                                        op0=ALU.mult, op1=ALU.add)
                        if k == 0:
                            last.then_inc(half_added, 1)


def attention_phase(nc, g, A):
    STEPS = 2 * TB
    PAIRS = H // 2
    projections = {1: ("y", 1, 0), 3: ("y", 1, 1), 5: ("v", 0, 0), 7: ("v", 0, 1),
                   9: ("y", 2, 0), 11: ("y", 2, 1), 13: ("v", 0, 2), 15: ("v", 0, 3)}
    at = sorted(projections)
    before = {s: at[n - 1] for n, s in enumerate(at)}
    V_CHUNKS = 4
    parts = [[(lo, min(lo + 4, s % TB + 1)) for lo in range(0, s % TB + 1, 4)] for s in range(STEPS)]
    upto = [sum(len(p) for p in parts[:s + 1]) for s in range(STEPS)]
    UNITS = upto[-1]
    PASSES = ((0, 0), (0, 1), (1, 0))
    with Scope(nc, "attn") as s_:
        xk = s_.sb("xk", [P, 2, 2, L], F32R)
        xs = s_.sb("xs", [P, 2, L], F32R)
        m_all = s_.sb("m_all", [P, 2, H * D], F32R)
        n_all = s_.sb("n_all", [P, 2, H * D], F32R)
        m = s_.sb("m", [P, 2, 2, D], F32R)
        y = s_.sb("y", [P, 2, 2, L], F32R)
        v = s_.sb("v", [P, 2, TB, 2 * D])
        probs = s_.sb("probs", [P, 2, L])
        pT = s_.sb("pT", [P, 2, L])
        neg_max = s_.sb("neg_max", [P, 2])
        row_sum = s_.sb("row_sum", [P, 4])
        inv_sum = s_.sb("inv_sum", [P, 2])
        ident16 = s_.sb("ident16", [P, P], BF16)
        causal = s_.sb("causal", [P, P], BF16)
        ps_s = s_.ps("ps_s", [P, 2, L])
        ps_t = s_.ps("ps_t", [P, 2, CH])
        ps_p = s_.ps("ps_p", [P, CH])
        ps_o = s_.ps("ps_o", [P, CH])
        mask_steps = s_.sem("mask_steps")
        folded = s_.sem("folded")
        fold_hi = s_.sem("fold_hi")
        fold_lo = s_.sem("fold_lo")
        x_hi = s_.sem("x_hi")
        x_lo = s_.sem("x_lo")
        x_staged = s_.sem("x_staged")
        m_staged = s_.sem("m_staged")
        waited = s_.sem("waited")
        y_ready = s_.sem("y_ready")
        y_hi = s_.sem("y_hi")
        y_lo = s_.sem("y_lo")
        v_ready = s_.sem("v_ready")
        v_copied = s_.sem("v_copied")
        scores_ready = s_.sem("scores_ready")
        max_ready = s_.sem("max_ready")
        probs_ready = s_.sem("probs_ready")
        turned = s_.sem("turned")
        pT_copied = s_.sem("pT_copied")
        pv_ready = s_.sem("pv_ready")
        inv_ready = s_.sem("inv_ready")
        added = s_.sem("added")
        block = s_.block()

        def sequence(G):
            return 0 if isinstance(G, int) else (G // PAIRS) % B

        @block.gpsimd
        def _(pool):
            pool.memset(ident16[:, :], 0.0).then_inc(mask_steps, 1)
            pool.memset(causal[:, :], 0.0).then_inc(mask_steps, 1)
            pool.wait_ge(mask_steps, 2)
            pool.affine_select(out=ident16[:, :], in_=ident16[:, :], compare_op=ALU.not_equal, fill=1.0,
                               base=0, pattern=[[-1, P]], channel_multiplier=1).then_inc(mask_steps, 1)
            pool.affine_select(out=causal[:, :], in_=causal[:, :], compare_op=ALU.is_ge, fill=-1e30,
                               base=0, pattern=[[-1, P]], channel_multiplier=1).then_inc(mask_steps, 1)

            def stage_x(b, slot):
                x = g.xnT[:, b, HALO:HALO + L]
                pool.wait_ge(v_ready, V_CHUNKS * PAIRS * b + 1)
                pool.sem_inc(waited, 1)
                pool.tensor_copy(xk[:, slot, 0, :], x).then_inc(x_hi, 1)
                pool.wait_ge(x_hi, b + 1)
                pool.sem_inc(waited, 1)
                pool.tensor_tensor(xk[:, slot, 1, :], x, xk[:, slot, 0, :].bitcast(F32), ALU.subtract)\
                    .then_inc(x_lo, 1)
                pool.wait_ge(x_lo, b + 1)
                pool.sem_inc(waited, 1)
                pool.tensor_copy(xs[:, :, :], xk[:, slot, :, :]).then_inc(x_staged, 1)

            def stage_m(head, h, slot):
                pool.wait_ge(y_ready, 2 * head + 2)
                pool.sem_inc(waited, 1)
                pool.tensor_copy(m[:, slot, :, :], m_all[:, :, bass.ds(h * D, D)]).then_inc(m_staged, 1)

            with pool.Fori(0, B) as b:
                stage_x(b, b % 2)
                pool.wait_ge(fold_lo, 1)
                with pool.Fori(0, PAIRS) as pair:
                    for slot in range(2):
                        stage_m(b * H + pair * 2 + slot, pair * 2 + slot, slot)
            stage_m(B * H, 0, 0)

        @block.tensor
        def _(pe):
            def project_y(G, c, head, slot):
                pe.wait_ge(m_staged, head + 1)
                b = sequence(G)
                for k, (one, two) in enumerate(PASSES):
                    last = pe.matmul(ps_p[:, :], m[:, slot, one, :], xk[:, b % 2, two, c * CH:(c + 1) * CH],
                                     start=(k == 0), stop=(k == 2))
                last.then_inc(y_ready, 1)

            def project_v(G, c):
                pe.wait_ge(x_staged, sequence(G) + 1)
                pair = 0 if isinstance(G, int) else G % PAIRS
                for j in range(2):
                    t = 2 * c + j
                    for k, (one, two) in enumerate(PASSES):
                        last = pe.matmul(ps_p[:, j * 2 * D:(j + 1) * 2 * D], xs[:, one, t * P:(t + 1) * P],
                                         n_all[:, two, bass.ds(pair * 2 * D, 2 * D)], start=(k == 0), stop=(k == 2))
                last.then_inc(v_ready, 1)

            def scores(G, s, head, slot):
                i = s % TB
                t = G * STEPS + s
                pe.wait_ge(y_lo, 2 * head + i // 4 + 1)
                pe.wait_ge(probs_ready, t + 1)
                b = sequence(G)
                n = (i + 1) * P
                for lo in range(0, n, CH):
                    hi = min(lo + CH, n)
                    wide = max(hi, lo + 2 * P)
                    for k, (one, two) in enumerate(PASSES):
                        pe.matmul(ps_s[:, i % 2, lo:wide], y[:, slot, one, i * P:(i + 1) * P],
                                  xk[:, b % 2, two, lo:wide], start=(k == 0), stop=(hi < n and k == 2))
                pe.matmul(ps_s[:, i % 2, i * P:n], ident16[:, :], causal[:, :], start=False, stop=True)\
                    .then_inc(scores_ready, 1)

            def turn(G, s):
                pe.wait_ge(probs_ready, G * STEPS + s + 3)
                for n, (lo, hi) in enumerate(parts[s]):
                    u = upto[s] - len(parts[s]) + n
                    pe.wait_ge(pT_copied, UNITS * G + u + 1)
                    for j in range(lo, hi):
                        last = pe.transpose(ps_t[:, u % 2, (j - lo) * P:(j - lo + 1) * P],
                                            probs[:, s % 2, j * P:(j + 1) * P], g.ident[:, :])
                    last.then_inc(turned, 1)

            def values(G, s):
                i = s % TB
                pe.wait_ge(pT_copied, UNITS * G + upto[s] + 2)
                pe.wait_ge(v_copied, V_CHUNKS * G + V_CHUNKS)
                pe.wait_ge(added, G * STEPS + s + 2)
                for j in range(i + 1):
                    last = pe.matmul(ps_o[:, 0:D], pT[:, s % 2, j * P:(j + 1) * P],
                                     v[:, G % 2, j, (s // TB) * D:(s // TB + 1) * D], start=(j == 0), stop=(j == i))
                last.then_inc(pv_ready, 1)

            pe.sem_inc(v_ready, 1)
            pe.sem_inc(y_ready, 4)
            pe.sem_inc(pv_ready, 2)
            pe.wait_ge(g.late_loaded, g.LATE_LOADED)
            for h in range(H):
                at = slice((h % 4) * D, (h % 4 + 1) * D)
                w = slice(h * D, (h + 1) * D)
                pe.matmul(ps_s[:, 0, (h // 4) * CH:(h // 4 + 1) * CH][:, at], g.w_qkv[:, 0, w], g.w_qkv[:, 1, w],
                          start=True, stop=True)
                last = pe.matmul(ps_s[:, 1, (h // 4) * CH:(h // 4 + 1) * CH][:, at], g.w_qkv[:, 2, w], g.w_o[:, w],
                                 start=True, stop=True)
            last.then_inc(folded, 1)
            pe.wait_ge(fold_lo, 2)
            pe.wait_ge(x_staged, 1)
            pe.wait_ge(mask_steps, 4)
            for c in range(2):
                if c > 0:
                    pe.wait_ge(y_lo, c)
                project_y(0, c, 0, 0)
            pe.wait_ge(y_lo, 2)
            for c in range(V_CHUNKS):
                if c > 0:
                    pe.wait_ge(v_copied, c)
                project_v(0, c)
            for s in range(2):
                scores(0, s, 0, 0)
            with pe.Fori(0, B * PAIRS) as G:
                for s in range(STEPS):
                    r = s + 2
                    scores(G + r // STEPS, r % STEPS, 2 * G + r // TB, (r // TB) % 2)
                    turn(G, s)
                    if s > 0:
                        values(G, s - 1)
                    if s in projections:
                        kind, ahead, c = projections[s]
                        was, ahead_was, c_was = projections[before[s]]
                        if was == "y":
                            pe.wait_ge(y_lo, 2 * (2 * G + ahead_was) + c_was + 1)
                        else:
                            pe.wait_ge(v_copied, V_CHUNKS * (G + (s > before[s])) + c_was + 1)
                        if kind == "y":
                            project_y(G + ahead // 2, c, 2 * G + ahead, ahead % 2)
                        else:
                            project_v(G + 1, c)
                values(G, STEPS - 1)

        @block.scalar
        def _(act):
            def take_y(c, head, slot):
                act.wait_ge(y_ready, 2 * head + c + 1 + 4)
                act.activation(y[:, slot, 0, c * CH:(c + 1) * CH], ps_p[:, :], ACT.Copy).then_inc(y_hi, 1)

            def take_v(G, c):
                act.wait_ge(v_ready, V_CHUNKS * G + c + 1 + 1)
                act.sem_inc(waited, 1)
                act.activation(v[:, G % 2, 2 * c:2 * c + 2, :].rearrange("p t c -> p (t c)"), ps_p[:, :], ACT.Copy)\
                    .then_inc(v_copied, 1)

            def exponentials(G, s):
                t = G * STEPS + s
                i = s % TB
                act.wait_ge(max_ready, t + 1)
                n = (i + 1) * P
                act.activation(probs[:, s % 2, 0:n], ps_s[:, s % 2, 0:n], ACT.Exp, bias=neg_max[:, s % 2:s % 2 + 1],
                               accum_out=row_sum[:, s % 4:s % 4 + 1]).then_inc(probs_ready, 1)

            act.sem_inc(probs_ready, 2)
            act.wait_ge(folded, 1)
            act.activation(m_all[:, 0, :], ps_s[:, 0, :], ACT.Copy, scale=DH ** -0.5).then_inc(fold_hi, 1)
            act.activation(n_all[:, 0, :], ps_s[:, 1, :], ACT.Copy).then_inc(fold_hi, 1)
            for c in range(2):
                take_y(c, 0, 0)
            for c in range(V_CHUNKS):
                take_v(0, c)
            for s in range(2):
                exponentials(0, s)
            with act.Fori(0, B * PAIRS) as G:
                for s in range(STEPS):
                    act.wait_ge(turned, UNITS * G + upto[s])
                    exponentials(G + (s + 2) // STEPS, (s + 2) % STEPS)
                    if s in projections:
                        kind, ahead, c = projections[s]
                        if kind == "y":
                            take_y(c, 2 * G + ahead, ahead % 2)
                        else:
                            take_v(G + 1, c)

        @block.vector
        def _(dve):
            def rest_of_y(c, head, slot):
                dve.wait_ge(y_hi, 2 * head + c + 1)
                dve.tensor_tensor(y[:, slot, 1, c * CH:(c + 1) * CH], ps_p[:, :],
                                  y[:, slot, 0, c * CH:(c + 1) * CH].bitcast(F32), ALU.subtract).then_inc(y_lo, 1)

            def maxima(G, s):
                dve.wait_ge(scores_ready, G * STEPS + s + 1)
                dve.tensor_reduce(neg_max[:, s % 2:s % 2 + 1], ps_s[:, s % 2, 0:(s % TB + 1) * P], AX.X, ALU.max,
                                  negate=True).then_inc(max_ready, 1)

            def add(G, s):
                t = G * STEPS + s
                dve.wait_ge(inv_ready, t + 1)
                dve.wait_ge(pv_ready, t + 3)
                x = g.x[:, (G // PAIRS) * TB + s % TB, :]
                dve.scalar_tensor_tensor(out=x, in0=ps_o[:, 0:D], scalar=inv_sum[:, s % 2:s % 2 + 1], in1=x,
                                         op0=ALU.mult, op1=ALU.add).then_inc(added, 1)

            dve.sem_inc(pT_copied, 2)
            dve.sem_inc(added, 2)
            for k, (to, scale) in enumerate(((m_all, DH ** -0.5), (n_all, 1.0))):
                dve.wait_ge(fold_hi, k + 1)
                dve.scalar_tensor_tensor(out=to[:, 1, :], in0=ps_s[:, k, :], scalar=scale, in1=to[:, 0, :].bitcast(F32),
                                         op0=ALU.mult, op1=ALU.subtract).then_inc(fold_lo, 1)
            for c in range(2):
                rest_of_y(c, 0, 0)
            for s in range(2):
                maxima(0, s)
            with dve.Fori(0, B * PAIRS) as G:
                for s in range(STEPS):
                    t = G * STEPS + s
                    maxima(G + (s + 2) // STEPS, (s + 2) % STEPS)
                    dve.wait_ge(probs_ready, t + 3)
                    dve.wait_ge(added, t + 1)
                    dve.reciprocal(inv_sum[:, s % 2:s % 2 + 1], row_sum[:, s % 4:s % 4 + 1]).then_inc(inv_ready, 1)
                    for n, (lo, hi) in enumerate(parts[s]):
                        u = upto[s] - len(parts[s]) + n
                        dve.wait_ge(turned, UNITS * G + u + 1)
                        dve.wait_ge(pv_ready, t + 1)
                        dve.tensor_copy(pT[:, s % 2, lo * P:hi * P], ps_t[:, u % 2, 0:(hi - lo) * P])\
                            .then_inc(pT_copied, 1)
                    if s > 0:
                        add(G, s - 1)
                    if s in projections and projections[s][0] == "y":
                        _, ahead, c = projections[s]
                        rest_of_y(c, 2 * G + ahead, ahead % 2)
                add(G, STEPS - 1)


def store_phase(nc, g, out):
    with Scope(nc, "store") as s:
        stored = s.sem("stored")
        block = s.block()

        @block.sync
        def _(sp):
            view = out.rearrange("b (n p) c -> p (b n) c", p=P)
            for q in range(4):
                n = NT // 4
                sp.dma_start(view[:, q * n:(q + 1) * n, :], g.x[:, q * n:(q + 1) * n, :]).then_inc(stored, 16)
            sp.wait_ge(stored, 64)


class Shared:
    pass


STAGES = 6
SKIP = 0


def program(nc, A, out):
    _ = 0
    with ExitStack() as stack:
        g = Shared()
        g.x = stack.enter_context(nc.sbuf_tensor("x", [P, NT, D], F32))
        g.xnT = stack.enter_context(nc.sbuf_tensor("xnT", [P, B, HALO + L], F32))
        g.ident = stack.enter_context(nc.sbuf_tensor("ident", [P, P], F32))
        g.w_ffn = stack.enter_context(nc.sbuf_tensor("w_ffn", [P, 3, D], F32))
        g.mu = stack.enter_context(nc.sbuf_tensor("mu", [P, 2], F32))
        g.w_in = stack.enter_context(nc.sbuf_tensor("w_in", [P, 2 * NB * P], F32))
        g.w_x = stack.enter_context(nc.sbuf_tensor("w_x", [P, NB, R + 3 * BC], F32))
        g.w_dt = stack.enter_context(nc.sbuf_tensor("w_dt", [R, NB * P], F32))
        g.w_out = stack.enter_context(nc.sbuf_tensor("w_out", [P, NB, D], F32))
        g.conv_w = stack.enter_context(nc.sbuf_tensor("conv_w", [P, NB, 2 * KW], F32))
        g.conv_b = stack.enter_context(nc.sbuf_tensor("conv_b", [P, NB, 2], F32))
        g.b_dt = stack.enter_context(nc.sbuf_tensor("b_dt", [P, NB], F32))
        g.d_param = stack.enter_context(nc.sbuf_tensor("d_param", [P, NB], F32))
        g.a_log = stack.enter_context(nc.sbuf_tensor("a_log", [P, NB, NS], F32))
        g.neg_a = stack.enter_context(nc.sbuf_tensor("neg_a", [P, NB, NS], F32))
        g.gates = stack.enter_context(nc.sbuf_tensor("gates", [P, 2], F32))
        g.weights = [(g.w_ffn[:, :, :], "w_ffn"), (g.mu[:, :], "mu"), (g.w_in[:, :], "w_in"), (g.w_x[:, :, :], "w_x"),
                     (g.w_dt[:, :], "w_dt"), (g.w_out[:, :, :], "w_out"), (g.conv_w[:, :, :], "conv_w"),
                     (g.conv_b[:, :, :], "conv_b"), (g.b_dt[:, :], "b_dt"), (g.d_param[:, :], "d_param"),
                     (g.a_log[:, :, :], "a_log"), (g.gates[:, :], "gates")]
        g.loaded = stack.enter_context(nc.semaphore("loaded"))
        g.LOADED = 16 * len(g.weights)
        g.token_rows = nc.dram_tensor("token_rows", (B * L, D), F32, kind="Internal").ap()
        g.expert_rows = nc.dram_tensor("expert_rows", (2 * B * L, D), F32, kind="Internal").ap()
        load_phase(nc, g, A)
        if STAGES >= 1:
            layernorm_phase(nc, g, "ln0")
            ffn_phase(nc, g, "ffn0")
        if STAGES >= 2 and not SKIP:
            layernorm_phase(nc, g, "ln1")
            mamba_phase(nc, g, A)
        if STAGES >= 3:
            layernorm_phase(nc, g, "ln2")
            g.w1 = stack.enter_context(nc.sbuf_tensor("w1", [P, E * F], F32))
            g.w2 = stack.enter_context(nc.sbuf_tensor("w2", [P, E * F], F32))
            g.b1 = stack.enter_context(nc.sbuf_tensor("b1", [P, E * F], F32))
            g.b2 = stack.enter_context(nc.sbuf_tensor("b2", [P, E * D], F32))
            g.router = stack.enter_context(nc.sbuf_tensor("router", [P, E], F32))
            g.source = stack.enter_context(nc.sbuf_tensor("source", [P, MT], U32))
            g.target = stack.enter_context(nc.sbuf_tensor("target", [P, MT], U32))
            g.weight = stack.enter_context(nc.sbuf_tensor("weight", [P, 2, NT], F32))
            g.owner = stack.enter_context(nc.sbuf_tensor("owner", [1, MT], I32))
            g.w_qkv = stack.enter_context(nc.sbuf_tensor("w_qkv", [P, 3, H * D], F32))
            g.w_o = stack.enter_context(nc.sbuf_tensor("w_o", [P, H * D], F32))
            g.gamma = stack.enter_context(nc.sbuf_tensor("gamma", [P, 1], F32))
            g.late_loaded = stack.enter_context(nc.semaphore("late_loaded"))
            g.late_weights = [(g.w1[:, :], "w1"), (g.w2[:, :], "w2"), (g.b1[:, :], "b1"), (g.b2[:, :], "b2"),
                              (g.router[:, :], "router"), (g.w_qkv[:, :, :], "w_qkv"), (g.w_o[:, :], "w_o"),
                              (g.gamma[:, :], "gamma")]
            g.LATE_LOADED = 16 * len(g.late_weights)
            load_experts_phase(nc, g, A)
            ffn_phase(nc, g, "ffn1")
        if STAGES >= 4:
            layernorm_phase(nc, g, "ln3", keep_tokens=True)
            moe_route_phase(nc, g, "route0")
            moe_expert_phase(nc, g, "experts0")
            moe_combine_phase(nc, g, "combine0")
        if STAGES >= 5:
            layernorm_phase(nc, g, "ln4", rms_gamma=g.gamma[:, 0:1])
            attention_phase(nc, g, A)
        if STAGES >= 6:
            layernorm_phase(nc, g, "ln5", keep_tokens=True)
            moe_route_phase(nc, g, "route1")
            moe_expert_phase(nc, g, "experts1")
            moe_combine_phase(nc, g, "combine1")
        store_phase(nc, g, out)




def laid_out(i):
    def t(a):
        return np.ascontiguousarray(np.asarray(a).T)
    def blocks(a):
        a = np.asarray(a)
        return np.ascontiguousarray(a.reshape(NB, P, -1).transpose(1, 0, 2))

    w_x = np.asarray(i["L0_attn_W_x"]).T
    return {
        "hidden": np.ascontiguousarray(np.asarray(i["L0_attn_hidden_states"]).reshape(B * L, D)),
        "w_ffn": np.stack([t(i["L0_ffn_W_r"]), t(i["L0_ffn_W_k"]), t(i["L0_ffn_W_v"])], axis=1),
        "mu": np.stack([np.asarray(i["L0_ffn_mu_r"]), np.asarray(i["L0_ffn_mu_k"])], axis=1),
        "w_in": t(i["L0_attn_W_in"]),
        "w_x": blocks(np.concatenate([w_x[:, :R]] + 3 * [w_x[:, R:]], axis=1)),
        "w_dt": t(i["L0_attn_W_dt"]),
        "w_out": blocks(t(i["L0_attn_W_out"])),
        "conv_w": blocks(np.concatenate([i["L0_attn_conv_w1"], i["L0_attn_conv_w2"]], axis=1)),
        "conv_b": blocks(np.stack([i["L0_attn_conv_b1"], i["L0_attn_conv_b2"]], axis=1)),
        "b_dt": blocks(i["L0_attn_b_dt"])[:, :, 0],
        "d_param": blocks(i["L0_attn_D_param"])[:, :, 0],
        "a_log": blocks(i["L0_attn_A_log"]),
        "w1": np.asarray(i["L1_ffn_w1"]).transpose(2, 0, 1).reshape(P, E * F),
        "w2": np.asarray(i["L1_ffn_w2"]).reshape(E, D, FC, P).transpose(3, 0, 2, 1).reshape(P, E * F),
        "b1": np.broadcast_to(np.asarray(i["L1_ffn_b1"]).reshape(1, E * F), (P, E * F)),
        "b2": np.broadcast_to(np.asarray(i["L1_ffn_b2"]).reshape(1, E * D), (P, E * D)),
        "w_qkv": np.asarray(i["L1_attn_w_qkv"]).reshape(3, H, DH, D).transpose(2, 0, 1, 3).reshape(DH, 3, H * D),
        "w_o": np.asarray(i["L1_attn_w_out"]).reshape(D, H, DH).transpose(2, 1, 0).reshape(DH, H * D),
        "gamma": np.asarray(i["L1_attn_gamma"])[:, None],
        "router": t(i["L1_ffn_router_w"]),
        "gates": np.broadcast_to(np.asarray(i["L0_attn_conv_gates"])[None], (P, 2)),
    }


def kernel(**inputs):
    import concourse.bacc as bacc
    from concourse.bass_utils import run_bass_kernel_spmd

    nc = bacc.Bacc("TRN2", target_bir_lowering=False, num_devices=1)
    arrays, aps = {}, {}
    for name, a in laid_out(inputs).items():
        a = np.ascontiguousarray(a)
        arrays[f"in_{name}"] = a
        aps[name] = nc.dram_tensor(f"in_{name}", a.shape, mybir.dt.from_np(a.dtype), kind="ExternalInput").ap()
    out = nc.dram_tensor("out_x", (B, L, D), F32, kind="ExternalOutput").ap()
    program(nc, aps, out)
    r = run_bass_kernel_spmd(nc, [arrays], core_ids=[0])
    return r.results[0]["out_x"]
```

```python
from contextlib import ExitStack

import numpy as np

import concourse.bass as bass
from concourse import mybir

F32 = mybir.dt.float32
F32R = mybir.dt.float32r
BF16 = mybir.dt.bfloat16
I32 = mybir.dt.int32
U32 = mybir.dt.uint32
ALU = mybir.AluOpType
ACT = mybir.ActivationFunctionType
AX = mybir.AxisListType

P = 128
B, L, D = 4, 1024, 128
NT = B * L // P
TB = L // P
CH = 512
HALVES = L // CH
HALO = 6
LN_EPS = 1e-5

NB = 2
NS = 16
R = 64
BC = 2 * NS
KW = 4

H, DH = 8, 128

E, F = 8, 512
FC = F // P
MT = 72
XSLOTS = 8
YSLOTS = 4
assert MT % XSLOTS == 0 and MT >= 2 * NT + E - 1


class Scope:

    def __init__(self, nc, tag):
        self.nc, self.tag, self.stack, self.sems = nc, tag, ExitStack(), []

    def __enter__(self):
        return self

    def __exit__(self, *e):
        self.stack.__exit__(*e)
        if e[0] is None and self.sems:
            self.nc.clear_and_free_semaphores(self.sems)
            self.nc.all_engine_barrier()

    def sb(self, name, shape, dt=F32):
        return self.stack.enter_context(self.nc.sbuf_tensor(f"{self.tag}_{name}", shape, dt))

    def ps(self, name, shape, dt=F32):
        return self.stack.enter_context(self.nc.psum_tensor(f"{self.tag}_{name}", shape, dt))

    def sem(self, name):
        handle = self.nc.alloc_semaphore(f"{self.tag}_{name}")
        self.sems.append(handle)
        return handle

    def block(self):
        return self.stack.enter_context(self.nc.Block())


def load_phase(nc, g, A):
    with Scope(nc, "load") as s:
        dma_in = s.sem("dma_in")
        halo_zero = s.sem("halo_zero")
        ident_zero = s.sem("ident_zero")
        ident_done = s.sem("ident_done")
        block = s.block()

        @block.sync
        def _(sp):
            hid = A["hidden"].rearrange("(n p) c -> p n c", p=P)
            for q in range(4):
                n = NT // 4
                sp.dma_start(g.x[:, q * n:(q + 1) * n, :], hid[:, q * n:(q + 1) * n, :]).then_inc(dma_in, 16)
            sp.wait_ge(dma_in, 64)

        @block.scalar
        def _(act):
            for dst, name in g.weights:
                act.dma_start(dst, A[name]).then_inc(g.loaded, 16)

        @block.gpsimd
        def _(pool):
            pool.memset(g.ident[:, :], 0.0).then_inc(ident_zero, 1)
            pool.wait_ge(ident_zero, 1)
            pool.affine_select(out=g.ident[:, :], in_=g.ident[:, :], compare_op=ALU.not_equal, fill=1.0,
                               base=0, pattern=[[-1, P]], channel_multiplier=1).then_inc(ident_done, 1)

        @block.vector
        def _(dve):
            dve.memset(g.xnT[:, :, 0:HALO], 0.0).then_inc(halo_zero, 1)


def layernorm_phase(nc, g, tag, keep_tokens=False, rms_gamma=None):
    with Scope(nc, tag) as s:
        stats = s.sb("stats", [P, NT, 6])
        work = s.sb("work", [P, 9, NT])
        SLOTS = 4
        CHUNKS = B * HALVES
        stage = s.sb("stage", [P, SLOTS, 4, P])
        psT = s.ps("psT", [P, SLOTS, CH])
        stats_done = s.sem("stats_done")
        chain = s.sem("chain")
        var_ready = s.sem("var_ready")
        std_ready = s.sem("std_ready")
        staged = s.sem("staged")
        staged_too = s.sem("staged_too")
        norm_ready = s.sem("norm_ready")
        rows_kept = [s.sem(f"rows_kept{c}") for c in range(SLOTS)]
        transposed = s.sem("transposed")
        psT_free = s.sem("psT_free")
        diff, total, m2, var, std, rstd, mean, shift, lengths = (work[:, k, :] for k in range(9))
        if rms_gamma is not None:
            lengths_ready = s.sem("lengths_ready")
            roots_ready = s.sem("roots_ready")
        block = s.block()

        @block.vector
        def _(dve):
            for t in range(NT):
                last = dve.bn_stats(out=stats[:, t, :], in_=g.x[:, t, :])
            last.then_inc(stats_done, 1)
            dve.wait_ge(stats_done, 1)
            dve.tensor_tensor(diff, stats[:, :, 1], stats[:, :, 4], ALU.subtract).then_inc(chain, 1)
            dve.tensor_tensor(total, stats[:, :, 1], stats[:, :, 4], ALU.add).then_inc(chain, 1)
            dve.tensor_tensor(m2, stats[:, :, 2], stats[:, :, 5], ALU.add).then_inc(chain, 1)
            dve.wait_ge(chain, 3)
            dve.tensor_tensor(diff, diff, diff, ALU.mult).then_inc(chain, 1)
            dve.tensor_scalar(mean, total, 0.5, None, ALU.mult).then_inc(chain, 1)
            dve.tensor_scalar(m2, m2, 1.0 / D, 0.0 if rms_gamma is not None else LN_EPS, ALU.mult, ALU.add)\
               .then_inc(chain, 1)
            dve.wait_ge(chain, 6)
            if rms_gamma is None:
                dve.scalar_tensor_tensor(out=var, in0=diff, scalar=0.25, in1=m2, op0=ALU.mult, op1=ALU.add)\
                   .then_inc(var_ready, 1)
            else:
                dve.scalar_tensor_tensor(out=lengths, in0=diff, scalar=0.25, in1=m2, op0=ALU.mult, op1=ALU.add)\
                   .then_inc(lengths_ready, 1)
                dve.wait_ge(lengths_ready, 1)
                dve.tensor_scalar(var, lengths, LN_EPS, None, ALU.add).then_inc(var_ready, 1)
            dve.wait_ge(std_ready, 1)
            dve.reciprocal(rstd, std).then_inc(chain, 1)
            dve.wait_ge(chain, 7)
            dve.scalar_tensor_tensor(out=shift, in0=mean, scalar=-1.0, in1=rstd, op0=ALU.mult, op1=ALU.mult)\
               .then_inc(chain if rms_gamma is not None else norm_ready, 1)
            if rms_gamma is not None:
                dve.wait_ge(roots_ready, 1)
                dve.tensor_tensor(lengths, lengths, rstd, ALU.mult).then_inc(chain, 1)
                dve.wait_ge(chain, 9)
                dve.tensor_scalar(lengths, lengths, 1e-12, float(D) ** -0.5, ALU.max, ALU.mult).then_inc(chain, 1)
                dve.wait_ge(chain, 10)
                dve.reciprocal(total, lengths).then_inc(chain, 1)
                dve.wait_ge(chain, 11)
                dve.tensor_tensor(rstd, rstd, total, ALU.mult).then_inc(chain, 1)
                dve.tensor_tensor(shift, shift, total, ALU.mult).then_inc(norm_ready, 1)
                dve.wait_ge(chain, 12)
            for c in range(CHUNKS):
                dve.wait_ge(psT_free, c + 1)
                if keep_tokens:
                    dve.wait_ge(rows_kept[c % SLOTS], 16 * (c // SLOTS) + 16)
                for j in range(3):
                    t = 4 * c + j
                    last = dve.tensor_scalar(stage[:, c % SLOTS, j, :], g.x[:, t, :], mean[:, t:t + 1],
                                             rstd[:, t:t + 1], ALU.subtract, ALU.mult)
                last.then_inc(staged, 1)

        @block.tensor
        def _(pe):
            for c in range(CHUNKS):
                pe.wait_ge(staged, c + 1)
                pe.wait_ge(staged_too, c + 1)
                for j in range(4):
                    last = pe.transpose(psT[:, c % SLOTS, j * P:(j + 1) * P], stage[:, c % SLOTS, j, :], g.ident[:, :])
                last.then_inc(transposed, 1)

        @block.scalar
        def _(act):
            act.sem_inc(psT_free, SLOTS)
            act.wait_ge(var_ready, 1)
            act.activation(std, var, ACT.Sqrt).then_inc(std_ready, 1)
            if rms_gamma is not None:
                act.activation(lengths, lengths, ACT.Sqrt, scale=float(D)).then_inc(roots_ready, 1)

            def normalise(c):
                if keep_tokens:
                    act.wait_ge(rows_kept[c % SLOTS], 16 * (c // SLOTS) + 16)
                t = 4 * c + 3
                act.activation(stage[:, c % SLOTS, 3, :], g.x[:, t, :], ACT.Identity, bias=shift[:, t:t + 1],
                               scale=rstd[:, t:t + 1]).then_inc(staged_too, 1)

            act.wait_ge(norm_ready, 1)
            for c in range(SLOTS):
                normalise(c)
            for c in range(CHUNKS):
                act.wait_ge(transposed, c + 1)
                h = c % HALVES
                to = g.xnT[:, c // HALVES, HALO + h * CH:HALO + (h + 1) * CH]
                if rms_gamma is None:
                    act.activation(to, psT[:, c % SLOTS, :], ACT.Copy).then_inc(psT_free, 1)
                else:
                    act.activation(to, psT[:, c % SLOTS, :], ACT.Identity, scale=rms_gamma).then_inc(psT_free, 1)
                if c + SLOTS < CHUNKS:
                    normalise(c + SLOTS)

        if keep_tokens:
            @block.sync
            def _(sp):
                for c in range(SLOTS):
                    sp.sem_inc(rows_kept[c], 16)
                for c in range(CHUNKS):
                    sp.wait_ge(staged, c + 1)
                    sp.wait_ge(staged_too, c + 1)
                    sp.dma_start(g.token_rows[c * CH:(c + 1) * CH, :].rearrange("(j p) c -> p j c", p=P),
                                 stage[:, c % SLOTS, :, :]).then_inc(rows_kept[c % SLOTS], 16)
                for c in range(SLOTS):
                    sp.wait_ge(rows_kept[c], 16 * (CHUNKS // SLOTS + 1))


def ffn_phase(nc, g, tag):
    with Scope(nc, tag) as s:
        w, mu = g.w_ffn, g.mu
        one_minus = s.sb("one_minus", [P, 2])
        table = s.sb("table", [P, 1])
        part = s.sb("part", [P, HALVES, 2, CH])
        mixed = s.sb("mixed", [P, HALVES, 2, CH])
        relu = s.sb("relu", [P, HALVES, CH])
        gate = s.sb("gate", [P, HALVES, CH])
        prod = s.sb("prod", [P, HALVES, CH])
        ps_r = s.ps("ps_r", [P, HALVES, CH])
        ps_k = s.ps("ps_k", [P, HALVES, CH])
        ps_v = s.ps("ps_v", [P, HALVES, CH])
        ps_t = s.ps("ps_t", [P, HALVES, CH])
        consts = s.sem("consts")
        waited = s.sem("waited")
        part_ready = s.sem("part_ready")
        mix_ready = s.sem("mix_ready")
        r_ready = s.sem("r_ready")
        k_ready = s.sem("k_ready")
        gate_ready = s.sem("gate_ready")
        relu_ready = s.sem("relu_ready")
        square_ready = s.sem("square_ready")
        v_ready = s.sem("v_ready")
        prod_ready = s.sem("prod_ready")
        back = s.sem("back")
        added = s.sem("added")
        block = s.block()
        PARTS = 2 * HALVES

        def sequence(b):
            return b if isinstance(b, int) else b % B

        @block.scalar
        def _(act):
            def parts(b):
                for h in range(HALVES):
                    for k in (1, 0):
                        act.wait_ge(mix_ready, PARTS * b + 2 * h + 2 - k)
                        act.sem_inc(waited, 1)
                        act.activation(part[:, h, k, :], g.xnT[:, sequence(b), HALO + h * CH:HALO + (h + 1) * CH],
                                       ACT.Identity, scale=mu[:, k:k + 1]).then_inc(part_ready, 1)

            act.wait_ge(g.loaded, g.LOADED)
            act.activation(table[:, :], mu[:, 0:1], ACT.Sigmoid)
            parts(0)
            with act.Fori(0, B) as b:
                for h in range(HALVES):
                    act.wait_ge(k_ready, HALVES * b + h + 1)
                    act.wait_ge(v_ready, HALVES * b + h + 1)
                    act.activation(relu[:, h, :], ps_k[:, h, :], ACT.Relu).then_inc(relu_ready, 1)
                    act.wait_ge(relu_ready, HALVES * b + h + 1)
                    act.activation(relu[:, h, :], relu[:, h, :], ACT.Square).then_inc(square_ready, 1)
                parts(b + 1)
                for h in range(HALVES):
                    act.wait_ge(r_ready, HALVES * b + h + 1)
                    act.wait_ge(prod_ready, HALVES * b + h + 1)
                    act.activation(gate[:, h, :], ps_r[:, h, :], ACT.Sigmoid).then_inc(gate_ready, 1)

        @block.tensor
        def _(pe):
            def project(b):
                for h in range(HALVES):
                    pe.wait_ge(mix_ready, PARTS * b + 2 * h + 1 + PARTS)
                    if not isinstance(b, int):
                        pe.wait_ge(relu_ready, HALVES * b - HALVES + h + 1)
                    pe.matmul(ps_k[:, h, :], w[:, 1, :], mixed[:, h, 1, :], start=True, stop=True).then_inc(k_ready, 1)
                    pe.wait_ge(mix_ready, PARTS * b + 2 * h + 2 + PARTS)
                    if not isinstance(b, int):
                        pe.wait_ge(gate_ready, HALVES * b - HALVES + h + 1)
                    pe.matmul(ps_r[:, h, :], w[:, 0, :], mixed[:, h, 0, :], start=True, stop=True).then_inc(r_ready, 1)

            pe.wait_ge(g.loaded, g.LOADED)
            pe.sem_inc(v_ready, HALVES)
            project(0)
            with pe.Fori(0, B) as b:
                for h in range(HALVES):
                    pe.wait_ge(square_ready, HALVES * b + h + 1)
                    pe.wait_ge(prod_ready, HALVES * b + h + 1)
                    pe.matmul(ps_v[:, h, :], w[:, 2, :], relu[:, h, :], start=True, stop=True).then_inc(v_ready, 1)
                project(b + 1)
                for h in range(HALVES):
                    pe.wait_ge(prod_ready, HALVES * b + h + 1 + HALVES)
                    pe.wait_ge(added, HALVES * b + h + 1)
                    for j in range(4):
                        last = pe.transpose(ps_t[:, h, j * P:(j + 1) * P], prod[:, h, j * P:(j + 1) * P], g.ident[:, :])
                    last.then_inc(back, 1)

        @block.vector
        def _(dve):
            def mix(b):
                for h in range(HALVES):
                    for k in (1, 0):
                        dve.wait_ge(part_ready, PARTS * b + 2 * h + 2 - k)
                        if not isinstance(b, int):
                            dve.wait_ge((r_ready, k_ready)[k], HALVES * b - HALVES + h + 1)
                        lo = HALO - 1 + h * CH
                        dve.scalar_tensor_tensor(out=mixed[:, h, k, :], in0=g.xnT[:, sequence(b), lo:lo + CH],
                                                 scalar=one_minus[:, k:k + 1], in1=part[:, h, k, :],
                                                 op0=ALU.mult, op1=ALU.add).then_inc(mix_ready, 1)

            dve.wait_ge(g.loaded, g.LOADED)
            dve.tensor_scalar(one_minus[:, :], mu[:, :], -1.0, 1.0, ALU.mult, ALU.add).then_inc(consts, 1)
            dve.wait_ge(consts, 1)
            dve.sem_inc(mix_ready, PARTS)
            dve.sem_inc(prod_ready, HALVES)
            dve.sem_inc(added, HALVES)
            mix(0)
            with dve.Fori(0, B) as b:
                mix(b + 1)
                for h in range(HALVES):
                    dve.wait_ge(gate_ready, HALVES * b + h + 1)
                    dve.wait_ge(v_ready, HALVES * b + h + 1 + HALVES)
                    dve.tensor_tensor(prod[:, h, :], gate[:, h, :], ps_v[:, h, :], ALU.mult).then_inc(prod_ready, 1)
                for h in range(HALVES):
                    dve.wait_ge(back, HALVES * b + h + 1)
                    x = g.x[:, bass.ds(b * TB + h * 4, 4), :]
                    dve.scalar_tensor_tensor(out=x, in0=ps_t[:, h, :].rearrange("p (j c) -> p j c", j=4), scalar=0.5,
                                             in1=x, op0=ALU.mult, op1=ALU.add).then_inc(added, 1)


def mamba_phase(nc, g, A):
    with Scope(nc, "mamba") as s_:
        xc = s_.sb("xc", [P, 2, NB, L])
        zs = s_.sb("zs", [P, 2, NB, L])
        delta = s_.sb("delta", [P, 2, NB, L])
        u = s_.sb("u", [P, 2, NB, L])
        bc = s_.sb("bc", [3 * BC, 2, L], BF16)
        xn = s_.sb("xn", [P, 2, HALO + L], F32R)
        silu = s_.sb("silu", [P, NB, CH])
        low = s_.sb("low", [R, CH])
        bc_hi = s_.sb("bc_hi", [3 * BC, CH], BF16)
        bc_rest = s_.sb("bc_rest", [3 * BC, CH])
        bc_mid = s_.sb("bc_mid", [3 * BC, CH], BF16)
        v = s_.sb("v", [P, NB, CH])
        ex = s_.sb("ex", [P, NB, CH])
        ln = s_.sb("ln", [P, NB, CH])
        low_bits = s_.sb("low_bits", [P, NB, CH])
        decay = s_.sb("decay", [P, 2, NB, L])
        drive = s_.sb("drive", [P, NB, L])
        state = s_.sb("state", [P, NB, L])
        c_all = s_.sb("c_all", [P, 2, L])
        read = g.taps_in
        pick = s_.sb("pick", [3 * BC, BC], BF16)
        taps = [s_.sb(f"taps{part}", [P, NB, 2 * KW, P], F32R) for part in ("_hi", "_lo")]
        gates = s_.sb("gates", [P, 2])
        gsum = s_.sb("gsum", [P, 1])
        neg_a = s_.sb("neg_a", [P, NB, NS])
        bank = s_.ps("bank", [P, 8, CH])
        TOP = 2

        taps_made = s_.sem("taps_made")
        taps_hi = s_.sem("taps_hi")
        x_hi = s_.sem("x_hi")
        x_lo = s_.sem("x_lo")
        waited = s_.sem("waited")
        gate_exp = s_.sem("gate_exp")
        consts = s_.sem("consts")
        neg_a_ready = s_.sem("neg_a_ready")
        taps_lo = s_.sem("taps_lo")
        pick_steps = s_.sem("pick_steps")
        conv_ready = s_.sem("conv_ready")
        silu_ready = s_.sem("silu_ready")
        xc_part = s_.sem("xc_part")
        xc_ready = s_.sem("xc_ready")
        z_ready = s_.sem("z_ready")
        zs_ready = s_.sem("zs_ready")
        low_ready = s_.sem("low_ready")
        low_copied = s_.sem("low_copied")
        bc_split = s_.sem("bc_split")
        bc_rest_ready = s_.sem("bc_rest_ready")
        bc_ready = s_.sem("bc_ready")
        dt_ready = s_.sem("dt_ready")
        v_ready = s_.sem("v_ready")
        mag_ready = s_.sem("mag_ready")
        ex_ready = s_.sem("ex_ready")
        ln_ready = s_.sem("ln_ready")
        delta_steps = s_.sem("delta_steps")
        delta_ready = s_.sem("delta_ready")
        u_ready = s_.sem("u_ready")
        b_spread = s_.sem("b_spread")
        c_spread = s_.sem("c_spread")
        c_copied = s_.sem("c_copied")
        decay_ready = s_.sem("decay_ready")
        driven = s_.sem("driven")
        scanned = s_.sem("scanned")
        read_ready = s_.sem("read_ready")
        summed = s_.sem("summed")
        y_part = s_.sem("y_part")
        y_ready = s_.sem("y_ready")
        projected = s_.sem("projected")
        added = s_.sem("added")
        block = s_.block()

        C00, C01, Z0, LB0, DT0 = ("C", 0, 0), ("C", 0, 1), ("Z", 0, 0), ("LB", 0, 0), ("DT", 0, 0)
        C10, C11, Z1, LB1, DT1 = ("C", 1, 0), ("C", 1, 1), ("Z", 1, 0), ("LB", 1, 0), ("DT", 1, 0)
        jobs = {0: C00, 1: C01, 3: Z0, 4: LB0, 6: DT0, 7: C10, 8: C11, 9: Z1, 10: LB1, 11: DT1}
        OUT = 2
        SPLIT = 12
        AHEAD = 4
        first_jobs = [(C00, 0), (C01, 4), (C10, 2), (LB0, 6), (C11, 0), (DT0, 4), (LB1, 6), (DT1, 2), (Z0, 0), (Z1, 4)]

        def cols(h):
            return slice(h * CH, (h + 1) * CH)

        def flat(two_banks):
            return two_banks.rearrange("p k t -> p (k t)")

        def first_of_all(b):
            return isinstance(b, int) and b == 0

        def there(b):
            return not isinstance(b, int) or b < B

        def run(eng, first, prepare, state_step):
            first()
            prepare()
            for n in range(AHEAD):
                state_step(0, 0, n, False)

            def both(turn):
                for k in range(2):
                    for n in range(AHEAD, NS + AHEAD):
                        state_step(2 * turn + k + n // NS, (k + n // NS) % 2, n % NS, True)

            with eng.Fori(0, B // 2 - 1) as turn:
                both(turn)
            both(B // 2 - 1)

        @block.gpsimd
        def _(pool):
            def make_u(b, p, h):
                pool.wait_ge(xc_ready, 4 * b + 2 * h + 4)
                pool.wait_ge(delta_ready, 2 * b + h + 2)
                if not first_of_all(b):
                    pool.wait_ge(projected, b)
                pool.tensor_tensor(u[:, p, :, cols(h)], delta[:, p, :, cols(h)], xc[:, p, :, cols(h)], ALU.mult)\
                    .then_inc(u_ready, 1)

            def first():
                pool.memset(pick[:, :], 0.0).then_inc(pick_steps, 1)
                for part in range(3):
                    pool.wait_ge(pick_steps, 1 + part)
                    pool.affine_select(out=pick[:, :], in_=pick[:, :], compare_op=ALU.not_equal, fill=1.0,
                                       base=-BC * part, pattern=[[-1, BC]], channel_multiplier=1)\
                        .then_inc(pick_steps, 1)
                pool.sem_inc(read_ready, 2 * NB)

            def prepare():
                for h in range(HALVES):
                    make_u(0, 0, h)

            def state_step(b, p, n, prev):
                N = NS * b + n
                for blk in range(NB if there(b) else 0):
                    pool.wait_ge(c_copied, N + 1)
                    pool.wait_ge(scanned, NB * N + blk + 1 + NB)
                    pool.wait_ge(summed, NB * N + blk + 1)
                    pool.tensor_tensor(read[:, blk, :], state[:, blk, :], c_all[:, n % 2, :], ALU.mult)\
                        .then_inc(read_ready, 1)
                for at, (kind, h, _blk) in jobs.items():
                    if kind == "DT" and at + 2 == n and there(b + 1):
                        make_u(b + 1, 1 - p, h)

            run(pool, first, prepare, state_step)

        @block.scalar
        def _(act):
            def first():
                act.wait_ge(g.loaded, g.LOADED)
                split(0)
                for blk in range(NB):
                    act.wait_ge(taps_made, blk + 1)
                    act.activation(taps[0][:, blk, :, :], decay[:, 0, blk, :].rearrange("p (k c) -> p k c", c=P),
                                   ACT.Copy).then_inc(taps_hi, 1)
                act.activation(gates[:, :], g.gates[:, :], ACT.Exp, accum_out=gsum[:, :]).then_inc(gate_exp, 1)
                act.activation(neg_a[:, :, :], g.a_log[:, :, :], ACT.Exp).then_inc(gate_exp, 1)

            def split(b):
                if not first_of_all(b):
                    act.wait_ge(conv_ready, 8 * b)
                    act.sem_inc(waited, 1)
                act.activation(xn[:, 0, :], g.xnT[:, b % B, :], ACT.Copy).then_inc(x_hi, 1)

            def job(b, p, kind, h, blk, at=0):
                half = 2 * b + h
                if kind == "C":
                    act.wait_ge(xc_ready, 2 * half + blk + 1)
                    if not first_of_all(b):
                        act.wait_ge(y_part, 2 * b)
                    for k, to in enumerate((xc[:, p, blk, cols(h)], silu[:, blk, :])):
                        act.wait_ge(conv_ready, 4 * half + 2 * blk + k + 1)
                        last = act.activation(to, bank[:, at + k, :], ACT.Silu, bias=g.conv_b[:, blk, k:k + 1])
                    last.then_inc(silu_ready, 1)
                elif kind == "Z":
                    act.wait_ge(z_ready, half + 1)
                    if not first_of_all(b):
                        act.wait_ge(y_ready, 2 * b)
                    act.activation(zs[:, p, :, cols(h)], bank[:, at:at + 2, :], ACT.Silu).then_inc(zs_ready, 1)
                elif kind == "LB":
                    act.wait_ge(low_ready, half + 1)
                    act.activation(low[:, :], bank[0:R, at, :], ACT.Copy).then_inc(low_copied, 1)
                    act.activation(bc_hi[:, :], bank[0:3 * BC, at + 1, :], ACT.Copy).then_inc(bc_split, 1)
                    act.activation(bc[0:BC, p, cols(h)], bank[0:BC, at + 1, :], ACT.Copy).then_inc(bc_split, 1)
                elif kind == "LB2":
                    act.wait_ge(bc_rest_ready, half + 1)
                    act.wait_ge(bc_ready, half + 1)
                    act.activation(bc_mid[2 * BC:3 * BC, :], bc_rest[2 * BC:3 * BC, :], ACT.Copy).then_inc(bc_split, 1)
                    act.activation(bc[BC:2 * BC, p, cols(h)], bc_rest[BC:2 * BC, :], ACT.Copy).then_inc(bc_split, 1)
                else:
                    act.wait_ge(dt_ready, half + 1)
                    act.wait_ge(delta_ready, half + 1)
                    for k in range(NB):
                        last = act.activation(v[:, k, :], bank[:, at + k, :], ACT.Identity, bias=g.b_dt[:, k:k + 1])
                    last.then_inc(v_ready, 1)
                    act.wait_ge(v_ready, half + 1)
                    act.activation(ex[:, :, :], v[:, :, :], ACT.Abs).then_inc(mag_ready, 1)
                    act.wait_ge(mag_ready, half + 1)
                    act.activation(ex[:, :, :], ex[:, :, :], ACT.Exp, scale=-1.0).then_inc(ex_ready, 1)
                    act.wait_ge(ex_ready, half + 1)
                    act.activation(ln[:, :, :], ex[:, :, :], ACT.Ln, bias=1.0).then_inc(ln_ready, 1)

            def decay_and_c(b, p, n):
                N = NS * b + n
                if n == 0:
                    act.wait_ge(delta_ready, 2 * b + 2 + 1)
                for blk in range(NB):
                    if not (isinstance(b, int) and N < 2):
                        act.wait_ge(scanned, NB * N + blk + 1 - NB)
                    act.activation(decay[:, n % 2, blk, :], delta[:, p, blk, :], ACT.Exp,
                                   scale=g.neg_a[:, blk, n:n + 1]).then_inc(decay_ready, 1)
                act.wait_ge(c_spread, N + 1)
                act.wait_ge(read_ready, NB * N + 2)
                act.activation(c_all[:, n % 2, :], flat(bank[:, TOP:TOP + 2, :]), ACT.Copy).then_inc(c_copied, 1)

            def prepare():
                for (kind, h, blk), at in first_jobs:
                    job(0, 0, kind, h, blk, at)
                    if kind == "LB":
                        job(0, 0, "LB2", h, blk)
                act.wait_ge(neg_a_ready, 1)
                decay_and_c(0, 0, 0)
                split(1)

            def state_step(b, p, n, prev):
                if there(b + (n + 1) // NS):
                    decay_and_c(b + (n + 1) // NS, (p + (n + 1) // NS) % 2, (n + 1) % NS)
                if n == SPLIT and there(b + 2):
                    split(b + 2)
                if not there(b + 1):
                    return
                for at, (kind, h, blk) in jobs.items():
                    if at + 1 == n:
                        job(b + 1, 1 - p, kind, h, blk)
                    if kind == "LB" and at + 2 == n:
                        job(b + 1, 1 - p, "LB2", h, blk)

            run(act, first, prepare, state_step)

        @block.vector
        def _(dve):
            def rest(b):
                dve.wait_ge(x_hi, b + 1)
                dve.tensor_tensor(xn[:, 1, :], g.xnT[:, b % B, :], xn[:, 0, :].bitcast(F32),
                                  ALU.subtract).then_inc(x_lo, 1)

            def first():
                dve.wait_ge(g.loaded, g.LOADED)
                for blk in range(NB):
                    w = g.w_in[:, None, blk * P:(blk + 1) * P].to_broadcast([P, 2 * KW, P])
                    dve.tensor_tensor(decay[:, 0, blk, :].rearrange("p (k c) -> p k c", c=P),
                                      g.taps_in[:, blk, :].rearrange("p (k c) -> p k c", c=P), w, ALU.mult)\
                        .then_inc(taps_made, 1)
                for blk in range(NB):
                    dve.wait_ge(taps_hi, blk + 1)
                    dve.tensor_tensor(taps[1][:, blk, :, :], decay[:, 0, blk, :].rearrange("p (k c) -> p k c", c=P),
                                      taps[0][:, blk, :, :].bitcast(F32), ALU.subtract).then_inc(taps_lo, 1)
                    if blk == 0:
                        rest(0)
                dve.wait_ge(gate_exp, 2)
                dve.reciprocal(gsum[:, :], gsum[:, :]).then_inc(consts, 1)
                dve.tensor_scalar(g.neg_a[:, :, :], neg_a[:, :, :], -1.0, None, ALU.mult).then_inc(neg_a_ready, 1)
                dve.wait_ge(consts, 1)
                dve.tensor_scalar(gates[:, :], gates[:, :], gsum[:, :], None, ALU.mult).then_inc(consts, 1)
                dve.wait_ge(consts, 2)
                dve.sem_inc(scanned, NB)
                dve.sem_inc(xc_ready, 2)
                dve.sem_inc(delta_ready, 1)
                dve.sem_inc(bc_ready, 1)
                dve.sem_inc(y_part, NB)
                dve.sem_inc(y_ready, 2 * NB)

            def job(b, p, kind, h, blk, at=0):
                half = 2 * b + h
                if kind == "C":
                    dve.wait_ge(silu_ready, 2 * half + blk + 1)
                    dve.tensor_scalar(xc[:, p, blk, cols(h)], xc[:, p, blk, cols(h)], gates[:, 0:1], None, ALU.mult)\
                        .then_inc(xc_part, 1)
                    dve.wait_ge(xc_part, 2 * half + blk + 1)
                    dve.scalar_tensor_tensor(out=xc[:, p, blk, cols(h)], in0=silu[:, blk, :], scalar=gates[:, 1:2],
                                             in1=xc[:, p, blk, cols(h)], op0=ALU.mult, op1=ALU.add).then_inc(xc_ready, 1)
                elif kind == "LB":
                    dve.wait_ge(bc_split, 4 * half + 1)
                    dve.tensor_tensor(bc_rest[BC:2 * BC, :], bank[BC:2 * BC, at + 1, :], bc_hi[BC:2 * BC, :], ALU.subtract)
                    dve.tensor_tensor(bc_rest[2 * BC:3 * BC, :], bank[2 * BC:3 * BC, at + 1, :], bc_hi[2 * BC:3 * BC, :],
                                      ALU.subtract).then_inc(bc_rest_ready, 1)
                elif kind == "LB2":
                    dve.wait_ge(bc_split, 4 * half + 4)
                    dve.tensor_tensor(bc[2 * BC:3 * BC, p, cols(h)], bc_rest[2 * BC:3 * BC, :],
                                      bc_mid[2 * BC:3 * BC, :], ALU.subtract).then_inc(bc_ready, 1)
                elif kind == "DT":
                    c = 3 * half
                    dve.wait_ge(ex_ready, half + 1)
                    dve.tensor_scalar(low_bits[:, :, :], ex[:, :, :], 1.0, -1.0, ALU.add, ALU.add).then_inc(delta_steps, 1)
                    dve.wait_ge(delta_steps, c + 1)
                    dve.tensor_tensor(low_bits[:, :, :], ex[:, :, :], low_bits[:, :, :], ALU.subtract)\
                        .then_inc(delta_steps, 1)
                    dve.wait_ge(ln_ready, half + 1)
                    dve.wait_ge(delta_steps, c + 2)
                    dve.tensor_tensor(low_bits[:, :, :], ln[:, :, :], low_bits[:, :, :], ALU.add).then_inc(delta_steps, 1)
                    dve.wait_ge(delta_steps, c + 3)
                    dve.scalar_tensor_tensor(out=delta[:, p, :, cols(h)], in0=v[:, :, :], scalar=0.0,
                                             in1=low_bits[:, :, :], op0=ALU.max, op1=ALU.add).then_inc(delta_ready, 1)

            def prepare():
                for (kind, h, blk), at in first_jobs:
                    job(0, 0, kind, h, blk, at)
                    if kind == "LB":
                        job(0, 0, "LB2", h, blk)
                rest(1)

            def state_step(b, p, n, prev):
                N = NS * b + n
                blocks = range(NB if there(b) else 0)
                if n == 0 and there(b):
                    dve.wait_ge(u_ready, 2 * b + 2)
                for blk in blocks:
                    dve.wait_ge(b_spread, N + 1)
                    dve.wait_ge(scanned, NB * N + blk + 1)
                    dve.tensor_tensor(drive[:, blk, :], u[:, p, blk, :], flat(bank[:, TOP:TOP + 2, :]), ALU.mult)\
                        .then_inc(driven, 1)
                for blk in blocks:
                    dve.wait_ge(decay_ready, NB * N + blk + 1)
                    dve.wait_ge(driven, NB * N + blk + 1)
                    dve.wait_ge(read_ready, NB * N + blk + 3)
                    dve.tensor_tensor_scan(state[:, blk, :], decay[:, n % 2, blk, :], drive[:, blk, :], 0.0,
                                           ALU.mult, ALU.add).then_inc(scanned, 1)
                if prev and n == 0:
                    q = 1 - p
                    dve.wait_ge(summed, NB * N + NB)
                    for blk in range(NB):
                        dve.scalar_tensor_tensor(out=u[:, q, blk, :], in0=xc[:, q, blk, :],
                                                 scalar=g.d_param[:, blk:blk + 1],
                                                 in1=flat(bank[:, 4 + 2 * blk:6 + 2 * blk, :]),
                                                 op0=ALU.mult, op1=ALU.add).then_inc(y_part, 1)
                if prev and n == 1:
                    for blk in range(NB):
                        dve.wait_ge(y_part, NB * b + blk + 1)
                        dve.wait_ge(zs_ready, 2 * b)
                        dve.tensor_tensor(u[:, 1 - p, blk, :], u[:, 1 - p, blk, :], zs[:, 1 - p, blk, :], ALU.mult)\
                            .then_inc(y_ready, 1)
                for at, (kind, h, blk) in jobs.items():
                    if not there(b + 1):
                        break
                    if at + (1 if kind == "LB" else 2) == n:
                        job(b + 1, 1 - p, kind, h, blk)
                    if kind == "LB" and at + 2 == n:
                        job(b + 1, 1 - p, "LB2", h, blk)
                if n == SPLIT and there(b + 2):
                    rest(b + 2)
                if prev and n == OUT:
                    dve.wait_ge(projected, b + 1)
                    xb = g.x[:, bass.ds((b - 1) * TB, TB), :]
                    dve.tensor_tensor(xb, xb, bank[:, 0:2, :].rearrange("p k (j c) -> p (k j) c", c=D), ALU.add)\
                        .then_inc(added, 1)

            run(dve, first, prepare, state_step)

        @block.tensor
        def _(pe):
            def first():
                pe.wait_ge(pick_steps, 4)
                pe.sem_inc(summed, NB)
                pe.sem_inc(projected, 1)

            def banks_free(b, kind, h, blk, prev):
                half = 2 * b + h
                if kind == "C" and blk == 0 and h == 0 and isinstance(b, int) and b == 1:
                    pe.wait_ge(zs_ready, 2)
                elif kind == "C" and blk == 0:
                    pe.wait_ge(v_ready, half)
                elif kind == "C":
                    pe.wait_ge(silu_ready, 2 * half + 1)
                elif kind == "Z":
                    pe.wait_ge(silu_ready, 2 * half + 2)
                    if prev and h == 0:
                        pe.wait_ge(added, b - 1)
                elif kind == "LB":
                    pe.wait_ge(zs_ready, half + 1)
                else:
                    pe.wait_ge(bc_rest_ready, half + 1)
                    pe.wait_ge(bc_split, 4 * half + 2)

            def job(b, p, kind, h, blk, at=0):
                half = 2 * b + h
                seq = b % B
                if kind == "C":
                    if h == 0 and blk == 0:
                        pe.wait_ge(x_lo, b + 1)
                    for k in range(2):
                        for tap in range(KW):
                            lo = HALO + h * CH - (k + 1) * (KW - 1 - tap)
                            for m, (w, x) in enumerate(((taps[0], 0), (taps[0], 1), (taps[1], 0))):
                                last = pe.matmul(bank[:, at + k, :], w[:, blk, k * KW + tap, :], xn[:, x, lo:lo + CH],
                                                 start=(tap == 0 and m == 0), stop=(tap == KW - 1 and m == 2))
                        last.then_inc(conv_ready, 1)
                elif kind == "Z":
                    for k in range(NB):
                        last = pe.matmul(bank[:, at + k, :], g.w_in[:, (NB + k) * P:(NB + k + 1) * P],
                                         g.xnT[:, seq, HALO + h * CH:HALO + (h + 1) * CH], start=True, stop=True)
                    last.then_inc(z_ready, 1)
                elif kind == "LB":
                    pe.wait_ge(xc_ready, 2 * half + 4)
                    for k in range(NB):
                        pe.matmul(bank[0:R, at, :], g.w_x[:, k, 0:R], xc[:, p, k, cols(h)],
                                  start=(k == 0), stop=(k == NB - 1))
                    for k in range(NB):
                        last = pe.matmul(bank[0:3 * BC, at + 1, :], g.w_x[:, k, R:R + 3 * BC], xc[:, p, k, cols(h)],
                                         start=(k == 0), stop=(k == NB - 1))
                    last.then_inc(low_ready, 1)
                else:
                    pe.wait_ge(low_copied, half + 1)
                    for k in range(NB):
                        last = pe.matmul(bank[:, at + k, :], g.w_dt[:, k * P:(k + 1) * P], low[:, :],
                                         start=True, stop=True)
                    last.then_inc(dt_ready, 1)

            def spread(p, row, to):
                for h in range(HALVES):
                    last = pe.matmul(bank[:, TOP + h, :], pick[:, row:row + 1].to_broadcast([3 * BC, P]),
                                     bc[:, p, cols(h)], start=True, stop=True)
                last.then_inc(to, 1)

            def spread_c(b, p, n):
                if n == 0:
                    pe.wait_ge(bc_ready, 2 * b + 2 + 1)
                spread(p, NS + n, c_spread)

            def spread_b(b, p, n):
                pe.wait_ge(c_copied, NS * b + n + 1)
                spread(p, n, b_spread)

            def prepare():
                taken = {C11: (silu_ready, 1), DT0: (silu_ready, 2), LB1: (bc_rest_ready, 1), DT1: (silu_ready, 3),
                         Z0: (silu_ready, 4), Z1: (v_ready, 1)}
                for which, at in first_jobs:
                    if which in (C00, C01):
                        pe.wait_ge(taps_lo, 1 + which[2])
                    if which in taken:
                        pe.wait_ge(*taken[which])
                    if which == LB1:
                        pe.wait_ge(bc_split, 2)
                    job(0, 0, *which, at=at)
                pe.wait_ge(v_ready, 2)
                spread_c(0, 0, 0)
                spread_b(0, 0, 0)

            def state_step(b, p, n, prev):
                N = NS * b + n
                ahead = (b + (n + 1) // NS, (p + (n + 1) // NS) % 2, (n + 1) % NS)
                if there(ahead[0]):
                    pe.wait_ge(driven, NB * N + NB)
                    spread_c(*ahead)
                m = (n - 1) % NS
                if m == 0 and prev and there(b):
                    pe.wait_ge(y_part, NB * b + NB)
                for blk in range(NB):
                    if (prev or n > 0) and (there(b) or n == 0):
                        pe.wait_ge(read_ready, NB * N + blk + 3)
                        for h in range(HALVES):
                            last = pe.matmul(bank[:, 4 + 2 * blk + h, :], g.ident[:, :], read[:, blk, cols(h)],
                                             start=(m == 0), stop=(m == NS - 1))
                        last.then_inc(summed, 1)
                    if blk == 0 and there(ahead[0]):
                        spread_b(*ahead)
                if n in jobs and there(b + 1):
                    banks_free(b + 1, *jobs[n], prev)
                    job(b + 1, 1 - p, *jobs[n])
                if prev and n == OUT:
                    pe.wait_ge(y_ready, NB * b + 2 * NB)
                    if there(b + 1):
                        pe.wait_ge(silu_ready, 4 * (b + 1) + 2)
                    else:
                        pe.wait_ge(v_ready, 2 * B)
                        pe.wait_ge(added, b - 1)
                    for t in range(TB):
                        for blk in range(NB):
                            last = pe.matmul(bank[:, t // 4, (t % 4) * P:(t % 4 + 1) * P],
                                             u[:, 1 - p, blk, t * P:(t + 1) * P],
                                             g.w_out[:, blk, :], start=(blk == 0), stop=(blk == NB - 1))
                    last.then_inc(projected, 1)

            run(pe, first, prepare, state_step)


def load_experts_phase(nc, g, A):
    with Scope(nc, "fetch") as s:
        block = s.block()

        @block.sync
        def _(sp):
            for dst, name in g.late_weights:
                sp.dma_start(dst, A[name]).then_inc(g.late_loaded, 16)


def moe_route_phase(nc, g, tag):
    with Scope(nc, tag) as s:
        def field(name):
            return s.sb(name, [P, NT, E])

        def column(name):
            return s.sb(name, [P, NT])

        prob, score, equal = field("prob"), field("score"), field("equal")
        first, second, both = field("first"), field("second"), field("both")
        total, until, place = field("total"), field("until"), field("place")
        top, denom, best, p1, p2 = (column(x) for x in ("top", "denom", "best", "p1", "p2"))
        both16 = s.sb("both16", [P, NT * E], BF16)
        rev = s.sb("rev", [P, E])
        ones_col = s.sb("ones_col", [P, NT])
        before = s.sb("before", [P, P], BF16)
        everyone = s.sb("everyone", [P, P], BF16)
        count_i = s.sb("count_i", [P, E], I32)
        tiles = s.sb("tiles", [P, E])
        tiles_until = s.sb("tiles_until", [P, E])
        base = s.sb("base", [P, E])
        row_f = s.sb("row_f", [P, 2, NT])
        row_i = s.sb("row_i", [P, 2 * NT], I32)
        part_i = s.sb("part_i", [P, 2, 2 * NT], I32)
        row_lo = s.sb("row_lo", [P, 2 * NT])
        row_hi = s.sb("row_hi", [P, 2 * NT])
        lane = s.sb("lane", [P, P])
        tile_of = s.sb("tile_of", [P, MT])
        choice_tile = s.sb("choice_tile", [P, 2 * NT])
        choice_lane = s.sb("choice_lane", [P, 1])
        in_lane = s.sb("in_lane", [P, 2 * NT, P], BF16)
        in_tile = s.sb("in_tile", [P, 2 * NT, MT], BF16)
        tile_part = s.sb("tile_part", [P, 2 * NT, MT], BF16)
        lane_part = s.sb("lane_part", [P, 2 * NT, MT], BF16)
        in_tile_ready = s.sem("in_tile_ready")
        lane_part_ready = s.sem("lane_part_ready")
        tile_part_ready = s.sem("tile_part_ready")
        found = s.sb("found", [P, MT])
        none = s.sb("none", [P, MT])
        source_f = s.sb("source_f", [P, MT])
        source_i = s.sb("source_i", [P, MT], I32)
        ps_list = s.ps("ps_list", [P, CH])
        lists_ready = s.sem("lists_ready")
        list_found = s.sem("list_found")
        tile_no = s.sb("tile_no", [1, MT, E])
        owner = s.sb("owner", [1, MT])
        ps_logit = s.ps("ps_logit", [P, CH])
        ps_before = s.ps("ps_before", [P, CH])
        ps_total = s.ps("ps_total", [P, CH])
        made = s.sem("made")
        before_zero = s.sem("before_zero")
        logits_ready = s.sem("logits_ready")
        shifted = s.sem("shifted")
        exp_ready = s.sem("exp_ready")
        chain = s.sem("chain")
        choice_ready = s.sem("choice_ready")
        ranks_ready = s.sem("ranks_ready")
        rows_ready = s.sem("rows_ready")
        block = s.block()
        logits = ps_logit[:, 0:NT * E].rearrange("p (t e) -> p t e", e=E)

        GROUP = 16

        def spread(col):
            return col[:, :, None].to_broadcast([P, NT, E])

        @block.gpsimd
        def _(pool):
            pool.iota(rev[:, :], [[-1, E]], base=E, channel_multiplier=0,
                      allow_small_or_imprecise_dtypes=True).then_inc(made, 1)
            pool.iota(tile_no[:, :, :], [[1, MT], [0, E]], base=0, channel_multiplier=0,
                      allow_small_or_imprecise_dtypes=True).then_inc(made, 1)
            pool.iota(lane[:, :], [[1, P]], base=0, channel_multiplier=0,
                      allow_small_or_imprecise_dtypes=True).then_inc(made, 1)
            pool.iota(tile_of[:, :], [[1, MT]], base=0, channel_multiplier=0,
                      allow_small_or_imprecise_dtypes=True).then_inc(made, 1)
            pool.iota(choice_tile[:, :], [[P, 2 * NT]], base=0, channel_multiplier=0,
                      allow_small_or_imprecise_dtypes=True).then_inc(made, 1)
            pool.iota(choice_lane[:, :], [[0, 1]], base=1, channel_multiplier=1,
                      allow_small_or_imprecise_dtypes=True).then_inc(made, 1)
            pool.memset(ones_col[:, :], 1.0).then_inc(made, 1)
            pool.memset(everyone[:, :], 1.0).then_inc(made, 1)
            pool.memset(before[:, :], 1.0).then_inc(before_zero, 1)
            pool.wait_ge(before_zero, 1)
            pool.affine_select(out=before[:, :], in_=before[:, :], compare_op=ALU.is_gt, fill=0.0,
                               base=0, pattern=[[1, P]], channel_multiplier=-1).then_inc(made, 1)
            pool.wait_ge(made, 9)
            for T in range(0, 2 * NT, GROUP):
                some = slice(T, T + GROUP)
                pool.wait_ge(in_tile_ready, T // GROUP + 1)
                pool.tensor_tensor(tile_part[:, some, :], in_tile[:, some, :],
                                   choice_tile[:, some, None].to_broadcast([P, GROUP, MT]), ALU.mult)\
                    .then_inc(tile_part_ready, 1)

        @block.tensor
        def _(pe):
            pe.wait_ge(g.late_loaded, g.LATE_LOADED)
            for t in range(NT):
                lo = HALO + (t % TB) * P
                last = pe.matmul(ps_logit[:, t * E:(t + 1) * E], g.xnT[:, t // TB, lo:lo + P], g.router[:, :],
                                 start=True, stop=True)
            last.then_inc(logits_ready, 1)
            pe.wait_ge(choice_ready, 1)
            pe.wait_ge(made, 9)
            pe.matmul(ps_before[:, 0:NT * E], before[:, :], both16[:, :], start=True, stop=True)
            pe.matmul(ps_total[:, 0:NT * E], everyone[:, :], both16[:, :], start=True, stop=True)\
                .then_inc(ranks_ready, 1)
            for T in range(2 * NT):
                if T % GROUP == 0:
                    pe.wait_ge(lists_ready, T // GROUP + 1)
                    pe.wait_ge(lane_part_ready, T // GROUP + 1)
                    pe.wait_ge(tile_part_ready, T // GROUP + 1)
                pe.matmul(ps_list[:, 0:MT], in_lane[:, T, :], tile_part[:, T, :], start=(T == 0), stop=False)
                last = pe.matmul(ps_list[:, 0:MT], in_lane[:, T, :], lane_part[:, T, :], start=False,
                                 stop=(T == 2 * NT - 1))
            last.then_inc(list_found, 1)

        @block.scalar
        def _(act):
            act.wait_ge(shifted, 1)
            act.activation(score[:, :, :], prob[:, :, :], ACT.Exp).then_inc(exp_ready, 1)
            for T in range(0, 2 * NT, GROUP):
                act.wait_ge(in_tile_ready, T // GROUP + 1)
                act.activation(lane_part[:, T:T + GROUP, :], in_tile[:, T:T + GROUP, :], ACT.Copy,
                               scale=choice_lane[:, :]).then_inc(lane_part_ready, 1)

        @block.vector
        def _(dve):
            done = [0]

            def then(instruction):
                done[0] += 1
                instruction.then_inc(chain, 1)
                dve.wait_ge(chain, done[0])

            dve.wait_ge(made, 9)
            dve.wait_ge(logits_ready, 1)
            then(dve.tensor_reduce(top[:, :], logits, AX.X, ALU.max))
            dve.tensor_tensor(prob[:, :, :], logits, spread(top), ALU.subtract).then_inc(shifted, 1)
            dve.wait_ge(exp_ready, 1)
            then(dve.tensor_reduce(denom[:, :], score[:, :, :], AX.X, ALU.add))
            then(dve.reciprocal(denom[:, :], denom[:, :]))
            then(dve.tensor_tensor(prob[:, :, :], score[:, :, :], spread(denom), ALU.mult))
            for chosen, p in ((first, p1), (second, p2)):
                then(dve.tensor_reduce(p[:, :], prob[:, :, :], AX.X, ALU.max))
                then(dve.tensor_tensor(equal[:, :, :], prob[:, :, :], spread(p), ALU.is_equal))
                then(dve.tensor_tensor(score[:, :, :], equal[:, :, :], rev[:, None, :].to_broadcast([P, NT, E]),
                                       ALU.mult))
                then(dve.tensor_reduce(best[:, :], score[:, :, :], AX.X, ALU.max))
                then(dve.tensor_tensor(chosen[:, :, :], score[:, :, :], spread(best), ALU.is_equal))
                if chosen is first:
                    then(dve.scalar_tensor_tensor(out=prob[:, :, :], in0=chosen[:, :, :], scalar=-2.0,
                                                  in1=prob[:, :, :], op0=ALU.mult, op1=ALU.add))
            then(dve.tensor_tensor(both[:, :, :], first[:, :, :], second[:, :, :], ALU.add))
            dve.tensor_copy(both16[:, :], both[:, :, :].rearrange("p t e -> p (t e)")).then_inc(choice_ready, 1)
            then(dve.tensor_tensor(denom[:, :], p1[:, :], p2[:, :], ALU.add))
            then(dve.tensor_scalar(denom[:, :], denom[:, :], 1e-9, None, ALU.add))
            then(dve.reciprocal(denom[:, :], denom[:, :]))
            then(dve.tensor_scalar(denom[:, :], denom[:, :], 0.5, None, ALU.mult))
            dve.tensor_tensor(g.weight[:, 0, :], p1[:, :], denom[:, :], ALU.mult).then_inc(rows_ready, 1)
            dve.tensor_tensor(g.weight[:, 1, :], p2[:, :], denom[:, :], ALU.mult).then_inc(rows_ready, 1)
            dve.wait_ge(ranks_ready, 1)
            then(dve.tensor_copy(total[:, :, :], ps_total[:, 0:NT * E].rearrange("p (t e) -> p t e", e=E)))
            for e in range(E):
                dve.tensor_tensor_scan(until[:, :, e], ones_col[:, :], total[:, :, e], 0.0, ALU.mult, ALU.add)\
                    .then_inc(chain, 1)
            done[0] += E
            dve.wait_ge(chain, done[0])
            then(dve.tensor_scalar(tiles[:, :], until[:, NT - 1, :], float(P - 1), None, ALU.add))
            then(dve.tensor_copy(count_i[:, :], tiles[:, :]))
            then(dve.tensor_scalar(count_i[:, :], count_i[:, :], 7, None, ALU.arith_shift_right))
            then(dve.tensor_copy(tiles[:, :], count_i[:, :]))
            then(dve.tensor_tensor_scan(tiles_until[:, :], ones_col[:, 0:E], tiles[:, :], 0.0, ALU.mult, ALU.add))
            then(dve.tensor_tensor(base[:, :], tiles_until[:, :], tiles[:, :], ALU.subtract))
            then(dve.tensor_tensor(until[:, :, :], until[:, :, :], total[:, :, :], ALU.subtract))
            then(dve.tensor_tensor(until[:, :, :], until[:, :, :],
                                   ps_before[:, 0:NT * E].rearrange("p (t e) -> p t e", e=E), ALU.add))
            then(dve.scalar_tensor_tensor(out=place[:, :, :], in0=base[:, None, :].to_broadcast([P, NT, E]),
                                          scalar=float(P), in1=until[:, :, :], op0=ALU.mult, op1=ALU.add))
            for k, chosen in enumerate((first, second)):
                then(dve.tensor_tensor(total[:, :, :], chosen[:, :, :], place[:, :, :], ALU.mult))
                then(dve.tensor_reduce(row_f[:, k, :], total[:, :, :], AX.X, ALU.add))
            then(dve.tensor_copy(row_i[:, :], row_f[:, :, :].rearrange("p k t -> p (k t)")))
            dve.tensor_scalar(part_i[:, 0, :], row_i[:, :], P - 1, None, ALU.bitwise_and).then_inc(chain, 1)
            dve.tensor_scalar(part_i[:, 1, :], row_i[:, :], 7, None, ALU.arith_shift_right).then_inc(chain, 1)
            done[0] += 2
            dve.wait_ge(chain, done[0])
            dve.tensor_copy(row_lo[:, :], part_i[:, 0, :]).then_inc(chain, 1)
            dve.tensor_copy(row_hi[:, :], part_i[:, 1, :]).then_inc(chain, 1)
            done[0] += 2
            dve.wait_ge(chain, done[0])
            for T in range(0, 2 * NT, GROUP):
                some = slice(T, T + GROUP)
                dve.tensor_tensor(in_tile[:, some, :], tile_of[:, None, :].to_broadcast([P, GROUP, MT]),
                                  row_hi[:, some, None].to_broadcast([P, GROUP, MT]), ALU.is_equal)\
                   .then_inc(in_tile_ready, 1)
                dve.tensor_tensor(in_lane[:, some, :], lane[:, None, :].to_broadcast([P, GROUP, P]),
                                  row_lo[:, some, None].to_broadcast([P, GROUP, P]), ALU.is_equal)\
                   .then_inc(lists_ready, 1)
            then(dve.tensor_tensor(tile_no[:, :, :], tile_no[:, :, :], base[0:1, None, :].to_broadcast([1, MT, E]),
                                   ALU.is_ge))
            then(dve.tensor_reduce(owner[:, :], tile_no[:, :, :], AX.X, ALU.add))
            then(dve.tensor_scalar(owner[:, :], owner[:, :], -1.0, None, ALU.add))
            then(dve.tensor_copy(g.owner[:, :], owner[:, :]))
            dve.wait_ge(list_found, 1)
            then(dve.tensor_scalar(found[:, :], ps_list[:, 0:MT], -1.0, None, ALU.add))
            dve.tensor_scalar(none[:, :], found[:, :], 0.0, float(4 * B * L), ALU.is_lt, ALU.mult).then_inc(chain, 1)
            dve.tensor_scalar(source_f[:, :], found[:, :], 0.0, None, ALU.max).then_inc(chain, 1)
            done[0] += 2
            dve.wait_ge(chain, done[0])
            dve.tensor_tensor(found[:, :], found[:, :], none[:, :], ALU.add).then_inc(chain, 1)
            dve.tensor_copy(source_i[:, :], source_f[:, :]).then_inc(chain, 1)
            done[0] += 2
            dve.wait_ge(chain, done[0])
            then(dve.tensor_copy(g.target[:, :], found[:, :]))
            then(dve.tensor_scalar(g.source[:, :], source_i[:, :].bitcast(U32), B * L - 1, None, ALU.bitwise_and))


def moe_expert_phase(nc, g, tag):
    with Scope(nc, tag) as s:
        xs = s.sb("xs", [P, XSLOTS, D])
        xT = s.sb("xT", [P, 2, P])
        w1 = s.sb("w1", [P, 2, F])
        b1 = s.sb("b1", [P, 2, FC])
        hT = s.sb("hT", [P, 2, FC, P])
        ys = s.sb("ys", [P, YSLOTS, D])
        ps_x = s.ps("ps_x", [P, 2, CH])
        ps_h = s.ps("ps_h", [P, 2, CH])
        ps_y = s.ps("ps_y", [P, 2, CH])
        x_in = [s.sem(f"x_in{k}") for k in range(XSLOTS)]
        x_turned = s.sem("x_turned")
        xT_ready = s.sem("xT_ready")
        w_staged = s.sem("w_staged")
        up_ready = s.sem("up_ready")
        hT_ready = s.sem("hT_ready")
        down_ready = s.sem("down_ready")
        y_ready = s.sem("y_ready")
        y_out = [s.sem(f"y_out{k}") for k in range(YSLOTS)]
        block = s.block()

        def steps(eng, step):
            for n in range(XSLOTS):
                step(n, n, n)
            with eng.Fori(1, MT // XSLOTS) as q:
                for r in range(XSLOTS):
                    step(q * XSLOTS + r, r, None)
            for n in range(MT, MT + 2):
                step(n, n % XSLOTS, n)

        def on(n, lag):
            return n is None or 0 <= n - lag < MT

        @block.gpsimd
        def _(pool):
            def gather(n):
                if n >= XSLOTS:
                    pool.wait_ge(x_turned, n - XSLOTS + 1)
                pool.indirect_dma_start(
                    out=xs[:, n % XSLOTS, :], out_offset=None, in_=g.token_rows[:, :],
                    in_offset=bass.IndirectOffsetOnAxis(ap=g.source[:, n:n + 1], axis=0))\
                    .then_inc(x_in[n % XSLOTS], 16)

            for n in range(XSLOTS - 2):
                gather(n)
            for n in range(MT):
                if n + XSLOTS - 2 < MT:
                    gather(n + XSLOTS - 2)
                pool.wait_ge(y_ready, n + 3)
                pool.indirect_dma_start(
                    out=g.expert_rows[:, :], out_offset=bass.IndirectOffsetOnAxis(ap=g.target[:, n:n + 1], axis=0),
                    in_=ys[:, n % YSLOTS, :], in_offset=None, bounds_check=2 * B * L - 1, oob_is_err=False)\
                    .then_inc(y_out[n % YSLOTS], 16)
            for k in range(YSLOTS):
                pool.wait_ge(y_out[k], 16 * (MT // YSLOTS))

        @block.tensor
        def _(pe):
            pe.sem_inc(up_ready, 2)
            pe.sem_inc(down_ready, 2)

            def step(n, r, known):
                if on(known, 0):
                    pe.wait_ge(x_in[r], (n - r) * (16 // XSLOTS) + 16 if known is None
                               else 16 * (known // XSLOTS + 1))
                    pe.wait_ge(xT_ready, n + 1)
                    pe.transpose(ps_x[:, r % 2, 0:P], xs[:, r, :], g.ident[:, :]).then_inc(x_turned, 1)
                if on(known, 1):
                    m = (r + 1) % 2
                    pe.wait_ge(xT_ready, n - 1 + 3)
                    pe.wait_ge(w_staged, n - 1 + 1)
                    pe.wait_ge(hT_ready, n - 1 + 1)
                    for c in range(FC):
                        last = pe.matmul(ps_h[:, m, c * P:(c + 1) * P], w1[:, m, c * P:(c + 1) * P], xT[:, m, :],
                                         start=True, stop=True)
                    last.then_inc(up_ready, 1)
                if on(known, 2):
                    m = r % 2
                    e = pe.value_load(g.owner[0:1, bass.ds(n - 2, 1)], min_val=0, max_val=E - 1)
                    pe.wait_ge(hT_ready, n - 2 + 3)
                    pe.wait_ge(y_ready, n - 2 + 1)
                    for c in range(FC):
                        last = pe.matmul(ps_y[:, m, 0:D], hT[:, m, c, :], g.w2[:, bass.ds(e * F + c * D, D)],
                                         start=(c == 0), stop=(c == FC - 1))
                    last.then_inc(down_ready, 1)

            steps(pe, step)

        @block.scalar
        def _(act):
            act.sem_inc(xT_ready, 2)
            act.sem_inc(hT_ready, 2)

            def step(n, r, known):
                if on(known, 0):
                    act.wait_ge(x_turned, n + 1)
                    act.wait_ge(up_ready, n + 1)
                    act.activation(xT[:, r % 2, :], ps_x[:, r % 2, 0:P], ACT.Copy).then_inc(xT_ready, 1)
                if on(known, 1):
                    m = (r + 1) % 2
                    act.wait_ge(up_ready, n - 1 + 3)
                    act.wait_ge(down_ready, n - 1 + 1)
                    for c in range(FC):
                        last = act.activation(hT[:, m, c, :], ps_h[:, m, c * P:(c + 1) * P], ACT.Relu,
                                              bias=b1[:, m, c:c + 1])
                    last.then_inc(hT_ready, 1)

            steps(act, step)

        @block.vector
        def _(dve):
            dve.sem_inc(y_ready, 2)

            def step(n, r, known):
                if on(known, 0):
                    m = r % 2
                    e = dve.value_load(g.owner[0:1, bass.ds(n, 1)], min_val=0, max_val=E - 1)
                    dve.wait_ge(up_ready, n + 1)
                    dve.wait_ge(hT_ready, n + 1)
                    dve.tensor_copy(b1[:, m, :], g.b1[:, bass.ds(e * FC, FC)])
                    dve.tensor_copy(w1[:, m, :], g.w1[:, bass.ds(e * F, F)]).then_inc(w_staged, 1)
                if on(known, 2):
                    k = (r + 2) % YSLOTS
                    e = dve.value_load(g.owner[0:1, bass.ds(n - 2, 1)], min_val=0, max_val=E - 1)
                    dve.wait_ge(down_ready, n - 2 + 3)
                    if known is None:
                        dve.wait_ge(y_out[k], (n - 2 - k) * (16 // YSLOTS))
                    elif known - 2 >= YSLOTS:
                        dve.wait_ge(y_out[k], 16 * ((known - 2) // YSLOTS))
                    dve.tensor_tensor(ys[:, k, :], ps_y[:, r % 2, 0:D], g.b2[:, bass.ds(e * D, D)], ALU.add)\
                        .then_inc(y_ready, 1)

            steps(dve, step)


def moe_combine_phase(nc, g, tag, out=None):
    with Scope(nc, tag) as s:
        GROUP = 4
        rows = s.sb("rows", [P, 2, NT, D])
        fetched = [s.sem(f"fetched{q}") for q in range(NT // GROUP)]
        half_added = s.sem("half_added")
        group_added = s.sem("group_added")
        stored = s.sem("stored")
        block = s.block()

        @block.sync
        def _(sp):
            src = g.expert_rows.rearrange("(k t p) c -> p k t c", p=P, t=NT)
            for q in range(NT // GROUP):
                some = slice(q * GROUP, (q + 1) * GROUP)
                for k in range(2):
                    sp.dma_start(rows[:, k, some, :], src[:, k, some, :]).then_inc(fetched[q], 16)
            if out is not None:
                view = out.rearrange("b (n p) c -> p (b n) c", p=P)
                for q in range(NT // GROUP):
                    some = slice(q * GROUP, (q + 1) * GROUP)
                    sp.wait_ge(group_added, q + 1)
                    sp.dma_start(view[:, some, :], g.x[:, some, :]).then_inc(stored, 16)
                sp.wait_ge(stored, 16 * (NT // GROUP))

        @block.vector
        def _(dve):
            for q in range(NT // GROUP):
                dve.wait_ge(fetched[q], 16 * 2)
                for k in range(2):
                    for t in range(q * GROUP, (q + 1) * GROUP):
                        if k == 1:
                            dve.wait_ge(half_added, t + 1)
                        last = dve.scalar_tensor_tensor(out=g.x[:, t, :], in0=rows[:, k, t, :],
                                                        scalar=g.weight[:, k, t:t + 1], in1=g.x[:, t, :],
                                                        op0=ALU.mult, op1=ALU.add)
                        if k == 0:
                            last.then_inc(half_added, 1)
                last.then_inc(group_added, 1)


def attention_phase(nc, g, A):
    STEPS = 2 * TB
    PAIRS = H // 2
    projections = {1: ("y", 1, 0), 3: ("y", 1, 1), 5: ("v", 0, 0), 7: ("v", 0, 1),
                   9: ("y", 2, 0), 11: ("y", 2, 1), 13: ("v", 0, 2), 15: ("v", 0, 3)}
    at = sorted(projections)
    before = {s: at[n - 1] for n, s in enumerate(at)}
    V_CHUNKS = 4
    parts = [[(lo, min(lo + 4, s % TB + 1)) for lo in range(0, s % TB + 1, 4)] for s in range(STEPS)]
    upto = [sum(len(p) for p in parts[:s + 1]) for s in range(STEPS)]
    UNITS = upto[-1]
    PASSES = ((0, 0), (0, 1), (1, 0))
    with Scope(nc, "attn") as s_:
        xk = s_.sb("xk", [P, 2, 2, L], F32R)
        xs = s_.sb("xs", [P, 2, L], F32R)
        m_all = s_.sb("m_all", [P, 2, H * D], F32R)
        n_all = s_.sb("n_all", [P, 2, H * D], F32R)
        m = s_.sb("m", [P, 2, 2, D], F32R)
        y = s_.sb("y", [P, 2, 2, L], F32R)
        v = s_.sb("v", [P, 2, TB, 2 * D])
        probs = s_.sb("probs", [P, 2, L])
        pT = s_.sb("pT", [P, 2, L])
        neg_max = s_.sb("neg_max", [P, 2])
        row_sum = s_.sb("row_sum", [P, 4])
        inv_sum = s_.sb("inv_sum", [P, 2])
        ident16 = s_.sb("ident16", [P, P], BF16)
        causal = s_.sb("causal", [P, P], BF16)
        ps_s = s_.ps("ps_s", [P, 2, L])
        ps_t = s_.ps("ps_t", [P, 2, CH])
        ps_p = s_.ps("ps_p", [P, CH])
        ps_o = s_.ps("ps_o", [P, CH])
        mask_steps = s_.sem("mask_steps")
        folded = s_.sem("folded")
        fold_hi = s_.sem("fold_hi")
        fold_lo = s_.sem("fold_lo")
        x_hi = s_.sem("x_hi")
        x_lo = s_.sem("x_lo")
        x_staged = s_.sem("x_staged")
        m_staged = s_.sem("m_staged")
        waited = s_.sem("waited")
        y_ready = s_.sem("y_ready")
        y_hi = s_.sem("y_hi")
        y_lo = s_.sem("y_lo")
        v_ready = s_.sem("v_ready")
        v_copied = s_.sem("v_copied")
        scores_ready = s_.sem("scores_ready")
        max_ready = s_.sem("max_ready")
        probs_ready = s_.sem("probs_ready")
        turned = s_.sem("turned")
        pT_copied = s_.sem("pT_copied")
        pv_ready = s_.sem("pv_ready")
        inv_ready = s_.sem("inv_ready")
        added = s_.sem("added")
        block = s_.block()

        def sequence(G):
            return 0 if isinstance(G, int) else (G // PAIRS) % B

        @block.gpsimd
        def _(pool):
            pool.memset(ident16[:, :], 0.0).then_inc(mask_steps, 1)
            pool.memset(causal[:, :], 0.0).then_inc(mask_steps, 1)
            pool.wait_ge(mask_steps, 2)
            pool.affine_select(out=ident16[:, :], in_=ident16[:, :], compare_op=ALU.not_equal, fill=1.0,
                               base=0, pattern=[[-1, P]], channel_multiplier=1).then_inc(mask_steps, 1)
            pool.affine_select(out=causal[:, :], in_=causal[:, :], compare_op=ALU.is_ge, fill=-1e30,
                               base=0, pattern=[[-1, P]], channel_multiplier=1).then_inc(mask_steps, 1)

            def stage_x(b, slot):
                x = g.xnT[:, b, HALO:HALO + L]
                pool.wait_ge(v_ready, V_CHUNKS * PAIRS * b + 1)
                pool.sem_inc(waited, 1)
                pool.tensor_copy(xk[:, slot, 0, :], x).then_inc(x_hi, 1)
                pool.wait_ge(x_hi, b + 1)
                pool.sem_inc(waited, 1)
                pool.tensor_tensor(xk[:, slot, 1, :], x, xk[:, slot, 0, :].bitcast(F32), ALU.subtract)\
                    .then_inc(x_lo, 1)
                pool.wait_ge(x_lo, b + 1)
                pool.sem_inc(waited, 1)
                pool.tensor_copy(xs[:, :, :], xk[:, slot, :, :]).then_inc(x_staged, 1)

            def stage_m(head, h, slot):
                pool.wait_ge(y_ready, 2 * head + 2)
                pool.sem_inc(waited, 1)
                pool.tensor_copy(m[:, slot, :, :], m_all[:, :, bass.ds(h * D, D)]).then_inc(m_staged, 1)

            with pool.Fori(0, B) as b:
                stage_x(b, b % 2)
                pool.wait_ge(fold_lo, 1)
                with pool.Fori(0, PAIRS) as pair:
                    for slot in range(2):
                        stage_m(b * H + pair * 2 + slot, pair * 2 + slot, slot)
            stage_m(B * H, 0, 0)

        @block.tensor
        def _(pe):
            def project_y(G, c, head, slot):
                pe.wait_ge(m_staged, head + 1)
                b = sequence(G)
                for k, (one, two) in enumerate(PASSES):
                    last = pe.matmul(ps_p[:, :], m[:, slot, one, :], xk[:, b % 2, two, c * CH:(c + 1) * CH],
                                     start=(k == 0), stop=(k == 2))
                last.then_inc(y_ready, 1)

            def project_v(G, c):
                pe.wait_ge(x_staged, sequence(G) + 1)
                pair = 0 if isinstance(G, int) else G % PAIRS
                for j in range(2):
                    t = 2 * c + j
                    for k, (one, two) in enumerate(PASSES):
                        last = pe.matmul(ps_p[:, j * 2 * D:(j + 1) * 2 * D], xs[:, one, t * P:(t + 1) * P],
                                         n_all[:, two, bass.ds(pair * 2 * D, 2 * D)], start=(k == 0), stop=(k == 2))
                last.then_inc(v_ready, 1)

            def scores(G, s, head, slot):
                i = s % TB
                t = G * STEPS + s
                pe.wait_ge(y_lo, 2 * head + i // 4 + 1)
                pe.wait_ge(probs_ready, t + 1)
                b = sequence(G)
                n = (i + 1) * P
                for lo in range(0, n, CH):
                    hi = min(lo + CH, n)
                    wide = max(hi, lo + 2 * P)
                    for k, (one, two) in enumerate(PASSES):
                        pe.matmul(ps_s[:, i % 2, lo:wide], y[:, slot, one, i * P:(i + 1) * P],
                                  xk[:, b % 2, two, lo:wide], start=(k == 0), stop=(hi < n and k == 2))
                pe.matmul(ps_s[:, i % 2, i * P:n], ident16[:, :], causal[:, :], start=False, stop=True)\
                    .then_inc(scores_ready, 1)

            def turn(G, s):
                pe.wait_ge(probs_ready, G * STEPS + s + 3)
                for n, (lo, hi) in enumerate(parts[s]):
                    u = upto[s] - len(parts[s]) + n
                    pe.wait_ge(pT_copied, UNITS * G + u + 1)
                    for j in range(lo, hi):
                        last = pe.transpose(ps_t[:, u % 2, (j - lo) * P:(j - lo + 1) * P],
                                            probs[:, s % 2, j * P:(j + 1) * P], g.ident[:, :])
                    last.then_inc(turned, 1)

            def values(G, s):
                i = s % TB
                pe.wait_ge(pT_copied, UNITS * G + upto[s] + 2)
                pe.wait_ge(v_copied, V_CHUNKS * G + V_CHUNKS)
                pe.wait_ge(added, G * STEPS + s + 2)
                for j in range(i + 1):
                    last = pe.matmul(ps_o[:, 0:D], pT[:, s % 2, j * P:(j + 1) * P],
                                     v[:, G % 2, j, (s // TB) * D:(s // TB + 1) * D], start=(j == 0), stop=(j == i))
                last.then_inc(pv_ready, 1)

            pe.sem_inc(v_ready, 1)
            pe.sem_inc(y_ready, 4)
            pe.sem_inc(pv_ready, 2)
            pe.wait_ge(g.late_loaded, g.LATE_LOADED)
            for h in range(H):
                at = slice((h % 4) * D, (h % 4 + 1) * D)
                w = slice(h * D, (h + 1) * D)
                pe.matmul(ps_s[:, 0, (h // 4) * CH:(h // 4 + 1) * CH][:, at], g.w_qkv[:, 0, w], g.w_qkv[:, 1, w],
                          start=True, stop=True)
                last = pe.matmul(ps_s[:, 1, (h // 4) * CH:(h // 4 + 1) * CH][:, at], g.w_qkv[:, 2, w], g.w_o[:, w],
                                 start=True, stop=True)
            last.then_inc(folded, 1)
            pe.wait_ge(fold_lo, 2)
            pe.wait_ge(x_staged, 1)
            pe.wait_ge(mask_steps, 4)
            for c in range(2):
                if c > 0:
                    pe.wait_ge(y_lo, c)
                project_y(0, c, 0, 0)
            pe.wait_ge(y_lo, 2)
            for c in range(V_CHUNKS):
                if c > 0:
                    pe.wait_ge(v_copied, c)
                project_v(0, c)
            for s in range(2):
                scores(0, s, 0, 0)
            with pe.Fori(0, B * PAIRS) as G:
                for s in range(STEPS):
                    r = s + 2
                    scores(G + r // STEPS, r % STEPS, 2 * G + r // TB, (r // TB) % 2)
                    turn(G, s)
                    if s > 0:
                        values(G, s - 1)
                    if s in projections:
                        kind, ahead, c = projections[s]
                        was, ahead_was, c_was = projections[before[s]]
                        if was == "y":
                            pe.wait_ge(y_lo, 2 * (2 * G + ahead_was) + c_was + 1)
                        else:
                            pe.wait_ge(v_copied, V_CHUNKS * (G + (s > before[s])) + c_was + 1)
                        if kind == "y":
                            project_y(G + ahead // 2, c, 2 * G + ahead, ahead % 2)
                        else:
                            project_v(G + 1, c)
                values(G, STEPS - 1)

        @block.scalar
        def _(act):
            def take_y(c, head, slot):
                act.wait_ge(y_ready, 2 * head + c + 1 + 4)
                act.activation(y[:, slot, 0, c * CH:(c + 1) * CH], ps_p[:, :], ACT.Copy).then_inc(y_hi, 1)

            def take_v(G, c):
                act.wait_ge(v_ready, V_CHUNKS * G + c + 1 + 1)
                act.sem_inc(waited, 1)
                act.activation(v[:, G % 2, 2 * c:2 * c + 2, :].rearrange("p t c -> p (t c)"), ps_p[:, :], ACT.Copy)\
                    .then_inc(v_copied, 1)

            def exponentials(G, s):
                t = G * STEPS + s
                i = s % TB
                act.wait_ge(max_ready, t + 1)
                n = (i + 1) * P
                act.activation(probs[:, s % 2, 0:n], ps_s[:, s % 2, 0:n], ACT.Exp, bias=neg_max[:, s % 2:s % 2 + 1],
                               accum_out=row_sum[:, s % 4:s % 4 + 1]).then_inc(probs_ready, 1)

            act.sem_inc(probs_ready, 2)
            act.wait_ge(folded, 1)
            act.activation(m_all[:, 0, :], ps_s[:, 0, :], ACT.Copy, scale=DH ** -0.5).then_inc(fold_hi, 1)
            act.activation(n_all[:, 0, :], ps_s[:, 1, :], ACT.Copy).then_inc(fold_hi, 1)
            for c in range(2):
                take_y(c, 0, 0)
            for c in range(V_CHUNKS):
                take_v(0, c)
            for s in range(2):
                exponentials(0, s)
            with act.Fori(0, B * PAIRS) as G:
                for s in range(STEPS):
                    act.wait_ge(turned, UNITS * G + upto[s])
                    exponentials(G + (s + 2) // STEPS, (s + 2) % STEPS)
                    if s in projections:
                        kind, ahead, c = projections[s]
                        if kind == "y":
                            take_y(c, 2 * G + ahead, ahead % 2)
                        else:
                            take_v(G + 1, c)

        @block.vector
        def _(dve):
            def rest_of_y(c, head, slot):
                dve.wait_ge(y_hi, 2 * head + c + 1)
                dve.tensor_tensor(y[:, slot, 1, c * CH:(c + 1) * CH], ps_p[:, :],
                                  y[:, slot, 0, c * CH:(c + 1) * CH].bitcast(F32), ALU.subtract).then_inc(y_lo, 1)

            def maxima(G, s):
                dve.wait_ge(scores_ready, G * STEPS + s + 1)
                dve.tensor_reduce(neg_max[:, s % 2:s % 2 + 1], ps_s[:, s % 2, 0:(s % TB + 1) * P], AX.X, ALU.max,
                                  negate=True).then_inc(max_ready, 1)

            def add(G, s):
                t = G * STEPS + s
                dve.wait_ge(inv_ready, t + 1)
                dve.wait_ge(pv_ready, t + 3)
                x = g.x[:, (G // PAIRS) * TB + s % TB, :]
                dve.scalar_tensor_tensor(out=x, in0=ps_o[:, 0:D], scalar=inv_sum[:, s % 2:s % 2 + 1], in1=x,
                                         op0=ALU.mult, op1=ALU.add).then_inc(added, 1)

            dve.sem_inc(pT_copied, 2)
            dve.sem_inc(added, 2)
            for k, (to, scale) in enumerate(((m_all, DH ** -0.5), (n_all, 1.0))):
                dve.wait_ge(fold_hi, k + 1)
                dve.scalar_tensor_tensor(out=to[:, 1, :], in0=ps_s[:, k, :], scalar=scale, in1=to[:, 0, :].bitcast(F32),
                                         op0=ALU.mult, op1=ALU.subtract).then_inc(fold_lo, 1)
            for c in range(2):
                rest_of_y(c, 0, 0)
            for s in range(2):
                maxima(0, s)
            with dve.Fori(0, B * PAIRS) as G:
                for s in range(STEPS):
                    t = G * STEPS + s
                    maxima(G + (s + 2) // STEPS, (s + 2) % STEPS)
                    dve.wait_ge(probs_ready, t + 3)
                    dve.wait_ge(added, t + 1)
                    dve.reciprocal(inv_sum[:, s % 2:s % 2 + 1], row_sum[:, s % 4:s % 4 + 1]).then_inc(inv_ready, 1)
                    for n, (lo, hi) in enumerate(parts[s]):
                        u = upto[s] - len(parts[s]) + n
                        dve.wait_ge(turned, UNITS * G + u + 1)
                        dve.wait_ge(pv_ready, t + 1)
                        dve.tensor_copy(pT[:, s % 2, lo * P:hi * P], ps_t[:, u % 2, 0:(hi - lo) * P])\
                            .then_inc(pT_copied, 1)
                    if s > 0:
                        add(G, s - 1)
                    if s in projections and projections[s][0] == "y":
                        _, ahead, c = projections[s]
                        rest_of_y(c, 2 * G + ahead, ahead % 2)
                add(G, STEPS - 1)


class Shared:
    pass


def program(nc, A, out):
    with ExitStack() as stack:
        g = Shared()
        g.x = stack.enter_context(nc.sbuf_tensor("x", [P, NT, D], F32))
        g.xnT = stack.enter_context(nc.sbuf_tensor("xnT", [P, B, HALO + L], F32))
        g.ident = stack.enter_context(nc.sbuf_tensor("ident", [P, P], F32))
        g.w_ffn = stack.enter_context(nc.sbuf_tensor("w_ffn", [P, 3, D], F32))
        g.mu = stack.enter_context(nc.sbuf_tensor("mu", [P, 2], F32))
        g.w_in = stack.enter_context(nc.sbuf_tensor("w_in", [P, 2 * NB * P], F32))
        g.w_x = stack.enter_context(nc.sbuf_tensor("w_x", [P, NB, R + 3 * BC], F32))
        g.w_dt = stack.enter_context(nc.sbuf_tensor("w_dt", [R, NB * P], F32))
        g.w_out = stack.enter_context(nc.sbuf_tensor("w_out", [P, NB, D], F32))
        g.taps_in = stack.enter_context(nc.sbuf_tensor("taps_in", [P, NB, 2 * KW * P], F32))
        g.conv_b = stack.enter_context(nc.sbuf_tensor("conv_b", [P, NB, 2], F32))
        g.b_dt = stack.enter_context(nc.sbuf_tensor("b_dt", [P, NB], F32))
        g.d_param = stack.enter_context(nc.sbuf_tensor("d_param", [P, NB], F32))
        g.a_log = stack.enter_context(nc.sbuf_tensor("a_log", [P, NB, NS], F32))
        g.neg_a = stack.enter_context(nc.sbuf_tensor("neg_a", [P, NB, NS], F32))
        g.gates = stack.enter_context(nc.sbuf_tensor("gates", [P, 2], F32))
        g.weights = [(g.w_ffn[:, :, :], "w_ffn"), (g.mu[:, :], "mu"), (g.w_in[:, :], "w_in"), (g.w_x[:, :, :], "w_x"),
                     (g.w_dt[:, :], "w_dt"), (g.w_out[:, :, :], "w_out"), (g.taps_in[:, :, :], "taps"),
                     (g.conv_b[:, :, :], "conv_b"), (g.b_dt[:, :], "b_dt"), (g.d_param[:, :], "d_param"),
                     (g.a_log[:, :, :], "a_log"), (g.gates[:, :], "gates")]
        g.loaded = stack.enter_context(nc.semaphore("loaded"))
        g.LOADED = 16 * len(g.weights)
        g.token_rows = nc.dram_tensor("token_rows", (B * L, D), F32, kind="Internal").ap()
        g.expert_rows = nc.dram_tensor("expert_rows", (2 * B * L, D), F32, kind="Internal").ap()
        load_phase(nc, g, A)
        layernorm_phase(nc, g, "ln0")
        ffn_phase(nc, g, "ffn0")
        layernorm_phase(nc, g, "ln1")
        mamba_phase(nc, g, A)
        layernorm_phase(nc, g, "ln2")
        g.w1 = stack.enter_context(nc.sbuf_tensor("w1", [P, E * F], F32))
        g.w2 = stack.enter_context(nc.sbuf_tensor("w2", [P, E * F], F32))
        g.b1 = stack.enter_context(nc.sbuf_tensor("b1", [P, E * FC], F32))
        g.b2 = stack.enter_context(nc.sbuf_tensor("b2", [P, E * D], F32))
        g.router = stack.enter_context(nc.sbuf_tensor("router", [P, E], F32))
        g.source = stack.enter_context(nc.sbuf_tensor("source", [P, MT], U32))
        g.target = stack.enter_context(nc.sbuf_tensor("target", [P, MT], U32))
        g.weight = stack.enter_context(nc.sbuf_tensor("weight", [P, 2, NT], F32))
        g.owner = stack.enter_context(nc.sbuf_tensor("owner", [1, MT], I32))
        g.w_qkv = stack.enter_context(nc.sbuf_tensor("w_qkv", [P, 3, H * D], F32))
        g.w_o = stack.enter_context(nc.sbuf_tensor("w_o", [P, H * D], F32))
        g.gamma = stack.enter_context(nc.sbuf_tensor("gamma", [P, 1], F32))
        g.late_loaded = stack.enter_context(nc.semaphore("late_loaded"))
        g.late_weights = [(g.w1[:, :], "w1"), (g.w2[:, :], "w2"), (g.b1[:, :], "b1"), (g.b2[:, :], "b2"),
                          (g.router[:, :], "router"), (g.w_qkv[:, :, :], "w_qkv"), (g.w_o[:, :], "w_o"),
                          (g.gamma[:, :], "gamma")]
        g.LATE_LOADED = 16 * len(g.late_weights)
        load_experts_phase(nc, g, A)
        ffn_phase(nc, g, "ffn1")
        layernorm_phase(nc, g, "ln3", keep_tokens=True)
        moe_route_phase(nc, g, "route0")
        moe_expert_phase(nc, g, "experts0")
        moe_combine_phase(nc, g, "combine0")
        layernorm_phase(nc, g, "ln4", rms_gamma=g.gamma[:, 0:1])
        attention_phase(nc, g, A)
        layernorm_phase(nc, g, "ln5", keep_tokens=True)
        moe_route_phase(nc, g, "route1")
        moe_expert_phase(nc, g, "experts1")
        moe_combine_phase(nc, g, "combine1", out)




def laid_out(i):
    def t(a):
        return np.ascontiguousarray(np.asarray(a).T)
    def blocks(a):
        a = np.asarray(a)
        return np.ascontiguousarray(a.reshape(NB, P, -1).transpose(1, 0, 2))

    w_x = np.asarray(i["L0_attn_W_x"]).T
    return {
        "hidden": np.ascontiguousarray(np.asarray(i["L0_attn_hidden_states"]).reshape(B * L, D)),
        "w_ffn": np.stack([t(i["L0_ffn_W_r"]), t(i["L0_ffn_W_k"]), t(i["L0_ffn_W_v"])], axis=1),
        "mu": np.stack([np.asarray(i["L0_ffn_mu_r"]), np.asarray(i["L0_ffn_mu_k"])], axis=1),
        "w_in": t(i["L0_attn_W_in"]),
        "w_x": blocks(np.concatenate([w_x[:, :R]] + 3 * [w_x[:, R:]], axis=1)),
        "w_dt": t(i["L0_attn_W_dt"]),
        "w_out": blocks(t(i["L0_attn_W_out"])),
        "taps": np.broadcast_to(
            t(np.concatenate([i["L0_attn_conv_w1"], i["L0_attn_conv_w2"]], axis=1))
            .reshape(1, 2 * KW, NB, P).transpose(0, 2, 1, 3), (P, NB, 2 * KW, P)).reshape(P, NB, 2 * KW * P),
        "conv_b": blocks(np.stack([i["L0_attn_conv_b1"], i["L0_attn_conv_b2"]], axis=1)),
        "b_dt": blocks(i["L0_attn_b_dt"])[:, :, 0],
        "d_param": blocks(i["L0_attn_D_param"])[:, :, 0],
        "a_log": blocks(i["L0_attn_A_log"]),
        "w1": np.asarray(i["L1_ffn_w1"]).transpose(2, 0, 1).reshape(P, E * F),
        "w2": np.asarray(i["L1_ffn_w2"]).reshape(E, D, FC, P).transpose(3, 0, 2, 1).reshape(P, E * F),
        "b1": np.asarray(i["L1_ffn_b1"]).reshape(E * FC, P).T,
        "b2": np.broadcast_to(np.asarray(i["L1_ffn_b2"]).reshape(1, E * D), (P, E * D)),
        "w_qkv": np.asarray(i["L1_attn_w_qkv"]).reshape(3, H, DH, D).transpose(2, 0, 1, 3).reshape(DH, 3, H * D),
        "w_o": np.asarray(i["L1_attn_w_out"]).reshape(D, H, DH).transpose(2, 1, 0).reshape(DH, H * D),
        "gamma": np.asarray(i["L1_attn_gamma"])[:, None],
        "router": t(i["L1_ffn_router_w"]),
        "gates": np.broadcast_to(np.asarray(i["L0_attn_conv_gates"])[None], (P, 2)),
    }


def kernel(**inputs):
    import concourse.bacc as bacc
    from concourse.bass_utils import run_bass_kernel_spmd

    nc = bacc.Bacc("TRN2", target_bir_lowering=False, num_devices=1)
    arrays, aps = {}, {}
    for name, a in laid_out(inputs).items():
        a = np.ascontiguousarray(a)
        arrays[f"in_{name}"] = a
        aps[name] = nc.dram_tensor(f"in_{name}", a.shape, mybir.dt.from_np(a.dtype), kind="ExternalInput").ap()
    out = nc.dram_tensor("out_x", (B, L, D), F32, kind="ExternalOutput").ap()
    program(nc, aps, out)
    r = run_bass_kernel_spmd(nc, [arrays], core_ids=[0])
    return r.results[0]["out_x"]
```
